# Optimizing a Trainium2 kernel written in Bass

```python
import numpy as np
import jax
import jax.numpy as jnp

def _softmax(x, axis=-1):
    return jax.nn.softmax(x, axis=axis)

def _gelu(x):
    return jax.nn.gelu(x, approximate=True)

def _silu(x):
    return jax.nn.silu(x)

def _sigmoid(x):
    return jax.nn.sigmoid(x)

def _layernorm(x, axis=-1, eps=1e-05):
    m = jnp.mean(x, axis=axis, keepdims=True)
    v = jnp.var(x, axis=axis, keepdims=True)
    return (x - m) / jnp.sqrt(v + eps)

def _scatter_add(tgt, idx, src, axis=0):
    return tgt.at[idx].add(src)

def _segment_sum(src, seg, n):
    return jax.ops.segment_sum(src, seg, n)
kernel_name = 'mk_xattn_seq_d4_seqx_r4_d36bcd'

def setup_inputs(seed: int=0):
    np.random.seed(seed)
    _w = jnp.asarray

    def _rec_inputs():
        import jax
        import jax.numpy as jnp
        _rk = jax.random.key(seed)
        x = 7.22e-05 + 1 * jax.random.normal(jax.random.fold_in(_rk, 1), (32, 128, 256), jnp.float32)
        _lenS = 128 - jax.random.randint(jax.random.fold_in(_rk, 7), (32,), 0, max(1, 128 // 4) + 1, jnp.int32)
        _lenS2 = 128 - jax.random.randint(jax.random.fold_in(_rk, 8), (32,), 0, max(1, 128 // 4) + 1, jnp.int32)
        _ctx_1024P = jax.random.normal(jax.random.fold_in(_rk, 11), (32, 16, 256), jnp.float32)
        _ctx_1024c = jax.random.dirichlet(jax.random.fold_in(_rk, 511), 0.3 * jnp.ones((16,), jnp.float32), (32, 128))
        _ctx_1024t = jnp.einsum('bsk,bkd->bsd', _ctx_1024c, _ctx_1024P)
        _ctx_1024t = _ctx_1024t * jax.lax.rsqrt(jnp.mean(jnp.square(_ctx_1024t)) + 1e-12) * 0.953939
        ctx_1024 = 4.13588e-05 + 0.999923 * (_ctx_1024t + 0.3 * jax.random.normal(jax.random.fold_in(_rk, 611), (32, 128, 256), jnp.float32))
        _validS = jnp.arange(128)[None, :] < _lenS[:, None]
        _validS2 = jnp.arange(128)[None, :] < _lenS2[:, None]
        _causal = jnp.tril(jnp.ones((128, 128), dtype=bool))
        mask_Bx1xS2_if1 = jnp.where(jnp.ones((32, 1, 128), dtype=bool), 1, 0).astype(jnp.int32)
        mask_BxSxS2_ik0 = jnp.where(jnp.broadcast_to(_validS2[:, None, :], (32, 128, 128)), 0, 1).astype(jnp.int32)
        mask_BxSxS2_if1 = jnp.where(jnp.ones((32, 128, 128), dtype=bool), 1, 0).astype(jnp.int32)
        mask_SxS_ik1 = jnp.where(jnp.broadcast_to(_validS[0:1, :], (128, 128)), 1, 0).astype(jnp.int32)
        return (x, ctx_1024, mask_Bx1xS2_if1, mask_BxSxS2_ik0, mask_BxSxS2_if1, mask_SxS_ik1)
    x, ctx_1024, mask_Bx1xS2_if1, mask_BxSxS2_ik0, mask_BxSxS2_if1, mask_SxS_ik1 = _rec_inputs()

    def _L0_xattn_setup():
        import jax, jax.numpy as jnp
        import numpy as np
        B, SD, SE, DM, H, DK, DV, DFF = (4, 512, 512, 256, 8, 128, 128, 1024)
        NEG = -jnp.inf

        def _linear(x, w, b):
            return jnp.einsum('...i,oi->...o', x, w) + b

        def _layer_norm(x, g, b, eps=1e-05):
            mu = jnp.mean(x, axis=-1, keepdims=True)
            var = jnp.var(x, axis=-1, keepdims=True)
            return (x - mu) * jax.lax.rsqrt(var + eps) * g + b

        def _mha(Q, K, V, wq, bq, wk, bk, wv, bv, wo, bo, pad_mask, seq_mask):
            Qh = jnp.einsum('bsd,hkd->bhsk', Q, wq) + bq[None, :, None, :]
            Kh = jnp.einsum('bsd,hkd->bhsk', K, wk) + bk[None, :, None, :]
            Vh = jnp.einsum('bsd,hvd->bhsv', V, wv) + bv[None, :, None, :]
            scores = jnp.einsum('bhqd,bhkd->bhqk', Qh, Kh) / np.sqrt(DK)
            scores = jnp.where(pad_mask[:, None, :, :] == 0, NEG, scores)
            if seq_mask is not None:
                scores = jnp.where(seq_mask[None, None, :, :] == 0, NEG, scores)
            w = jax.nn.softmax(scores, axis=-1)
            out = jnp.einsum('bhqk,bhkv->bhqv', w, Vh)
            out = out.transpose(0, 2, 1, 3).reshape(Q.shape[0], Q.shape[1], H * DV)
            return _linear(out, wo, bo)
        key = jax.random.key(seed)
        ks = iter(jax.random.split(key, 40))
        s = 0.02
        d = {'output_embs': jax.random.normal(next(ks), (B, SD, DM), jnp.float32), 'encoder_output': jax.random.normal(next(ks), (B, SE, DM), jnp.float32), 'inputs_padding_mask': jnp.ones((B, 1, SE), jnp.int32), 'outputs_padding_mask': jnp.ones((B, 1, SD), jnp.int32)}
        for name in ['q1', 'k1', 'v1', 'q2', 'k2', 'v2']:
            d[name + '_w'] = jax.random.normal(next(ks), (DM, DM), jnp.float32) * s
            d[name + '_b'] = jnp.zeros((DM,), jnp.float32)
        for p in ['sa', 'ed']:
            d[p + '_qw'] = jax.random.normal(next(ks), (H, DK, DM), jnp.float32) * s
            d[p + '_qb'] = jnp.zeros((H, DK), jnp.float32)
            d[p + '_kw'] = jax.random.normal(next(ks), (H, DK, DM), jnp.float32) * s
            d[p + '_kb'] = jnp.zeros((H, DK), jnp.float32)
            d[p + '_vw'] = jax.random.normal(next(ks), (H, DV, DM), jnp.float32) * s
            d[p + '_vb'] = jnp.zeros((H, DV), jnp.float32)
            d[p + '_ow'] = jax.random.normal(next(ks), (DM, H * DV), jnp.float32) * s
            d[p + '_ob'] = jnp.zeros((DM,), jnp.float32)
        d['ff_w1'] = jax.random.normal(next(ks), (DFF, DM), jnp.float32) * s
        d['ff_b1'] = jnp.zeros((DFF,), jnp.float32)
        d['ff_w2'] = jax.random.normal(next(ks), (DM, DFF), jnp.float32) * s
        d['ff_b2'] = jnp.zeros((DM,), jnp.float32)
        d['ln1_g'] = jnp.ones((DM,), jnp.float32)
        d['ln1_b'] = jnp.zeros((DM,), jnp.float32)
        d['ln2_g'] = jnp.ones((DM,), jnp.float32)
        d['ln2_b'] = jnp.zeros((DM,), jnp.float32)
        return d
    _L0_xattn_all = _L0_xattn_setup()
    _L0_xattn_in = {k: v for k, v in _L0_xattn_all.items() if k in ('q1_w', 'q1_b', 'k1_w', 'k1_b', 'v1_w', 'v1_b', 'q2_w', 'q2_b', 'k2_w', 'k2_b', 'v2_w', 'v2_b', 'sa_qw', 'sa_qb', 'sa_kw', 'sa_kb', 'sa_vw', 'sa_vb', 'sa_ow', 'sa_ob', 'ed_qw', 'ed_qb', 'ed_kw', 'ed_kb', 'ed_vw', 'ed_vb', 'ed_ow', 'ed_ob', 'ff_w1', 'ff_b1', 'ff_w2', 'ff_b2', 'ln1_g', 'ln1_b', 'ln2_g', 'ln2_b')}
    del _L0_xattn_all

    def _L1_xattn_setup():
        import jax, jax.numpy as jnp
        import numpy as np
        B, S, D, H, DFF = (2, 512, 256, 16, 1024)
        DK = D // H
        LN_EPS = 1e-05

        def _mha(q, k, v, mask, wq, bq, wk, bk, wv, bv, wo, bo):
            b, sq, _ = q.shape
            sk = k.shape[1]
            Q = (q @ wq + bq).reshape(b, sq, H, DK).transpose(0, 2, 1, 3)
            K = (k @ wk + bk).reshape(b, sk, H, DK).transpose(0, 2, 1, 3)
            V = (v @ wv + bv).reshape(b, sk, H, DK).transpose(0, 2, 1, 3)
            scores = jnp.einsum('bhqd,bhkd->bhqk', Q, K) / np.float32(np.sqrt(DK))
            if mask is not None:
                scores = jnp.where(mask[:, None, :, :] == 0, jnp.float32(-1e+20), scores)
            A = jax.nn.softmax(scores, axis=-1)
            out = jnp.einsum('bhqk,bhkd->bhqd', A, V).transpose(0, 2, 1, 3).reshape(b, sq, D)
            return out @ wo + bo

        def _ln(x, g, b):
            m = jnp.mean(x, axis=-1, keepdims=True)
            v = jnp.var(x, axis=-1, keepdims=True)
            return (x - m) * jax.lax.rsqrt(v + LN_EPS) * g + b
        key = jax.random.key(seed)
        ks = jax.random.split(key, 32)
        ki = iter(range(32))

        def w(shape, scale=0.02):
            return (jax.random.normal(ks[next(ki)], shape, jnp.float32) * scale).astype(jnp.float32)
        inp = {}
        inp['x'] = jax.random.normal(ks[next(ki)], (B, S, D), jnp.float32)
        inp['enc_output'] = jax.random.normal(ks[next(ki)], (B, S, D), jnp.float32)
        causal = jnp.tril(jnp.ones((S, S), jnp.int32))
        inp['tgt_mask'] = jnp.broadcast_to(causal, (B, S, S))
        inp['memory_mask'] = jnp.ones((B, S, S), jnp.int32)
        for p in ('sa', 'ca'):
            for n in ('q', 'k', 'v', 'o'):
                inp[f'{p}_w{n}'] = w((D, D))
                inp[f'{p}_b{n}'] = jnp.zeros((D,), jnp.float32)
        inp['ff_w1'] = w((D, DFF))
        inp['ff_b1'] = jnp.zeros((DFF,), jnp.float32)
        inp['ff_w2'] = w((DFF, D))
        inp['ff_b2'] = jnp.zeros((D,), jnp.float32)
        for i in (1, 2, 3):
            inp[f'ln{i}_g'] = jnp.ones((D,), jnp.float32)
            inp[f'ln{i}_b'] = jnp.zeros((D,), jnp.float32)
        return inp
    _L1_xattn_all = _L1_xattn_setup()
    _L1_xattn_in = {k: v for k, v in _L1_xattn_all.items() if k in ('sa_wq', 'sa_bq', 'sa_wk', 'sa_bk', 'sa_wv', 'sa_bv', 'sa_wo', 'sa_bo', 'ca_wq', 'ca_bq', 'ca_wk', 'ca_bk', 'ca_wv', 'ca_bv', 'ca_wo', 'ca_bo', 'ff_w1', 'ff_b1', 'ff_w2', 'ff_b2', 'ln1_g', 'ln1_b', 'ln2_g', 'ln2_b', 'ln3_g', 'ln3_b')}
    del _L1_xattn_all

    def _L2_xattn_setup():
        import jax, jax.numpy as jnp
        import numpy as np
        D_MODEL = 256
        N_HEAD = 16
        D_FF = 1024
        EPS = 1e-05

        def _linear(x, w, b):
            return jnp.einsum('bli,io->blo', x, w) + b

        def _layernorm(x, g, b):
            mu = jnp.mean(x, -1, keepdims=True)
            var = jnp.mean(jnp.square(x - mu), -1, keepdims=True)
            return (x - mu) * jax.lax.rsqrt(var + EPS) * g + b

        def _attention(q, k, v, mask):
            B, Lq, D = q.shape
            H = N_HEAD
            hd = D // H
            qh = q.reshape(B, Lq, H, hd)
            kh = k.reshape(B, k.shape[1], H, hd)
            vh = v.reshape(B, v.shape[1], H, hd)
            scores = jnp.einsum('bqhd,bkhd->bhqk', qh, kh) / jnp.sqrt(jnp.float32(hd)).astype(q.dtype)
            if mask is not None:
                scores = jnp.where(mask[None, None] != 0, jnp.finfo(scores.dtype).min, scores)
            p = jax.nn.softmax(scores, axis=-1)
            out = jnp.einsum('bhqk,bkhd->bqhd', p, vh).reshape(B, Lq, D)
            return out
        key = jax.random.key(seed)
        ks = jax.random.split(key, 32)
        B, L, S, D, F = (2, 512, 512, D_MODEL, D_FF)
        std = 0.02
        inp = {'tgt': jax.random.normal(ks[0], (B, L, D), jnp.float32), 'memory': jax.random.normal(ks[1], (B, S, D), jnp.float32), 'tgt_mask': jnp.triu(jnp.ones((L, L), jnp.int32), k=1)}
        names = ['q', 'k', 'v', 'o', 'cq', 'ck', 'cv', 'co']
        for i, n in enumerate(names):
            inp[n + '_w'] = jax.random.normal(ks[2 + i], (D, D), jnp.float32) * std
            inp[n + '_b'] = jnp.zeros((D,), jnp.float32)
        inp['lin1_w'] = jax.random.normal(ks[12], (D, F), jnp.float32) * std
        inp['lin1_b'] = jnp.zeros((F,), jnp.float32)
        inp['lin2_w'] = jax.random.normal(ks[13], (F, D), jnp.float32) * std
        inp['lin2_b'] = jnp.zeros((D,), jnp.float32)
        for i, n in enumerate(['ln1', 'ln2', 'ln3']):
            inp[n + '_g'] = jnp.ones((D,), jnp.float32)
            inp[n + '_b'] = jnp.zeros((D,), jnp.float32)
        return inp
    _L2_xattn_all = _L2_xattn_setup()
    _L2_xattn_in = {k: v for k, v in _L2_xattn_all.items() if k in ('q_w', 'q_b', 'k_w', 'k_b', 'v_w', 'v_b', 'o_w', 'o_b', 'cq_w', 'cq_b', 'ck_w', 'ck_b', 'cv_w', 'cv_b', 'co_w', 'co_b', 'lin1_w', 'lin1_b', 'lin2_w', 'lin2_b', 'ln1_g', 'ln1_b', 'ln2_g', 'ln2_b', 'ln3_g', 'ln3_b')}
    del _L2_xattn_all

    def _L3_xattn_setup():
        import jax, jax.numpy as jnp
        import numpy as np
        D_MODEL = 256
        HEADS = 16
        D_K = D_MODEL // HEADS
        key = jax.random.key(seed)
        ks = jax.random.split(key, 12)
        B, S = (2, 512)
        s = 1.0 / np.sqrt(D_MODEL)
        return {'queries': jax.random.normal(ks[0], (B, S, D_MODEL), jnp.float32), 'keys': jax.random.normal(ks[1], (B, S, D_MODEL), jnp.float32), 'values': jax.random.normal(ks[2], (B, S, D_MODEL), jnp.float32), 'Wq': jax.random.normal(ks[3], (D_MODEL, D_MODEL), jnp.float32) * s, 'bq': jnp.zeros((D_MODEL,), jnp.float32), 'Wk': jax.random.normal(ks[4], (D_MODEL, D_MODEL), jnp.float32) * s, 'bk': jnp.zeros((D_MODEL,), jnp.float32), 'Wv': jax.random.normal(ks[5], (D_MODEL, D_MODEL), jnp.float32) * s, 'bv': jnp.zeros((D_MODEL,), jnp.float32), 'Wo': jax.random.normal(ks[6], (D_MODEL, D_MODEL), jnp.float32) * s, 'bo': jnp.zeros((D_MODEL,), jnp.float32), 'gamma': jnp.ones((D_MODEL,), jnp.float32), 'beta': jnp.zeros((D_MODEL,), jnp.float32)}
    _L3_xattn_all = _L3_xattn_setup()
    _L3_xattn_in = {k: v for k, v in _L3_xattn_all.items() if k in ('Wq', 'bq', 'Wk', 'bk', 'Wv', 'bv', 'Wo', 'bo', 'gamma', 'beta')}
    del _L3_xattn_all
    return {'x': x, 'ctx_1024': ctx_1024, 'mask_Bx1xS2_if1': mask_Bx1xS2_if1, 'mask_BxSxS2_ik0': mask_BxSxS2_ik0, 'mask_BxSxS2_if1': mask_BxSxS2_if1, 'mask_SxS_ik1': mask_SxS_ik1, 'L0_xattn_q1_w': _L0_xattn_in['q1_w'], 'L0_xattn_q1_b': _L0_xattn_in['q1_b'], 'L0_xattn_k1_w': _L0_xattn_in['k1_w'], 'L0_xattn_k1_b': _L0_xattn_in['k1_b'], 'L0_xattn_v1_w': _L0_xattn_in['v1_w'], 'L0_xattn_v1_b': _L0_xattn_in['v1_b'], 'L0_xattn_q2_w': _L0_xattn_in['q2_w'], 'L0_xattn_q2_b': _L0_xattn_in['q2_b'], 'L0_xattn_k2_w': _L0_xattn_in['k2_w'], 'L0_xattn_k2_b': _L0_xattn_in['k2_b'], 'L0_xattn_v2_w': _L0_xattn_in['v2_w'], 'L0_xattn_v2_b': _L0_xattn_in['v2_b'], 'L0_xattn_sa_qw': _L0_xattn_in['sa_qw'], 'L0_xattn_sa_qb': _L0_xattn_in['sa_qb'], 'L0_xattn_sa_kw': _L0_xattn_in['sa_kw'], 'L0_xattn_sa_kb': _L0_xattn_in['sa_kb'], 'L0_xattn_sa_vw': _L0_xattn_in['sa_vw'], 'L0_xattn_sa_vb': _L0_xattn_in['sa_vb'], 'L0_xattn_sa_ow': _L0_xattn_in['sa_ow'], 'L0_xattn_sa_ob': _L0_xattn_in['sa_ob'], 'L0_xattn_ed_qw': _L0_xattn_in['ed_qw'], 'L0_xattn_ed_qb': _L0_xattn_in['ed_qb'], 'L0_xattn_ed_kw': _L0_xattn_in['ed_kw'], 'L0_xattn_ed_kb': _L0_xattn_in['ed_kb'], 'L0_xattn_ed_vw': _L0_xattn_in['ed_vw'], 'L0_xattn_ed_vb': _L0_xattn_in['ed_vb'], 'L0_xattn_ed_ow': _L0_xattn_in['ed_ow'], 'L0_xattn_ed_ob': _L0_xattn_in['ed_ob'], 'L0_xattn_ff_w1': _L0_xattn_in['ff_w1'], 'L0_xattn_ff_b1': _L0_xattn_in['ff_b1'], 'L0_xattn_ff_w2': _L0_xattn_in['ff_w2'], 'L0_xattn_ff_b2': _L0_xattn_in['ff_b2'], 'L0_xattn_ln1_g': _L0_xattn_in['ln1_g'], 'L0_xattn_ln1_b': _L0_xattn_in['ln1_b'], 'L0_xattn_ln2_g': _L0_xattn_in['ln2_g'], 'L0_xattn_ln2_b': _L0_xattn_in['ln2_b'], 'L1_xattn_sa_wq': _L1_xattn_in['sa_wq'], 'L1_xattn_sa_bq': _L1_xattn_in['sa_bq'], 'L1_xattn_sa_wk': _L1_xattn_in['sa_wk'], 'L1_xattn_sa_bk': _L1_xattn_in['sa_bk'], 'L1_xattn_sa_wv': _L1_xattn_in['sa_wv'], 'L1_xattn_sa_bv': _L1_xattn_in['sa_bv'], 'L1_xattn_sa_wo': _L1_xattn_in['sa_wo'], 'L1_xattn_sa_bo': _L1_xattn_in['sa_bo'], 'L1_xattn_ca_wq': _L1_xattn_in['ca_wq'], 'L1_xattn_ca_bq': _L1_xattn_in['ca_bq'], 'L1_xattn_ca_wk': _L1_xattn_in['ca_wk'], 'L1_xattn_ca_bk': _L1_xattn_in['ca_bk'], 'L1_xattn_ca_wv': _L1_xattn_in['ca_wv'], 'L1_xattn_ca_bv': _L1_xattn_in['ca_bv'], 'L1_xattn_ca_wo': _L1_xattn_in['ca_wo'], 'L1_xattn_ca_bo': _L1_xattn_in['ca_bo'], 'L1_xattn_ff_w1': _L1_xattn_in['ff_w1'], 'L1_xattn_ff_b1': _L1_xattn_in['ff_b1'], 'L1_xattn_ff_w2': _L1_xattn_in['ff_w2'], 'L1_xattn_ff_b2': _L1_xattn_in['ff_b2'], 'L1_xattn_ln1_g': _L1_xattn_in['ln1_g'], 'L1_xattn_ln1_b': _L1_xattn_in['ln1_b'], 'L1_xattn_ln2_g': _L1_xattn_in['ln2_g'], 'L1_xattn_ln2_b': _L1_xattn_in['ln2_b'], 'L1_xattn_ln3_g': _L1_xattn_in['ln3_g'], 'L1_xattn_ln3_b': _L1_xattn_in['ln3_b'], 'L2_xattn_q_w': _L2_xattn_in['q_w'], 'L2_xattn_q_b': _L2_xattn_in['q_b'], 'L2_xattn_k_w': _L2_xattn_in['k_w'], 'L2_xattn_k_b': _L2_xattn_in['k_b'], 'L2_xattn_v_w': _L2_xattn_in['v_w'], 'L2_xattn_v_b': _L2_xattn_in['v_b'], 'L2_xattn_o_w': _L2_xattn_in['o_w'], 'L2_xattn_o_b': _L2_xattn_in['o_b'], 'L2_xattn_cq_w': _L2_xattn_in['cq_w'], 'L2_xattn_cq_b': _L2_xattn_in['cq_b'], 'L2_xattn_ck_w': _L2_xattn_in['ck_w'], 'L2_xattn_ck_b': _L2_xattn_in['ck_b'], 'L2_xattn_cv_w': _L2_xattn_in['cv_w'], 'L2_xattn_cv_b': _L2_xattn_in['cv_b'], 'L2_xattn_co_w': _L2_xattn_in['co_w'], 'L2_xattn_co_b': _L2_xattn_in['co_b'], 'L2_xattn_lin1_w': _L2_xattn_in['lin1_w'], 'L2_xattn_lin1_b': _L2_xattn_in['lin1_b'], 'L2_xattn_lin2_w': _L2_xattn_in['lin2_w'], 'L2_xattn_lin2_b': _L2_xattn_in['lin2_b'], 'L2_xattn_ln1_g': _L2_xattn_in['ln1_g'], 'L2_xattn_ln1_b': _L2_xattn_in['ln1_b'], 'L2_xattn_ln2_g': _L2_xattn_in['ln2_g'], 'L2_xattn_ln2_b': _L2_xattn_in['ln2_b'], 'L2_xattn_ln3_g': _L2_xattn_in['ln3_g'], 'L2_xattn_ln3_b': _L2_xattn_in['ln3_b'], 'L3_xattn_Wq': _L3_xattn_in['Wq'], 'L3_xattn_bq': _L3_xattn_in['bq'], 'L3_xattn_Wk': _L3_xattn_in['Wk'], 'L3_xattn_bk': _L3_xattn_in['bk'], 'L3_xattn_Wv': _L3_xattn_in['Wv'], 'L3_xattn_bv': _L3_xattn_in['bv'], 'L3_xattn_Wo': _L3_xattn_in['Wo'], 'L3_xattn_bo': _L3_xattn_in['bo'], 'L3_xattn_gamma': _L3_xattn_in['gamma'], 'L3_xattn_beta': _L3_xattn_in['beta']}

def reference(x, ctx_1024, mask_Bx1xS2_if1, mask_BxSxS2_ik0, mask_BxSxS2_if1, mask_SxS_ik1, L0_xattn_q1_w, L0_xattn_q1_b, L0_xattn_k1_w, L0_xattn_k1_b, L0_xattn_v1_w, L0_xattn_v1_b, L0_xattn_q2_w, L0_xattn_q2_b, L0_xattn_k2_w, L0_xattn_k2_b, L0_xattn_v2_w, L0_xattn_v2_b, L0_xattn_sa_qw, L0_xattn_sa_qb, L0_xattn_sa_kw, L0_xattn_sa_kb, L0_xattn_sa_vw, L0_xattn_sa_vb, L0_xattn_sa_ow, L0_xattn_sa_ob, L0_xattn_ed_qw, L0_xattn_ed_qb, L0_xattn_ed_kw, L0_xattn_ed_kb, L0_xattn_ed_vw, L0_xattn_ed_vb, L0_xattn_ed_ow, L0_xattn_ed_ob, L0_xattn_ff_w1, L0_xattn_ff_b1, L0_xattn_ff_w2, L0_xattn_ff_b2, L0_xattn_ln1_g, L0_xattn_ln1_b, L0_xattn_ln2_g, L0_xattn_ln2_b, L1_xattn_sa_wq, L1_xattn_sa_bq, L1_xattn_sa_wk, L1_xattn_sa_bk, L1_xattn_sa_wv, L1_xattn_sa_bv, L1_xattn_sa_wo, L1_xattn_sa_bo, L1_xattn_ca_wq, L1_xattn_ca_bq, L1_xattn_ca_wk, L1_xattn_ca_bk, L1_xattn_ca_wv, L1_xattn_ca_bv, L1_xattn_ca_wo, L1_xattn_ca_bo, L1_xattn_ff_w1, L1_xattn_ff_b1, L1_xattn_ff_w2, L1_xattn_ff_b2, L1_xattn_ln1_g, L1_xattn_ln1_b, L1_xattn_ln2_g, L1_xattn_ln2_b, L1_xattn_ln3_g, L1_xattn_ln3_b, L2_xattn_q_w, L2_xattn_q_b, L2_xattn_k_w, L2_xattn_k_b, L2_xattn_v_w, L2_xattn_v_b, L2_xattn_o_w, L2_xattn_o_b, L2_xattn_cq_w, L2_xattn_cq_b, L2_xattn_ck_w, L2_xattn_ck_b, L2_xattn_cv_w, L2_xattn_cv_b, L2_xattn_co_w, L2_xattn_co_b, L2_xattn_lin1_w, L2_xattn_lin1_b, L2_xattn_lin2_w, L2_xattn_lin2_b, L2_xattn_ln1_g, L2_xattn_ln1_b, L2_xattn_ln2_g, L2_xattn_ln2_b, L2_xattn_ln3_g, L2_xattn_ln3_b, L3_xattn_Wq, L3_xattn_bq, L3_xattn_Wk, L3_xattn_bk, L3_xattn_Wv, L3_xattn_bv, L3_xattn_Wo, L3_xattn_bo, L3_xattn_gamma, L3_xattn_beta):
    import jax
    import jax.numpy as jnp

    def _L0_xattn_ref(output_embs, encoder_output, inputs_padding_mask, outputs_padding_mask, q1_w, q1_b, k1_w, k1_b, v1_w, v1_b, q2_w, q2_b, k2_w, k2_b, v2_w, v2_b, sa_qw, sa_qb, sa_kw, sa_kb, sa_vw, sa_vb, sa_ow, sa_ob, ed_qw, ed_qb, ed_kw, ed_kb, ed_vw, ed_vb, ed_ow, ed_ob, ff_w1, ff_b1, ff_w2, ff_b2, ln1_g, ln1_b, ln2_g, ln2_b):
        import jax, jax.numpy as jnp
        import numpy as np
        B, SD, SE, DM, H, DK, DV, DFF = (4, 512, 512, 256, 8, 128, 128, 1024)
        NEG = -jnp.inf

        def _linear(x, w, b):
            return jnp.einsum('...i,oi->...o', x, w) + b

        def _layer_norm(x, g, b, eps=1e-05):
            mu = jnp.mean(x, axis=-1, keepdims=True)
            var = jnp.var(x, axis=-1, keepdims=True)
            return (x - mu) * jax.lax.rsqrt(var + eps) * g + b

        def _mha(Q, K, V, wq, bq, wk, bk, wv, bv, wo, bo, pad_mask, seq_mask):
            Qh = jnp.einsum('bsd,hkd->bhsk', Q, wq) + bq[None, :, None, :]
            Kh = jnp.einsum('bsd,hkd->bhsk', K, wk) + bk[None, :, None, :]
            Vh = jnp.einsum('bsd,hvd->bhsv', V, wv) + bv[None, :, None, :]
            scores = jnp.einsum('bhqd,bhkd->bhqk', Qh, Kh) / np.sqrt(DK)
            scores = jnp.where(pad_mask[:, None, :, :] == 0, NEG, scores)
            if seq_mask is not None:
                scores = jnp.where(seq_mask[None, None, :, :] == 0, NEG, scores)
            w = jax.nn.softmax(scores, axis=-1)
            out = jnp.einsum('bhqk,bhkv->bhqv', w, Vh)
            out = out.transpose(0, 2, 1, 3).reshape(Q.shape[0], Q.shape[1], H * DV)
            return _linear(out, wo, bo)
        seq_len = output_embs.shape[1]
        seq_mask = jnp.tril(jnp.ones((seq_len, seq_len), jnp.float32))
        Q = _linear(output_embs, q1_w, q1_b)
        K = _linear(output_embs, k1_w, k1_b)
        V = _linear(output_embs, v1_w, v1_b)
        x = output_embs + _mha(Q, K, V, sa_qw, sa_qb, sa_kw, sa_kb, sa_vw, sa_vb, sa_ow, sa_ob, outputs_padding_mask, seq_mask)
        x = _layer_norm(x, ln1_g, ln1_b)
        Q2 = _linear(x, q2_w, q2_b)
        K2 = _linear(encoder_output, k2_w, k2_b)
        V2 = _linear(encoder_output, v2_w, v2_b)
        y = output_embs + _mha(Q2, K2, V2, ed_qw, ed_qb, ed_kw, ed_kb, ed_vw, ed_vb, ed_ow, ed_ob, inputs_padding_mask, None)
        y = _layer_norm(y, ln2_g, ln2_b)
        ff = _linear(jax.nn.relu(_linear(y, ff_w1, ff_b1)), ff_w2, ff_b2)
        out = y + ff
        out = _layer_norm(out, ln2_g, ln2_b)
        return out

    def _L1_xattn_ref(x, enc_output, tgt_mask, memory_mask, sa_wq, sa_bq, sa_wk, sa_bk, sa_wv, sa_bv, sa_wo, sa_bo, ca_wq, ca_bq, ca_wk, ca_bk, ca_wv, ca_bv, ca_wo, ca_bo, ff_w1, ff_b1, ff_w2, ff_b2, ln1_g, ln1_b, ln2_g, ln2_b, ln3_g, ln3_b):
        import jax, jax.numpy as jnp
        import numpy as np
        B, S, D, H, DFF = (2, 512, 256, 16, 1024)
        DK = D // H
        LN_EPS = 1e-05

        def _mha(q, k, v, mask, wq, bq, wk, bk, wv, bv, wo, bo):
            b, sq, _ = q.shape
            sk = k.shape[1]
            Q = (q @ wq + bq).reshape(b, sq, H, DK).transpose(0, 2, 1, 3)
            K = (k @ wk + bk).reshape(b, sk, H, DK).transpose(0, 2, 1, 3)
            V = (v @ wv + bv).reshape(b, sk, H, DK).transpose(0, 2, 1, 3)
            scores = jnp.einsum('bhqd,bhkd->bhqk', Q, K) / np.float32(np.sqrt(DK))
            if mask is not None:
                scores = jnp.where(mask[:, None, :, :] == 0, jnp.float32(-1e+20), scores)
            A = jax.nn.softmax(scores, axis=-1)
            out = jnp.einsum('bhqk,bhkd->bhqd', A, V).transpose(0, 2, 1, 3).reshape(b, sq, D)
            return out @ wo + bo

        def _ln(x, g, b):
            m = jnp.mean(x, axis=-1, keepdims=True)
            v = jnp.var(x, axis=-1, keepdims=True)
            return (x - m) * jax.lax.rsqrt(v + LN_EPS) * g + b
        sa = _mha(x, x, x, tgt_mask, sa_wq, sa_bq, sa_wk, sa_bk, sa_wv, sa_bv, sa_wo, sa_bo)
        x = _ln(x + sa, ln1_g, ln1_b)
        ca = _mha(x, enc_output, enc_output, memory_mask, ca_wq, ca_bq, ca_wk, ca_bk, ca_wv, ca_bv, ca_wo, ca_bo)
        x = _ln(x + ca, ln2_g, ln2_b)
        ff = jax.nn.relu(x @ ff_w1 + ff_b1) @ ff_w2 + ff_b2
        x = _ln(x + ff, ln3_g, ln3_b)
        return x

    def _L2_xattn_ref(tgt, memory, tgt_mask, q_w, q_b, k_w, k_b, v_w, v_b, o_w, o_b, cq_w, cq_b, ck_w, ck_b, cv_w, cv_b, co_w, co_b, lin1_w, lin1_b, lin2_w, lin2_b, ln1_g, ln1_b, ln2_g, ln2_b, ln3_g, ln3_b):
        import jax, jax.numpy as jnp
        import numpy as np
        D_MODEL = 256
        N_HEAD = 16
        D_FF = 1024
        EPS = 1e-05

        def _linear(x, w, b):
            return jnp.einsum('bli,io->blo', x, w) + b

        def _layernorm(x, g, b):
            mu = jnp.mean(x, -1, keepdims=True)
            var = jnp.mean(jnp.square(x - mu), -1, keepdims=True)
            return (x - mu) * jax.lax.rsqrt(var + EPS) * g + b

        def _attention(q, k, v, mask):
            B, Lq, D = q.shape
            H = N_HEAD
            hd = D // H
            qh = q.reshape(B, Lq, H, hd)
            kh = k.reshape(B, k.shape[1], H, hd)
            vh = v.reshape(B, v.shape[1], H, hd)
            scores = jnp.einsum('bqhd,bkhd->bhqk', qh, kh) / jnp.sqrt(jnp.float32(hd)).astype(q.dtype)
            if mask is not None:
                scores = jnp.where(mask[None, None] != 0, jnp.finfo(scores.dtype).min, scores)
            p = jax.nn.softmax(scores, axis=-1)
            out = jnp.einsum('bhqk,bkhd->bqhd', p, vh).reshape(B, Lq, D)
            return out
        q = _linear(tgt, q_w, q_b)
        k = _linear(tgt, k_w, k_b)
        v = _linear(tgt, v_w, v_b)
        tgt2 = _linear(_attention(q, k, v, tgt_mask), o_w, o_b)
        x = _layernorm(tgt + tgt2, ln1_g, ln1_b)
        q = _linear(x, cq_w, cq_b)
        k = _linear(memory, ck_w, ck_b)
        v = _linear(memory, cv_w, cv_b)
        tgt2 = _linear(_attention(q, k, v, None), co_w, co_b)
        x = _layernorm(x + tgt2, ln2_g, ln2_b)
        tgt2 = _linear(jax.nn.relu(_linear(x, lin1_w, lin1_b)), lin2_w, lin2_b)
        x = _layernorm(x + tgt2, ln3_g, ln3_b)
        return x

    def _L3_xattn_ref(queries, keys, values, Wq, bq, Wk, bk, Wv, bv, Wo, bo, gamma, beta):
        import jax, jax.numpy as jnp
        import numpy as np
        D_MODEL = 256
        HEADS = 16
        D_K = D_MODEL // HEADS
        B, Nq, D = queries.shape
        Nk = keys.shape[1]
        q = (queries @ Wq.T + bq).reshape(B, Nq, HEADS, D_K).transpose(0, 2, 1, 3)
        k = (keys @ Wk.T + bk).reshape(B, Nk, HEADS, D_K).transpose(0, 2, 1, 3)
        v = (values @ Wv.T + bv).reshape(B, Nk, HEADS, D_K).transpose(0, 2, 1, 3)
        att = jnp.einsum('bhqd,bhkd->bhqk', q, k) / np.sqrt(D_K).astype(np.float32)
        att = jax.nn.softmax(att, axis=-1)
        out = jnp.einsum('bhqk,bhkd->bhqd', att, v)
        out = out.transpose(0, 2, 1, 3).reshape(B, Nq, HEADS * D_K)
        out = out @ Wo.T + bo
        out = queries + out
        mean = jnp.mean(out, axis=-1, keepdims=True)
        var = jnp.var(out, axis=-1, keepdims=True)
        out = (out - mean) / jnp.sqrt(var + 1e-05) * gamma + beta
        return out
    x = _L0_xattn_ref(x, ctx_1024, mask_Bx1xS2_if1, mask_Bx1xS2_if1, L0_xattn_q1_w, L0_xattn_q1_b, L0_xattn_k1_w, L0_xattn_k1_b, L0_xattn_v1_w, L0_xattn_v1_b, L0_xattn_q2_w, L0_xattn_q2_b, L0_xattn_k2_w, L0_xattn_k2_b, L0_xattn_v2_w, L0_xattn_v2_b, L0_xattn_sa_qw, L0_xattn_sa_qb, L0_xattn_sa_kw, L0_xattn_sa_kb, L0_xattn_sa_vw, L0_xattn_sa_vb, L0_xattn_sa_ow, L0_xattn_sa_ob, L0_xattn_ed_qw, L0_xattn_ed_qb, L0_xattn_ed_kw, L0_xattn_ed_kb, L0_xattn_ed_vw, L0_xattn_ed_vb, L0_xattn_ed_ow, L0_xattn_ed_ob, L0_xattn_ff_w1, L0_xattn_ff_b1, L0_xattn_ff_w2, L0_xattn_ff_b2, L0_xattn_ln1_g, L0_xattn_ln1_b, L0_xattn_ln2_g, L0_xattn_ln2_b)
    x = _L1_xattn_ref(x, ctx_1024, mask_BxSxS2_ik0, mask_BxSxS2_if1, L1_xattn_sa_wq, L1_xattn_sa_bq, L1_xattn_sa_wk, L1_xattn_sa_bk, L1_xattn_sa_wv, L1_xattn_sa_bv, L1_xattn_sa_wo, L1_xattn_sa_bo, L1_xattn_ca_wq, L1_xattn_ca_bq, L1_xattn_ca_wk, L1_xattn_ca_bk, L1_xattn_ca_wv, L1_xattn_ca_bv, L1_xattn_ca_wo, L1_xattn_ca_bo, L1_xattn_ff_w1, L1_xattn_ff_b1, L1_xattn_ff_w2, L1_xattn_ff_b2, L1_xattn_ln1_g, L1_xattn_ln1_b, L1_xattn_ln2_g, L1_xattn_ln2_b, L1_xattn_ln3_g, L1_xattn_ln3_b)
    x = _L2_xattn_ref(x, ctx_1024, mask_SxS_ik1, L2_xattn_q_w, L2_xattn_q_b, L2_xattn_k_w, L2_xattn_k_b, L2_xattn_v_w, L2_xattn_v_b, L2_xattn_o_w, L2_xattn_o_b, L2_xattn_cq_w, L2_xattn_cq_b, L2_xattn_ck_w, L2_xattn_ck_b, L2_xattn_cv_w, L2_xattn_cv_b, L2_xattn_co_w, L2_xattn_co_b, L2_xattn_lin1_w, L2_xattn_lin1_b, L2_xattn_lin2_w, L2_xattn_lin2_b, L2_xattn_ln1_g, L2_xattn_ln1_b, L2_xattn_ln2_g, L2_xattn_ln2_b, L2_xattn_ln3_g, L2_xattn_ln3_b)
    x = _L3_xattn_ref(x, ctx_1024, ctx_1024, L3_xattn_Wq, L3_xattn_bq, L3_xattn_Wk, L3_xattn_bk, L3_xattn_Wv, L3_xattn_bv, L3_xattn_Wo, L3_xattn_bo, L3_xattn_gamma, L3_xattn_beta)
    return x

_drawn_inputs = setup_inputs


def setup_inputs(seed=0):
    import zlib

    import numpy as np

    out = dict(_drawn_inputs(seed))
    spreads = {'L0_xattn_q1_b': (0.0, 0.8),
     'L0_xattn_k1_b': (0.0, 2.0),
     'L0_xattn_v1_b': (0.0, 0.8),
     'L0_xattn_q2_b': (0.0, 0.8),
     'L0_xattn_k2_b': (0.0, 2.0),
     'L0_xattn_v2_b': (0.0, 0.488),
     'L0_xattn_sa_qb': (0.0, 0.8),
     'L0_xattn_sa_kb': (0.0, 2.0),
     'L0_xattn_sa_vb': (0.0, 2.0),
     'L0_xattn_sa_ob': (0.0, 2.0),
     'L0_xattn_ed_qb': (0.0, 2.0),
     'L0_xattn_ed_kb': (0.0, 2.0),
     'L0_xattn_ed_vb': (0.0, 0.1),
     'L0_xattn_ed_ob': (0.0, 0.1),
     'L0_xattn_ff_b1': (0.0, 0.1),
     'L0_xattn_ff_b2': (0.0, 0.1),
     'L0_xattn_ln1_g': (1.0, 0.6),
     'L0_xattn_ln1_b': (0.0, 0.8),
     'L0_xattn_ln2_g': (1.0, 0.2),
     'L0_xattn_ln2_b': (0.0, 0.1),
     'L1_xattn_sa_bq': (0.0, 0.8),
     'L1_xattn_sa_bk': (0.0, 2.0),
     'L1_xattn_sa_bv': (0.0, 0.348),
     'L1_xattn_sa_bo': (0.0, 0.1),
     'L1_xattn_ca_bq': (0.0, 0.8),
     'L1_xattn_ca_bk': (0.0, 2.0),
     'L1_xattn_ca_bv': (0.0, 0.318),
     'L1_xattn_ca_bo': (0.0, 0.1),
     'L1_xattn_ff_b1': (0.0, 0.1),
     'L1_xattn_ff_b2': (0.0, 0.1),
     'L1_xattn_ln1_g': (1.0, 0.2),
     'L1_xattn_ln1_b': (0.0, 0.1),
     'L1_xattn_ln2_g': (1.0, 0.2),
     'L1_xattn_ln2_b': (0.0, 0.1),
     'L1_xattn_ln3_g': (1.0, 0.2),
     'L1_xattn_ln3_b': (0.0, 0.1),
     'L2_xattn_q_b': (0.0, 2.0),
     'L2_xattn_k_b': (0.0, 2.0),
     'L2_xattn_v_b': (0.0, 0.267),
     'L2_xattn_o_b': (0.0, 0.1),
     'L2_xattn_cq_b': (0.0, 0.8),
     'L2_xattn_ck_b': (0.0, 2.0),
     'L2_xattn_cv_b': (0.0, 0.274),
     'L2_xattn_co_b': (0.0, 0.1),
     'L2_xattn_lin1_b': (0.0, 0.1),
     'L2_xattn_lin2_b': (0.0, 0.1),
     'L2_xattn_ln1_g': (1.0, 0.2),
     'L2_xattn_ln1_b': (0.0, 0.1),
     'L2_xattn_ln2_g': (1.0, 0.2),
     'L2_xattn_ln2_b': (0.0, 0.1),
     'L2_xattn_ln3_g': (1.0, 0.2),
     'L2_xattn_ln3_b': (0.0, 0.1),
     'L3_xattn_bq': (0.0, 0.404),
     'L3_xattn_bk': (0.0, 2.0),
     'L3_xattn_bv': (0.0, 0.1),
     'L3_xattn_bo': (0.0, 0.1),
     'L3_xattn_gamma': (1.0, 0.2),
     'L3_xattn_beta': (0.0, 0.1)}
    factors = {'L0_xattn_q1_w': 8.0,
     'L0_xattn_k1_w': 8.0,
     'L0_xattn_v1_w': 8.0,
     'L0_xattn_q2_w': 8.0,
     'L0_xattn_k2_w': 8.0,
     'L0_xattn_sa_qw': 8.0,
     'L0_xattn_sa_kw': 8.0,
     'L0_xattn_sa_vw': 8.0,
     'L0_xattn_sa_ow': 8.0,
     'L0_xattn_ed_qw': 8.0,
     'L0_xattn_ed_kw': 8.0,
     'L1_xattn_sa_wq': 8.0,
     'L1_xattn_sa_wk': 8.0,
     'L1_xattn_ca_wq': 8.0,
     'L1_xattn_ca_wk': 8.0,
     'L2_xattn_q_w': 8.0,
     'L2_xattn_k_w': 8.0,
     'L2_xattn_cq_w': 8.0,
     'L2_xattn_ck_w': 8.0}
    for name, (base, spread) in spreads.items():
        noise = np.random.default_rng([zlib.crc32(name.encode()), seed]).standard_normal(out[name].shape)
        drawn = base * np.exp(spread * noise) if base else spread * noise
        out[name] = jnp.asarray(drawn.astype(out[name].dtype))
    for name, factor in factors.items():
        out[name] = (out[name] * factor).astype(out[name].dtype)
    return out
```

```python
from contextlib import ExitStack

import numpy as np
import concourse.bass as bass
from concourse import mybir

F32 = mybir.dt.float32
F32R = mybir.dt.float32r
BF16 = mybir.dt.bfloat16
I32 = mybir.dt.int32
ALU = mybir.AluOpType
ACT = mybir.ActivationFunctionType
AX_X = mybir.AxisListType.X

P = 128
BATCH, SEQ, DM, DFF = 32, 128, 256, 1024
G = 4
ROUNDS = BATCH // G
TOK = G * SEQ
C = DM // P
M = DFF // P
EPS = 1e-5


class Signal:

    def __init__(self, nc, ctx, name, per_round):
        self.sem = nc.alloc_semaphore(name)
        ctx.callback(nc.clear_and_free_semaphores, [self.sem])
        self.per_round = per_round

    def at(self, r, n):
        return r * self.per_round + n + 1 if self.per_round else n


class Kit:

    def __init__(self, nc, ctx, tag):
        self.nc, self.ctx, self.tag = nc, ctx, tag
        self.round_signals = []
        ctx.callback(nc.all_engine_barrier)
        self.gate = Signal(nc, ctx, f"{tag}_gate", 0)

    def sb(self, name, shape, dt):
        return self.ctx.enter_context(self.nc.sbuf_tensor(f"{self.tag}_{name}", shape, dt))

    def counter(self, name, per_round):
        signal = Signal(self.nc, self.ctx, f"{self.tag}_{name}", per_round)
        if per_round:
            self.round_signals.append(signal)
        return signal

    def gated(self, engine):
        engine.sem_inc(self.gate.sem, 1)

    def start(self, pe):
        for signal in self.round_signals:
            pe.sem_inc(signal.sem, 1)


class Split:

    def __init__(self, kit, name, shape):
        self.hi = kit.sb(name + "_hi", shape, F32R)
        self.lo = kit.sb(name + "_lo", shape, F32R)


def f32(ap):
    return ap.bitcast(F32)


def product(pe, out, stationary, moving, first, last, skip=False):
    n = 0
    total = 3 * len(stationary)
    for (w_hi, w_lo), (x_hi, x_lo) in zip(stationary, moving):
        for w, x in ((w_lo, x_hi), (w_hi, x_lo), (w_hi, x_hi)):
            ins = pe.matmul(out, w, x, start=first and n == 0, stop=last and n == total - 1,
                            skip_group_check=skip)
            n += 1
    return ins


class Banks:

    def __init__(self, psum):
        self.psum = psum
        self.read_by = {}

    def claim(self, pe, r, *banks):
        need = {}
        for b in banks:
            signal, n = self.read_by[b]
            need[signal] = max(n, need.get(signal, 0))
        for signal, n in need.items():
            pe.wait_ge(signal.sem, signal.at(r, n))

    def read(self, bank, signal, n):
        self.read_by[bank] = (signal, n)


Q_BANKS, K_BANKS, V_BANKS = (2, 3), (4, 5), (6, 7)
SCORE_BANKS = ((0, 1), (2, 3))
TURN_BANKS = (4, 5)
MIX_BANKS = (6, 7)
OUT_BANKS = (0, 1)
NORM_BANKS = (2, 3)
HIDDEN_BANKS = (4, 5, 2, 3)
FF_OUT_BANKS = (6, 7)
HIDDEN_SLOTS = 3

HEADS = 16
DK = DM // HEADS
UNITS = G * C
HU = HEADS // C


class Project16:

    def __init__(self, kit, name, w, sh):
        self.w, self.sh = w, sh
        self.q_in_psum = kit.counter(name + "_q_in_psum", C)
        self.q_ready = kit.counter(name + "_q_ready", C)
        self.k_in_psum = kit.counter(name + "_k_in_psum", C)
        self.k_ready = kit.counter(name + "_k_ready", C)
        self.k_blocked = [kit.counter(f"{name}_k_blocked{c}", 16 * HU) for c in range(C)]
        self.v_in_psum = kit.counter(name + "_v_in_psum", 2)
        self.v_ready = kit.counter(name + "_v_ready", 2)

    def pe_q(self, pe, r, banks, src):
        ps = banks.psum
        for c in range(C):
            banks.claim(pe, r, Q_BANKS[c])
            product(pe, ps[:, Q_BANKS[c], :],
                    [(self.w["q"].hi[:, k, c * P:(c + 1) * P], self.w["q"].lo[:, k, c * P:(c + 1) * P])
                     for k in range(C)],
                    [(src.hi[:, k, :], src.lo[:, k, :]) for k in range(C)],
                    True, True).then_inc(self.q_in_psum.sem, 1)
            banks.read(Q_BANKS[c], self.q_ready, c + 1)

    def pe_k(self, pe, r, banks, src):
        ps = banks.psum
        for c in range(C):
            banks.claim(pe, r, K_BANKS[c])
            product(pe, ps[:, K_BANKS[c], :],
                    [(self.w["k"].hi[:, k, c * P:(c + 1) * P], self.w["k"].lo[:, k, c * P:(c + 1) * P])
                     for k in range(C)],
                    [(src.hi[:, k, :], src.lo[:, k, :]) for k in range(C)],
                    True, True).then_inc(self.k_in_psum.sem, 1)
            banks.read(K_BANKS[c], self.k_ready, c + 1)

    def pe_v(self, pe, r, banks, src):
        ps = banks.psum
        for pair in range(2):
            banks.claim(pe, r, V_BANKS[pair])
            for b in (2 * pair, 2 * pair + 1):
                last = product(pe, ps[:, V_BANKS[pair], (b % 2) * DM:(b % 2 + 1) * DM],
                               [(src.hi[:, k, b * SEQ:(b + 1) * SEQ], src.lo[:, k, b * SEQ:(b + 1) * SEQ])
                                for k in range(C)],
                               [(self.w["v"].hi[:, k, :], self.w["v"].lo[:, k, :]) for k in range(C)],
                               True, True)
            last.then_inc(self.v_in_psum.sem, 1)
            banks.read(V_BANKS[pair], self.v_ready, pair + 1)

    def act_q(self, act, r, psum):
        for c in range(C):
            act.wait_ge(self.q_in_psum.sem, self.q_in_psum.at(r, c + 1))
            act.activation(self.sh.q[:, c, :], psum[:, Q_BANKS[c], :], ACT.Identity,
                           bias=self.w["q_bias"][:, c:c + 1], scale=DK ** -0.5) \
               .then_inc(self.q_ready.sem, 1)

    def dve_k(self, dve, r, psum, scattered_before):
        project, n = scattered_before
        for c in range(C):
            dve.wait_ge(project.k_blocked[c].sem, project.k_blocked[c].at(r, n))
            dve.wait_ge(self.k_in_psum.sem, self.k_in_psum.at(r, c + 1))
            dve.tensor_scalar(self.sh.k[:, c, :], psum[:, K_BANKS[c], :],
                              self.w["k_bias"][:, c:c + 1], None, ALU.add) \
               .then_inc(self.k_ready.sem, 1)

    def sp_k(self, sp, r):
        for c in range(C):
            sp.wait_ge(self.k_ready.sem, self.k_ready.at(r, c + 1))
            for e in range(2):
                for j in range(4):
                    rows = slice(32 * j + DK * e, 32 * j + DK * (e + 1))
                    sp.dma_start(self.sh.k_block[rows, c, e, j, :], self.sh.k[rows, c, :]) \
                      .then_inc(self.k_blocked[c].sem, 16)

    def dve_v(self, dve, r, psum):
        for b in range(G):
            dve.wait_ge(self.v_in_psum.sem, self.v_in_psum.at(r, b // 2 + 1))
            ins = dve.tensor_tensor(
                self.sh.v_slots[b],
                psum[:, V_BANKS[b // 2], (b % 2) * DM:(b % 2 + 1) * DM].rearrange(
                    "p (g e d) -> p g e d", e=2, d=DK),
                self.w["v_row"].rearrange("p (g e d) -> p g e d", e=2, d=DK), ALU.add)
            if b % 2:
                ins.then_inc(self.v_ready.sem, 1)


class Attend16:

    def __init__(self, kit, name, proj, mask, sh):
        self.proj, self.mask, self.sh = proj, mask, sh
        self.scores_ready = kit.counter(name + "_scores_ready", UNITS)
        self.max_ready = kit.counter(name + "_max_ready", UNITS)
        self.exp_done = kit.counter(name + "_exp_done", UNITS)
        self.inverse_made = kit.counter(name + "_inverse_made", G)
        self.inverse_ready = kit.counter(name + "_inverse_ready", G)
        self.turned = kit.counter(name + "_turned", 2 * UNITS)
        self.turned_ready = kit.counter(name + "_turned_ready", 2 * UNITS)
        self.mixed = kit.counter(name + "_mixed", G)
        self.spread_ready = kit.counter(name + "_spread_ready", G)
        self.normed = kit.counter(name + "_normed", G)
        self.hi_ready = kit.counter(name + "_hi_ready", G)
        self.lo_ready = kit.counter(name + "_lo_ready", G)

    def pe_scores(self, pe, r, banks, n):
        b, c = n // C, n % C
        if n < C:
            if n == 0:
                pe.wait_ge(self.proj.q_ready.sem, self.proj.q_ready.at(r, C))
            pe.wait_ge(self.proj.k_blocked[c].sem, self.proj.k_blocked[c].at(r, 16 * HU))
        if n == 0 and self.mask is not None:
            pe.wait_ge(self.mask.ready.sem, self.mask.ready.at(r, 1))
        if n != 1:
            banks.claim(pe, r, *SCORE_BANKS[c])
        for e in range(2):
            out = banks.psum[:, SCORE_BANKS[c][e], :].rearrange("p (j k) -> p j k", j=4)
            if self.mask is not None:
                flags = self.mask.flags[:, b if self.mask.per_batch else 0, :]
                pe.matmul(out, self.mask.value_eye[:], flags.unsqueeze(1).broadcast_to([P, 4, SEQ]),
                          start=True, stop=False)
            ins = pe.matmul(out, self.sh.q[:, c, b * SEQ:(b + 1) * SEQ],
                            self.sh.k_block[:, c, e, :, b * SEQ:(b + 1) * SEQ],
                            start=self.mask is None, stop=True)
        ins.then_inc(self.scores_ready.sem, 1)
        for bank in SCORE_BANKS[c]:
            banks.read(bank, self.exp_done, n + 1)

    def pe_turn(self, pe, r, banks, n):
        for e in range(2):
            u = 2 * n + e
            if e == 0:
                pe.wait_ge(self.exp_done.sem, self.exp_done.at(r, n + 1))
            banks.claim(pe, r, TURN_BANKS[e])
            for j in range(4):
                ins = pe.transpose(banks.psum[:, TURN_BANKS[e], j * SEQ:(j + 1) * SEQ],
                                   self.sh.p[:, n % 2, 4 * e + j, :], self.sh.eye[:])
            ins.then_inc(self.turned.sem, 1)
            banks.read(TURN_BANKS[e], self.turned_ready, u + 1)

    def pe_mix(self, pe, r, banks, n):
        b, c = n // C, n % C
        bank = MIX_BANKS[b % 2]
        if n == 0:
            pe.wait_ge(self.proj.v_ready.sem, self.proj.v_ready.at(r, 2))
        if c == 0:
            banks.claim(pe, r, bank)
        for e in range(2):
            u = 2 * n + e
            pe.wait_ge(self.turned_ready.sem, self.turned_ready.at(r, u + 1))
            for j in range(4):
                pe.matmul(banks.psum[32 * j:32 * j + 32, bank, c * SEQ:(c + 1) * SEQ],
                          self.sh.v[:, b, c, j, e, :], self.sh.p_turned[:, u % 4, j, :],
                          start=e == 0, stop=e == 1)
        if c == 1:
            pe.wait_ge(self.inverse_ready.sem, self.inverse_ready.at(r, b + 1))
            for k in range(C):
                ins = pe.transpose(banks.psum[:, bank, DM + k * SEQ:DM + (k + 1) * SEQ],
                                   self.sh.inverse_row[:, b % 2, k * P:(k + 1) * P], self.sh.eye[:])
            ins.then_inc(self.mixed.sem, 1)
            banks.read(bank, self.normed, b + 1)

    def pe(self, pe, r, banks):
        for n in range(UNITS + 2):
            if n == 0:
                self.pe_scores(pe, r, banks, 0)
            if n + 1 < UNITS:
                self.pe_scores(pe, r, banks, n + 1)
            if n < UNITS:
                self.pe_turn(pe, r, banks, n)
            if 1 <= n <= UNITS:
                self.pe_mix(pe, r, banks, n - 1)

    def dve_max(self, dve, r, psum, n):
        dve.wait_ge(self.scores_ready.sem, self.scores_ready.at(r, n + 1))
        c = n % C
        s = psum[:, SCORE_BANKS[c][0]:SCORE_BANKS[c][1] + 1, :].rearrange("p e (j k) -> p (e j) k", j=4)
        dve.tensor_reduce(self.sh.neg_max[:, n % 2, :], s, AX_X, ALU.max, negate=True) \
           .then_inc(self.max_ready.sem, 1)

    def dve_turned(self, dve, r, psum, n):
        for e in range(2):
            u = 2 * n + e
            dve.wait_ge(self.turned.sem, self.turned.at(r, u + 1))
            dve.tensor_copy(self.sh.p_turned[:, u % 4, :, :],
                            psum[:, TURN_BANKS[e], :].rearrange("p (j k) -> p j k", j=4)) \
               .then_inc(self.turned_ready.sem, 1)

    def dve(self, dve, r, psum):
        sh = self.sh
        for n in range(UNITS + 2):
            b, c = n // C, n % C
            if n == 0:
                self.dve_max(dve, r, psum, 0)
            if n + 1 < UNITS:
                self.dve_max(dve, r, psum, n + 1)
            if n < UNITS and c == 1:
                dve.wait_ge(self.exp_done.sem, self.exp_done.at(r, n + 1))
                dve.reciprocal(sh.inverse[:, b % 2, :], sh.sums[:, b % 2, :]) \
                   .then_inc(self.inverse_made.sem, 1)
                dve.wait_ge(self.inverse_made.sem, self.inverse_made.at(r, b + 1))
                for k in range(C):
                    ins = dve.tensor_copy(
                        sh.inverse_row[:, b % 2, k * P:(k + 1) * P].rearrange(
                            "p (j e d) -> p j e d", j=4, e=2),
                        sh.inverse[:, b % 2, k * HU:(k + 1) * HU].rearrange(
                            "p (e j) -> p j e", e=2).unsqueeze(3).broadcast_to([P, 4, 2, DK]))
                ins.then_inc(self.inverse_ready.sem, 1)
            if n < UNITS:
                self.dve_turned(dve, r, psum, n)
            if n >= 2 and c == 1:
                self.dve_norm(dve, r, psum, b - 1)

    def dve_norm(self, dve, r, psum, b):
        dve.wait_ge(self.spread_ready.sem, self.spread_ready.at(r, b + 1))
        if b >= 2:
            dve.wait_ge(self.lo_ready.sem, self.lo_ready.at(r, b - 1))
            dve.wait_ge(self.hi_ready.sem, self.hi_ready.at(r, b - 1))
        dve.tensor_tensor(self.sh.mix[:, b % 2, :], psum[:, MIX_BANKS[b % 2], 0:DM],
                          self.sh.spread[:, b % 2, :], ALU.mult).then_inc(self.normed.sem, 1)

    def act(self, act, r, psum):
        sh = self.sh
        for n in range(UNITS + 2):
            b, c = n // C, n % C
            if n < UNITS:
                act.wait_ge(self.max_ready.sem, self.max_ready.at(r, n + 1))
                for i in range(HU):
                    ins = act.activation(
                        sh.p[:, n % 2, i, :],
                        psum[:, SCORE_BANKS[c][i // 4], (i % 4) * SEQ:(i % 4 + 1) * SEQ],
                        ACT.Exp, bias=sh.neg_max[:, n % 2, i:i + 1],
                        accum_out=sh.sums[:, b % 2, c * HU + i:c * HU + i + 1])
                ins.then_inc(self.exp_done.sem, 1)
            if n >= 2 and c == 0:
                act.wait_ge(self.mixed.sem, self.mixed.at(r, b))
                act.copy(sh.spread[:, (b - 1) % 2, :], psum[:, MIX_BANKS[(b - 1) % 2], DM:2 * DM]) \
                   .then_inc(self.spread_ready.sem, 1)
            if n >= 2 and c == 1:
                act.wait_ge(self.normed.sem, self.normed.at(r, b))
                act.copy(sh.attended.hi[:, :, (b - 1) * SEQ:b * SEQ],
                         sh.mix[:, (b - 1) % 2, :].rearrange("p (c q) -> p c q", c=C)) \
                   .then_inc(self.hi_ready.sem, 1)

    def pool(self, pool, r):
        sh = self.sh
        for b in range(G):
            pool.wait_ge(self.hi_ready.sem, self.hi_ready.at(r, b + 1))
            pool.tensor_tensor(sh.attended.lo[:, :, b * SEQ:(b + 1) * SEQ],
                               sh.mix[:, b % 2, :].rearrange("p (c q) -> p c q", c=C),
                               f32(sh.attended.hi[:, :, b * SEQ:(b + 1) * SEQ]),
                               ALU.subtract).then_inc(self.lo_ready.sem, 1)


class OutProject:

    def __init__(self, kit, name, attend, w, sh):
        self.attend, self.w, self.sh = attend, w, sh
        self.out_ready = kit.counter(name + "_out_ready", 2)

    def pe(self, pe, r, banks, reader):
        for b in range(G):
            if b % 2 == 0:
                banks.claim(pe, r, OUT_BANKS[b // 2])
            pe.wait_ge(self.attend.lo_ready.sem, self.attend.lo_ready.at(r, b + 1))
            at = self.sh.attended
            ins = product(pe, banks.psum[:, OUT_BANKS[b // 2], (b % 2) * DM:(b % 2 + 1) * DM],
                          [(at.hi[:, k, b * SEQ:(b + 1) * SEQ], at.lo[:, k, b * SEQ:(b + 1) * SEQ])
                           for k in range(C)],
                          [(self.w.hi[:, k, :], self.w.lo[:, k, :]) for k in range(C)], True, True)
            if b % 2:
                ins.then_inc(self.out_ready.sem, 1)
                banks.read(OUT_BANKS[b // 2], reader, b // 2 + 1)


class Norm:

    def __init__(self, kit, name, source, source_banks, gain, shift, gain_row, shift_row, sh,
                 norm_banks=NORM_BANKS):
        self.source, self.source_banks, self.norm_banks = source, source_banks, norm_banks
        self.gain, self.shift, self.gain_row, self.shift_row = gain, shift, gain_row, shift_row
        self.sh, self.gate = sh, kit.gate
        self.sum_ready = kit.counter(name + "_sum_ready", 2)
        self.stats_made = kit.counter(name + "_stats_made", G)
        self.moments_ready = kit.counter(name + "_moments_ready", G)
        self.var_made = kit.counter(name + "_var_made", 2)
        self.rstd_made = kit.counter(name + "_rstd_made", 2)
        self.hat_ready = kit.counter(name + "_hat_ready", G)
        self.hat_turned = kit.counter(name + "_hat_turned", 2)
        self.turned_ready = kit.counter(name + "_turned_ready", 2)
        self.hi_ready = kit.counter(name + "_hi_ready", 2)
        self.lo_ready = kit.counter(name + "_lo_ready", 2)
        self.scaled = kit.counter(name + "_scaled", 2)
        self.rows_ready = kit.counter(name + "_rows_ready", 2)

    def dve_sum(self, dve, r, psum, residual, hat_read):
        sh = self.sh
        for pair in range(2):
            dve.wait_ge(residual[0].sem, residual[0].at(r, residual[1] if residual[1] == 1 else pair + 1))
            if pair == 0 and hat_read is not None:
                dve.wait_ge(hat_read[0].sem, hat_read[0].at(r, hat_read[1]))
            dve.wait_ge(self.source.sem, self.source.at(r, pair + 1))
            bank = self.source_banks[pair]
            dve.tensor_tensor(sh.z[:, 2 * pair:2 * pair + 2, :],
                              psum[:, bank, :].rearrange("p (b f) -> p b f", b=2),
                              sh.residual[:, 2 * pair:2 * pair + 2, :], ALU.add) \
               .then_inc(self.sum_ready.sem, 1)
            dve.wait_ge(self.sum_ready.sem, self.sum_ready.at(r, pair + 1))
            for b in (2 * pair, 2 * pair + 1):
                dve.bn_stats(sh.stats[:, b, :], sh.z[:, b, :]).then_inc(self.stats_made.sem, 1)
            for b in (2 * pair, 2 * pair + 1):
                dve.wait_ge(self.stats_made.sem, self.stats_made.at(r, b + 1))
                dve.sem_inc(self.gate.sem, 1)
                dve.bn_aggr(sh.moments[:, b, :], sh.stats[:, b, :]).then_inc(self.moments_ready.sem, 1)

    def pool(self, pool, r, rows_read=None):
        sh = self.sh
        for pair in range(2):
            two = slice(2 * pair, 2 * pair + 2)
            pool.wait_ge(self.moments_ready.sem, self.moments_ready.at(r, 2 * pair + 2))
            pool.sem_inc(self.gate.sem, 1)
            pool.tensor_scalar(sh.variance[:, two], sh.moments[:, two, 1], EPS, None, ALU.add) \
                .then_inc(self.var_made.sem, 1)
            pool.wait_ge(self.var_made.sem, self.var_made.at(r, pair + 1))
            pool.tensor_tensor(sh.rstd[:, two], sh.variance[:, two], sh.minus_half[:, 0:2], ALU.pow) \
                .then_inc(self.rstd_made.sem, 1)
            pool.wait_ge(self.rstd_made.sem, self.rstd_made.at(r, pair + 1))
            pool.sem_inc(self.gate.sem, 1)
            for b in (2 * pair, 2 * pair + 1):
                pool.tensor_scalar(sh.z[:, b, :], sh.z[:, b, :], sh.moments[:, b, 0:1],
                                   sh.rstd[:, b:b + 1], ALU.subtract, ALU.mult) \
                    .then_inc(self.hat_ready.sem, 1)
        if self.gain_row is None:
            return
        for pair in range(2):
            two = slice(2 * pair, 2 * pair + 2)
            pool.wait_ge(self.hat_ready.sem, self.hat_ready.at(r, 2 * pair + 2))
            pool.tensor_tensor(sh.residual[:, two, :], sh.z[:, two, :],
                               self.gain_row.unsqueeze(1).broadcast_to([P, 2, DM]), ALU.mult) \
                .then_inc(self.scaled.sem, 1)
            pool.wait_ge(self.scaled.sem, self.scaled.at(r, pair + 1))
            pool.tensor_tensor(sh.residual[:, two, :], sh.residual[:, two, :],
                               self.shift_row.unsqueeze(1).broadcast_to([P, 2, DM]), ALU.add) \
                .then_inc(self.rows_ready.sem, 1)

    def pe(self, pe, r, banks):
        for pair in range(2):
            bank = self.norm_banks[pair]
            banks.claim(pe, r, bank)
            pe.wait_ge(self.hat_ready.sem, self.hat_ready.at(r, 2 * pair + 2))
            for k in range(C):
                for b in range(2):
                    at = (2 * k + b) * SEQ
                    ins = pe.transpose(banks.psum[:, bank, at:at + SEQ],
                                       self.sh.z[:, 2 * pair + b, k * P:(k + 1) * P], self.sh.eye[:])
            ins.then_inc(self.hat_turned.sem, 1)
            banks.read(bank, self.turned_ready, pair + 1)

    def act(self, act, r, psum, y_read):
        for pair in range(2):
            bank = self.norm_banks[pair]
            act.wait_ge(self.hat_turned.sem, self.hat_turned.at(r, pair + 1))
            if pair == 0 and y_read is not None:
                act.wait_ge(y_read[0].sem, y_read[0].at(r, y_read[1]))
            for k in range(C):
                ins = act.activation(self.sh.y[:, pair, k, :], psum[:, bank, 2 * k * SEQ:(2 * k + 2) * SEQ],
                                     ACT.Identity, bias=self.shift[:, k:k + 1],
                                     scale=self.gain[:, k:k + 1])
            ins.then_inc(self.turned_ready.sem, 1)

    def dve_split(self, dve, r, stored=None):
        sh = self.sh
        if stored is not None:
            dve.wait_ge(stored[0].sem, stored[0].at(r, stored[1]))
        for pair in range(2):
            cols = slice(2 * pair * SEQ, (2 * pair + 2) * SEQ)
            dve.wait_ge(self.turned_ready.sem, self.turned_ready.at(r, pair + 1))
            dve.tensor_copy(sh.yt.hi[:, :, cols], sh.y[:, pair, :, :]).then_inc(self.hi_ready.sem, 1)
            dve.wait_ge(self.hi_ready.sem, self.hi_ready.at(r, pair + 1))
            dve.tensor_tensor(sh.yt.lo[:, :, cols], sh.y[:, pair, :, :], f32(sh.yt.hi[:, :, cols]),
                              ALU.subtract).then_inc(self.lo_ready.sem, 1)


class FeedForward:

    def __init__(self, kit, name, w1, w2, b1, sh):
        self.w1, self.w2, self.b1, self.sh = w1, w2, b1, sh
        self.hidden_in_psum = kit.counter(name + "_hidden_in_psum", M)
        self.hidden_ready = kit.counter(name + "_hidden_ready", M)
        self.hi_ready = kit.counter(name + "_hidden_hi", M)
        self.lo_ready = kit.counter(name + "_hidden_lo", M)
        self.out_ready = kit.counter(name + "_ff_out", 2)

    def pe(self, pe, r, banks, y_ready, reader):
        yt, h = self.sh.yt, self.sh.hidden
        pe.wait_ge(y_ready.sem, y_ready.at(r, 2))
        for m in range(M + 2):
            if m < M:
                bank = HIDDEN_BANKS[m % 4]
                banks.claim(pe, r, bank)
                product(pe, banks.psum[:, bank, :],
                        [(self.w1.hi[:, k, m * P:(m + 1) * P], self.w1.lo[:, k, m * P:(m + 1) * P])
                         for k in range(C)],
                        [(yt.hi[:, k, :], yt.lo[:, k, :]) for k in range(C)],
                        True, True).then_inc(self.hidden_in_psum.sem, 1)
                banks.read(bank, self.hidden_ready, m + 1)
            if m == 0:
                banks.claim(pe, r, *FF_OUT_BANKS)
            if m >= 2:
                i = m - 2
                pe.wait_ge(self.lo_ready.sem, self.lo_ready.at(r, i + 1))
                for b in range(G):
                    cols = slice(b * SEQ, (b + 1) * SEQ)
                    ins = product(pe, banks.psum[:, FF_OUT_BANKS[b // 2], (b % 2) * DM:(b % 2 + 1) * DM],
                                  [(h.hi[:, i % HIDDEN_SLOTS, cols], h.lo[:, i % HIDDEN_SLOTS, cols])],
                                  [(self.w2.hi[:, i, :], self.w2.lo[:, i, :])],
                                  i == 0 and b % 2 == 0, i == M - 1 and b % 2 == 1, skip=True)
                    if i == M - 1 and b % 2:
                        ins.then_inc(self.out_ready.sem, 1)
        for pair in range(2):
            banks.read(FF_OUT_BANKS[pair], reader, pair + 1)

    def act(self, act, r, psum):
        for m in range(M):
            act.wait_ge(self.hidden_in_psum.sem, self.hidden_in_psum.at(r, m + 1))
            if m >= 2:
                act.wait_ge(self.lo_ready.sem, self.lo_ready.at(r, m - 1))
            act.activation(self.sh.relu[:, m % 2, :], psum[:, HIDDEN_BANKS[m % 4], :], ACT.Relu,
                           bias=self.b1[:, m:m + 1]).then_inc(self.hidden_ready.sem, 1)

    def dve(self, dve, r):
        for m in range(M):
            dve.wait_ge(self.hidden_ready.sem, self.hidden_ready.at(r, m + 1))
            dve.tensor_copy(self.sh.hidden.hi[:, m % HIDDEN_SLOTS, :], self.sh.relu[:, m % 2, :]) \
               .then_inc(self.hi_ready.sem, 1)

    def pool(self, pool, r):
        for m in range(M):
            pool.wait_ge(self.hi_ready.sem, self.hi_ready.at(r, m + 1))
            pool.tensor_tensor(self.sh.hidden.lo[:, m % HIDDEN_SLOTS, :], self.sh.relu[:, m % 2, :],
                               f32(self.sh.hidden.hi[:, m % HIDDEN_SLOTS, :]), ALU.subtract) \
                .then_inc(self.lo_ready.sem, 1)


class Mask:

    def __init__(self, kit, name, nonzero_masked, value_eye, per_batch):
        self.nonzero_masked, self.value_eye, self.per_batch = nonzero_masked, value_eye, per_batch
        self.gate = kit.gate
        width = G if per_batch else 1
        self.ints = kit.sb(name + "_ints", [P, width, SEQ], I32)
        self.flags = kit.sb(name + "_flags", [P, width, SEQ], BF16)
        self.loaded = kit.counter(name + "_loaded", 16 if per_batch else 0)
        self.ready = kit.counter(name + "_flags_ready", 1 if per_batch else 0)

    def sp(self, sp, r, src):
        if self.per_batch:
            sp.wait_ge(self.ready.sem, self.ready.at(r, 0))
            sp.sem_inc(self.gate.sem, 1)
        sp.dma_start(self.ints[:], src).then_inc(self.loaded.sem, 16)

    def pool(self, pool, r, scores_read=None):
        if scores_read is not None:
            pool.wait_ge(scores_read.sem, scores_read.at(r, 0))
        pool.wait_ge(self.loaded.sem, self.loaded.at(r, 16))
        pool.sem_inc(self.gate.sem, 1)
        if self.nonzero_masked:
            pool.tensor_scalar(self.flags[:], self.ints[:], 0.0, 0.0, ALU.is_equal, ALU.is_equal) \
                .then_inc(self.ready.sem, 1)
        else:
            pool.tensor_scalar(self.flags[:], self.ints[:], 0.0, None, ALU.is_equal) \
                .then_inc(self.ready.sem, 1)


class Shared16:

    def __init__(self, kit, feed_forward):
        sb = kit.sb
        self.k_block = sb("k_block", [P, C, 2, 4, TOK], F32)
        self.q = sb("q", [P, C, TOK], F32)
        self.k = sb("k", [P, C, TOK], F32)
        self.v = sb("v", [P, G, C, 4, 2, 32], F32)
        self.p = sb("p", [P, 2, HU, SEQ], F32)
        self.p_turned = sb("p_turned", [P, 4, 4, SEQ], F32)
        self.neg_max = sb("neg_max", [P, 2, HU], F32)
        self.sums = sb("sums", [P, 2, HEADS], F32)
        self.inverse = sb("inverse", [P, 2, HEADS], F32)
        both = sb("inverse_row_and_spread", [P, 4, DM], F32)
        self.inverse_row, self.spread = both[:, 0:2, :], both[:, 2:4, :]
        self.y = both[:].rearrange("p (s c) t -> p s c t", s=2)
        self.mix = sb("mix", [P, 2, DM], F32)
        self.attended = Split(kit, "attended", [P, C, TOK])
        self.z = sb("z", [P, G, DM], F32)
        self.residual = sb("residual", [P, G, DM], F32)
        self.stats = sb("stats", [P, G, 6], F32)
        self.moments = sb("moments", [P, G, 2], F32)
        self.variance = sb("variance", [P, G], F32)
        self.rstd = sb("rstd", [P, G], F32)
        self.minus_half = sb("minus_half", [P, 4], F32)
        self.eye = sb("eye", [P, P], F32)
        self.v_slots = [self.v[:, b].rearrange("p c j e f -> p (c j) (e f)").rearrange(
            "p g (x d) -> p g x d", d=DK)[:, :, 0:4:3, :] for b in range(G)]
        if feed_forward:
            self.yt = Split(kit, "yt", [P, C, TOK])
            self.relu = self.p_turned[:].rearrange("p u j q -> p (u j q)").rearrange(
                "p (s t) -> p s t", t=TOK)
            self.hidden = Split(kit, "hidden", [P, HIDDEN_SLOTS, TOK])


class View:

    def __init__(self, split, cut):
        self.hi, self.lo = cut(split.hi), cut(split.lo)


STAGE_COLS = 2048


FULL_COLS = dict(q1=0, k1=2, q2=4, k2=6, g1=8, s1=10, g2=12, s2=14, g3=16, s3=18, ff=20)
FULL_ROWS = ["v1", "v2", "o1", "g1", "s1", "g2", "s2", "g3", "s3", "o2", "ff"]
LAST_COLS = dict(q1=0, k1=2)
LAST_ROWS = ["v1", "o1", "g1", "s1"]


def phase16(nc, tag, full, x, ctx_t, masks, packed, cols, rows, out):
    with ExitStack() as ctx:
        kit = Kit(nc, ctx, tag)
        sh = Shared16(kit, full)
        psum = ctx.enter_context(nc.psum_tensor(f"{tag}_psum", [P, 8, 512], F32))
        col = kit.sb("cols", list(cols.shape), F32)
        names = FULL_ROWS if full else LAST_ROWS
        at_col = FULL_COLS if full else LAST_COLS
        extra = 2 if full else 0
        row = kit.sb("rows", [P, len(names) - extra, DM], F32)
        n_cols = packed.shape[1]
        weights = Split(kit, "w", [P, n_cols])
        xt = Split(kit, "xt", [P, C, TOK])
        ct = Split(kit, "ct", [P, C, TOK])
        x_rows = kit.sb("x_rows", [P, G, DM], F32)
        stage = sh.k_block[:].rearrange("p c e j t -> p (c e j t)")

        def take(at, width, inner):
            return View(weights, lambda t: t[:, at:at + width].rearrange("p (c n) -> p c n", n=inner))

        def rowv(name):
            i = names.index(name)
            return row[:, i, :] if i < len(names) - extra else sh.z[:, i - len(names) + extra, :]

        def colv(name, n=2):
            return col[:, at_col[name]:at_col[name] + n]

        W1, W2 = 4 * 512 * (2 if full else 1), 4 * 512 * (2 if full else 1) + 2048
        wq = [take(i * 2048, 512, DM) for i in range(2 if full else 1)]
        wk = [take(i * 2048 + 512, 512, DM) for i in range(2 if full else 1)]
        wv = [take(i * 2048 + 1024, 512, DM) for i in range(2 if full else 1)]
        wo = [take(i * 2048 + 1536, 512, DM) for i in range(2 if full else 1)]

        def weights_of(i):
            n = str(i + 1)
            return {"q": wq[i], "k": wk[i], "v": wv[i], "q_bias": colv("q" + n), "k_bias": colv("k" + n),
                    "v_row": rowv("v" + n)}

        small_loaded = kit.counter("small_loaded", 0)
        hi_made = kit.counter("w_hi_made", 0)
        lo_made = kit.counter("w_lo_made", 0)
        consts = kit.counter("consts", 0)
        biases = kit.counter("biases", 0)
        zeroed = kit.counter("zeroed", 0)
        slots = n_cols // STAGE_COLS
        stage_loaded = [kit.counter(f"stage_loaded{s}", 0) for s in range(slots)]

        x_loaded = kit.counter("x_loaded", 32)
        ct_loaded = kit.counter("ct_loaded", 32)
        rows_loaded = kit.counter("rows_loaded", 16)
        residual_ready = kit.counter("residual_ready", 1)
        stored = kit.counter("stored", 48 if full else 16)

        def mask_of(name, spec):
            if spec is None:
                return None
            src, nonzero_masked, value, per_batch = spec
            eye = kit.sb(name + "_eye", [P, P], BF16)
            m = Mask(kit, name, nonzero_masked, eye, per_batch)
            m.src, m.value = src, value
            return m

        mask = [mask_of(f"mask{i + 1}", spec) for i, spec in enumerate(masks)]
        proj = [Project16(kit, f"a{i + 1}", weights_of(i), sh) for i in range(2 if full else 1)]
        att = [Attend16(kit, f"a{i + 1}", proj[i], mask[i], sh) for i in range(2 if full else 1)]
        outp = [OutProject(kit, f"o{i + 1}", att[i], wo[i], sh) for i in range(2 if full else 1)]
        norm = [Norm(kit, f"n{i + 1}", outp[i].out_ready, OUT_BANKS,
                     colv(f"g{i + 1}") if full else None, colv(f"s{i + 1}") if full else None,
                     rowv(f"g{i + 1}"), rowv(f"s{i + 1}"), sh) for i in range(2 if full else 1)]
        if full:
            w1 = take(W1, 2048, DFF)
            w2 = take(W2, 2048, DM)
            ff = FeedForward(kit, "ff", w1, w2, colv("ff", M), sh)
            norm.append(Norm(kit, "n3", ff.out_ready, FF_OUT_BANKS, colv("g3"), colv("s3"),
                             rowv("g3"), rowv("s3"), sh))
        final = norm[-1]

        block = ctx.enter_context(nc.Block())

        @block.sync
        def _(sp):
            sp.dma_start(col[:], cols).then_inc(small_loaded.sem, 16)
            for i in range(len(names)):
                sp.dma_start(rowv(names[i]), rows[i:i + 1, :].broadcast_to([P, DM])) \
                  .then_inc(small_loaded.sem, 16)
            for s in range(slots):
                sp.dma_start(stage[:, s * STAGE_COLS:(s + 1) * STAGE_COLS],
                             packed[:, s * STAGE_COLS:(s + 1) * STAGE_COLS]) \
                  .then_inc(stage_loaded[s].sem, 16)
            for m in mask:
                if m is not None and not m.per_batch:
                    m.sp(sp, 0, m.src)

            def load_x(r):
                tok = bass.ds(r * TOK, TOK)
                sp.wait_ge(proj[0].v_in_psum.sem, proj[0].v_in_psum.at(r, 0))
                if not full:
                    sp.wait_ge(proj[0].q_in_psum.sem, proj[0].q_in_psum.at(r, 0))
                kit.gated(sp)
                sp.dma_start(f32(xt.hi[:]), x[0][:, tok].rearrange("(c p) t -> p c t", p=P)) \
                  .then_inc(x_loaded.sem, 16)
                sp.dma_start(f32(xt.lo[:]), x[1][:, tok].rearrange("(c p) t -> p c t", p=P)) \
                  .then_inc(x_loaded.sem, 16)
                sp.wait_ge(residual_ready.sem, residual_ready.at(r, 0))
                kit.gated(sp)
                sp.dma_start(x_rows[:], x[2][tok, :].rearrange("(b t) f -> t b f", b=G)) \
                  .then_inc(rows_loaded.sem, 16)
                for m in mask:
                    if m is not None and m.per_batch:
                        m.sp(sp, r, m.src[bass.ds(r * G, G)].rearrange("b q k -> q b k"))

            def load_context(r):
                tok = bass.ds(r * TOK, TOK)
                sp.wait_ge(proj[-1].v_in_psum.sem, proj[-1].v_in_psum.at(r, 0))
                kit.gated(sp)
                sp.dma_start(f32(ct.hi[:]), ctx_t[0][:, tok].rearrange("(c p) t -> p c t", p=P)) \
                  .then_inc(ct_loaded.sem, 16)
                sp.dma_start(f32(ct.lo[:]), ctx_t[1][:, tok].rearrange("(c p) t -> p c t", p=P)) \
                  .then_inc(ct_loaded.sem, 16)

            def one_round(r, more):
                tok = bass.ds(r * TOK, TOK)
                proj[0].sp_k(sp, r)
                if more:
                    load_x(r + 1)
                if full:
                    proj[1].sp_k(sp, r)
                if more:
                    load_context(r + 1)
                sp.wait_ge(final.rows_ready.sem, final.rows_ready.at(r, 2))
                kit.gated(sp)
                sp.dma_start(out[2][tok, :].rearrange("(b t) f -> t b f", b=G), sh.residual[:]) \
                  .then_inc(stored.sem, 16)
                if full:
                    sp.wait_ge(final.lo_ready.sem, final.lo_ready.at(r, 2))
                    kit.gated(sp)
                    for part, dst in ((sh.yt.hi, out[0]), (sh.yt.lo, out[1])):
                        sp.dma_start(dst[:, tok].rearrange("(c p) t -> p c t", p=P), f32(part[:])) \
                          .then_inc(stored.sem, 16)

            load_x(0)
            load_context(0)
            with sp.Fori(0, ROUNDS - 1) as r:
                one_round(r, True)
            one_round(ROUNDS - 1, False)
            sp.wait_ge(stored.sem, stored.at(ROUNDS, 0))

        @block.scalar
        def _(act):
            for s in range(slots):
                act.wait_ge(stage_loaded[s].sem, 16)
                at = slice(s * STAGE_COLS, (s + 1) * STAGE_COLS)
                act.copy(weights.hi[:, at], stage[:, at]).then_inc(hi_made.sem, 1)
            act.wait_ge(biases.sem, 1)
            with act.Fori(0, ROUNDS) as r:
                proj[0].act_q(act, r, psum)
                att[0].act(act, r, psum)
                if full:
                    norm[0].act(act, r, psum, (norm[2].lo_ready, 0))
                    proj[1].act_q(act, r, psum)
                    att[1].act(act, r, psum)
                    norm[1].act(act, r, psum, (norm[0].lo_ready, 2))
                    ff.act(act, r, psum)
                    norm[2].act(act, r, psum, (norm[1].lo_ready, 2))

        @block.vector
        def _(dve):
            dve.memset(sh.minus_half[:], -0.5)
            dve.memset(sh.v[:], 0.0).then_inc(zeroed.sem, 1)
            dve.wait_ge(small_loaded.sem, 16 * (1 + len(names)))
            for i in range(len(proj)):
                dve.tensor_scalar(colv(f"q{i + 1}"), colv(f"q{i + 1}"), DK ** -0.5, None, ALU.mult)
            if full:
                dve.tensor_tensor(rowv("s1"), rowv("s1"), rowv("o2"), ALU.add)
                dve.tensor_tensor(rowv("s2"), rowv("s2"), rowv("ff"), ALU.add)
            dve.memset(sh.stats[:], 0.0).then_inc(biases.sem, 1)
            dve.wait_ge(biases.sem, 1)
            for s in range(slots):
                dve.wait_ge(hi_made.sem, s + 1)
                at = slice(s * STAGE_COLS, (s + 1) * STAGE_COLS)
                dve.tensor_tensor(weights.lo[:, at], stage[:, at], f32(weights.hi[:, at]),
                                  ALU.subtract).then_inc(lo_made.sem, 1)
            dve.wait_ge(lo_made.sem, slots)
            dve.memset(sh.k_block[:], 0.0).then_inc(zeroed.sem, 1)
            dve.wait_ge(zeroed.sem, 2)
            with dve.Fori(0, ROUNDS) as r:
                if full:
                    proj[0].dve_k(dve, r, psum, (proj[1], 0))
                else:
                    proj[0].dve_k(dve, r, psum, (proj[0], 0))
                proj[0].dve_v(dve, r, psum)
                att[0].dve(dve, r, psum)
                norm[0].dve_sum(dve, r, psum, (residual_ready, 1), (final.scaled, 0))
                if full:
                    proj[1].dve_k(dve, r, psum, (proj[0], 16 * HU))
                    proj[1].dve_v(dve, r, psum)
                    norm[0].dve_split(dve, r, (stored, 0))
                    att[1].dve(dve, r, psum)
                    norm[1].dve_sum(dve, r, psum, (norm[0].rows_ready, 2), None)
                    norm[1].dve_split(dve, r)
                    ff.dve(dve, r)
                    norm[2].dve_sum(dve, r, psum, (norm[1].rows_ready, 2), None)
                    norm[2].dve_split(dve, r)

        @block.gpsimd
        def _(pool):
            pool.memset(sh.eye[:], 1.0).then_inc(consts.sem, 1)
            pool.wait_ge(consts.sem, 1)
            pool.affine_select(out=sh.eye[:], in_=sh.eye[:], compare_op=ALU.is_equal, fill=0.0,
                               base=0, pattern=[[1, P]], channel_multiplier=-1).then_inc(consts.sem, 1)
            pool.wait_ge(consts.sem, 2)
            made = 2
            for m in mask:
                if m is not None:
                    pool.tensor_scalar(m.value_eye[:], sh.eye[:], m.value, None, ALU.mult) \
                        .then_inc(consts.sem, 1)
                    made += 1
                    if not m.per_batch:
                        m.pool(pool, 0)
            pool.wait_ge(consts.sem, made)
            pool.wait_ge(biases.sem, 1)
            with pool.Fori(0, ROUNDS) as r:
                for m, a in zip(mask, att):
                    if m is not None and m.per_batch:
                        m.pool(pool, r, a.scores_ready)
                pool.wait_ge(stored.sem, stored.at(r, 0))
                pool.wait_ge(rows_loaded.sem, rows_loaded.at(r, 16))
                pool.tensor_tensor(sh.residual[:], x_rows[:],
                                   rowv("o1").unsqueeze(1).broadcast_to([P, G, DM]), ALU.add) \
                    .then_inc(residual_ready.sem, 1)
                att[0].pool(pool, r)
                norm[0].pool(pool, r)
                if full:
                    att[1].pool(pool, r)
                    norm[1].pool(pool, r)
                    ff.pool(pool, r)
                    norm[2].pool(pool, r)
                tok = bass.ds(r * TOK, TOK)

        @block.tensor
        def _(pe):
            kit.start(pe)
            pe.wait_ge(lo_made.sem, slots)
            pe.wait_ge(zeroed.sem, 2)
            pe.wait_ge(consts.sem, 2 + sum(m is not None for m in mask))
            with pe.Fori(0, ROUNDS) as r:
                banks = Banks(psum)
                banks.read(0, norm[-2 if full else 0].sum_ready, 0)
                banks.read(1, norm[-2 if full else 0].sum_ready, 0)
                if full:
                    banks.read(2, final.turned_ready, 0)
                    banks.read(3, final.turned_ready, 0)
                    banks.read(4, ff.hidden_ready, 0)
                    banks.read(5, ff.hidden_ready, 0)
                    banks.read(6, final.sum_ready, 0)
                    banks.read(7, final.sum_ready, 0)
                else:
                    banks.read(2, att[0].exp_done, 0)
                    banks.read(3, att[0].exp_done, 0)
                    banks.read(4, att[0].turned_ready, 0)
                    banks.read(5, att[0].turned_ready, 0)
                    banks.read(6, att[0].normed, 0)
                    banks.read(7, att[0].normed, 0)
                pe.wait_ge(x_loaded.sem, x_loaded.at(r, 32))
                proj[0].pe_q(pe, r, banks, xt)
                if not full:
                    pe.wait_ge(ct_loaded.sem, ct_loaded.at(r, 32))
                kv = xt if full else ct
                proj[0].pe_k(pe, r, banks, kv)
                proj[0].pe_v(pe, r, banks, kv)
                att[0].pe(pe, r, banks)
                outp[0].pe(pe, r, banks, norm[0].sum_ready)
                if full:
                    pe.wait_ge(ct_loaded.sem, ct_loaded.at(r, 32))
                    proj[1].pe_k(pe, r, banks, ct)
                    proj[1].pe_v(pe, r, banks, ct)
                    norm[0].pe(pe, r, banks)
                    pe.wait_ge(norm[0].lo_ready.sem, norm[0].lo_ready.at(r, 2))
                    proj[1].pe_q(pe, r, banks, sh.yt)
                    att[1].pe(pe, r, banks)
                    outp[1].pe(pe, r, banks, norm[1].sum_ready)
                    norm[1].pe(pe, r, banks)
                    ff.pe(pe, r, banks, norm[1].lo_ready, norm[2].sum_ready)
                    norm[2].pe(pe, r, banks)



H8 = 8
OUT8_BANKS = (0, 1)
Q8_BANK, K8_BANK, V8_BANK, S8_BANK, TURN8_BANK, MIX8_BANK = 2, 3, 4, 5, 6, 7
DK8 = 128
MASKED = -1.5e38


class Attend8:

    def __init__(self, kit, name, w, sh):
        self.w, self.sh = w, sh
        self.q_in_psum = kit.counter(name + "_q_in_psum", H8)
        self.q_ready = kit.counter(name + "_q_ready", H8)
        self.k_in_psum = kit.counter(name + "_k_in_psum", H8)
        self.k_ready = kit.counter(name + "_k_ready", H8)
        self.v_in_psum = kit.counter(name + "_v_in_psum", H8)
        self.v_ready = kit.counter(name + "_v_ready", H8)
        self.scores_ready = kit.counter(name + "_scores_ready", H8)
        self.max_ready = kit.counter(name + "_max_ready", H8)
        self.exp_done = kit.counter(name + "_exp_done", H8)
        self.inverse_ready = kit.counter(name + "_inverse_ready", H8)
        self.p_ready = kit.counter(name + "_p_ready", H8)
        self.turned = kit.counter(name + "_turned", H8)
        self.turned_ready = kit.counter(name + "_turned_ready", H8)
        self.mixed = kit.counter(name + "_mixed", H8)
        self.hi_ready = kit.counter(name + "_hi_ready", H8)
        self.lo_ready = kit.counter(name + "_lo_ready", H8)
        self.out_ready = kit.counter(name + "_out_ready", 2)

    def pe_project(self, pe, r, banks, which, bank, src, h, done, reader):
        banks.claim(pe, r, bank)
        w = self.w[which]
        product(pe, banks.psum[:, bank, :],
                [(w.hi[:, k, h * P:(h + 1) * P], w.lo[:, k, h * P:(h + 1) * P]) for k in range(C)],
                [(src.hi[:, k, :], src.lo[:, k, :]) for k in range(C)],
                True, True).then_inc(done.sem, 1)
        banks.read(bank, reader, h + 1)

    def pe_v(self, pe, r, banks, src, i):
        banks.claim(pe, r, V8_BANK)
        w = self.w["v"]
        heads = slice((i // 2) * 2 * DK8, (i // 2 + 1) * 2 * DK8)
        for k in range(2):
            b = 2 * (i % 2) + k
            ins = product(pe, banks.psum[:, V8_BANK, k * DM:(k + 1) * DM],
                          [(src.hi[:, c, b * SEQ:(b + 1) * SEQ], src.lo[:, c, b * SEQ:(b + 1) * SEQ])
                           for c in range(C)],
                          [(w.hi[:, c, heads], w.lo[:, c, heads]) for c in range(C)], True, True)
        ins.then_inc(self.v_in_psum.sem, 1)
        banks.read(V8_BANK, self.v_ready, i + 1)

    def pe_scores(self, pe, r, banks, h):
        sh = self.sh
        banks.claim(pe, r, S8_BANK)
        out = banks.psum[:, S8_BANK, :]
        pe.matmul(out, sh.masked_eye[:], sh.flags[:].rearrange("p b k -> p (b k)"),
                  start=True, stop=False, skip_group_check=True)
        pe.wait_ge(self.q_ready.sem, self.q_ready.at(r, h + 1))
        pe.wait_ge(self.k_ready.sem, self.k_ready.at(r, h + 1))
        for b in range(G):
            at = slice(b * SEQ, (b + 1) * SEQ)
            ins = pe.matmul(out[:, at], sh.q[:, h % 2, at], sh.k[:, h % 2, at],
                            start=False, stop=b == G - 1, skip_group_check=True)
        ins.then_inc(self.scores_ready.sem, 1)
        banks.read(S8_BANK, self.exp_done, h + 1)

    def pe_turn(self, pe, r, banks, h):
        banks.claim(pe, r, TURN8_BANK)
        pe.wait_ge(self.p_ready.sem, self.p_ready.at(r, h + 1))
        for b in range(G):
            ins = pe.transpose(banks.psum[:, TURN8_BANK, b * SEQ:(b + 1) * SEQ],
                               self.sh.p[:, h % 2, b, :], self.sh.eye[:])
        ins.then_inc(self.turned.sem, 1)
        banks.read(TURN8_BANK, self.turned_ready, h + 1)

    def pe_mix(self, pe, r, banks, h):
        banks.claim(pe, r, MIX8_BANK)
        if h % 2 == 0:
            pe.wait_ge(self.v_ready.sem, self.v_ready.at(r, h + 2))
        pe.wait_ge(self.turned_ready.sem, self.turned_ready.at(r, h + 1))
        for b in range(G):
            ins = pe.matmul(banks.psum[:, MIX8_BANK, b * SEQ:(b + 1) * SEQ],
                            self.sh.v[:, (h // 2) % 2, b, (h % 2) * DK8:(h % 2 + 1) * DK8],
                            self.sh.p_turned[:, h % 2, b, :], start=True, stop=True)
        ins.then_inc(self.mixed.sem, 1)
        banks.read(MIX8_BANK, self.lo_ready, h + 1)

    def pe_out(self, pe, r, banks, h, reader):
        at, w = self.sh.attended, self.w["o"]
        if h == 0:
            banks.claim(pe, r, *OUT8_BANKS)
        pe.wait_ge(self.lo_ready.sem, self.lo_ready.at(r, h + 1))
        for b in range(G):
            cols = slice(b * SEQ, (b + 1) * SEQ)
            ins = product(pe, banks.psum[:, OUT8_BANKS[b // 2], (b % 2) * DM:(b % 2 + 1) * DM],
                          [(at.hi[:, h % 2, cols], at.lo[:, h % 2, cols])],
                          [(w.hi[:, h, :], w.lo[:, h, :])],
                          h == 0 and b % 2 == 0, h == H8 - 1 and b % 2 == 1, skip=True)
            if h == H8 - 1 and b % 2:
                ins.then_inc(self.out_ready.sem, 1)
                banks.read(OUT8_BANKS[b // 2], reader, b // 2 + 1)

    def pe(self, pe, r, banks, q_src, kv_src, reader):
        for j in range(H8 + 2):
            if j < H8:
                self.pe_v(pe, r, banks, kv_src, j)
                self.pe_project(pe, r, banks, "q", Q8_BANK, q_src, j, self.q_in_psum, self.q_ready)
                self.pe_project(pe, r, banks, "k", K8_BANK, kv_src, j, self.k_in_psum, self.k_ready)
            if 1 <= j <= H8:
                self.pe_turn(pe, r, banks, j - 1)
            if j >= 2:
                self.pe_out(pe, r, banks, j - 2, reader)
            if 1 <= j <= H8:
                self.pe_mix(pe, r, banks, j - 1)
            if j < H8:
                self.pe_scores(pe, r, banks, j)

    def act(self, act, r, psum):
        sh = self.sh
        for j in range(H8 + 1):
            if j < H8:
                act.wait_ge(self.q_in_psum.sem, self.q_in_psum.at(r, j + 1))
                act.activation(sh.q[:, j % 2, :], psum[:, Q8_BANK, :], ACT.Identity,
                               bias=self.w["q_bias"][:, j:j + 1], scale=DK8 ** -0.5) \
                   .then_inc(self.q_ready.sem, 1)
            if j >= 1:
                h = j - 1
                act.wait_ge(self.turned.sem, self.turned.at(r, h + 1))
                act.copy(sh.p_turned[:, h % 2, :, :],
                         psum[:, TURN8_BANK, :].rearrange("p (b q) -> p b q", b=G)) \
                   .then_inc(self.turned_ready.sem, 1)
                act.wait_ge(self.mixed.sem, self.mixed.at(r, h + 1))
                act.copy(sh.attended.hi[:, h % 2, :], psum[:, MIX8_BANK, :]) \
                   .then_inc(self.hi_ready.sem, 1)
            if j < H8:
                act.wait_ge(self.max_ready.sem, self.max_ready.at(r, j + 1))
                for b in range(G):
                    ins = act.activation(sh.p[:, j % 2, b, :], psum[:, S8_BANK, b * SEQ:(b + 1) * SEQ],
                                         ACT.Exp, bias=sh.neg_max[:, j % 2, b:b + 1],
                                         accum_out=sh.sums[:, j % 2, b:b + 1])
                ins.then_inc(self.exp_done.sem, 1)

    def dve(self, dve, r, psum):
        sh = self.sh
        for j in range(H8 + 1):
            if j < H8:
                dve.wait_ge(self.v_in_psum.sem, self.v_in_psum.at(r, j + 1))
                heads = slice((j // 2) * 2 * DK8, (j // 2 + 1) * 2 * DK8)
                two = 2 * (j % 2)
                dve.tensor_tensor(sh.v[:, (j // 2) % 2, two:two + 2, :],
                                  psum[:, V8_BANK, :].rearrange("p (b f) -> p b f", b=2),
                                  self.w["v_row"][:, heads].unsqueeze(1).broadcast_to([P, 2, DM]),
                                  ALU.add).then_inc(self.v_ready.sem, 1)
                dve.wait_ge(self.k_in_psum.sem, self.k_in_psum.at(r, j + 1))
                dve.tensor_scalar(sh.k[:, j % 2, :], psum[:, K8_BANK, :],
                                  self.w["k_bias"][:, j:j + 1], None, ALU.add) \
                   .then_inc(self.k_ready.sem, 1)
            if j >= 1:
                h = j - 1
                dve.wait_ge(self.hi_ready.sem, self.hi_ready.at(r, h + 1))
                dve.tensor_tensor(sh.attended.lo[:, h % 2, :], psum[:, MIX8_BANK, :],
                                  f32(sh.attended.hi[:, h % 2, :]), ALU.subtract) \
                   .then_inc(self.lo_ready.sem, 1)
            if j < H8:
                dve.wait_ge(self.scores_ready.sem, self.scores_ready.at(r, j + 1))
                dve.tensor_reduce(sh.neg_max[:, j % 2, :],
                                  psum[:, S8_BANK, :].rearrange("p (b k) -> p b k", b=G),
                                  AX_X, ALU.max, negate=True).then_inc(self.max_ready.sem, 1)
                dve.wait_ge(self.exp_done.sem, self.exp_done.at(r, j + 1))
                dve.reciprocal(sh.inverse[:, j % 2, :], sh.sums[:, j % 2, :]) \
                   .then_inc(self.inverse_ready.sem, 1)
                dve.wait_ge(self.inverse_ready.sem, self.inverse_ready.at(r, j + 1))
                dve.tensor_tensor(sh.p[:, j % 2, :, :], sh.p[:, j % 2, :, :],
                                  sh.inverse[:, j % 2, :].unsqueeze(2).broadcast_to([P, G, SEQ]),
                                  ALU.mult).then_inc(self.p_ready.sem, 1)


class Shared8:

    def __init__(self, kit, feed_forward):
        sb = kit.sb
        arena = sb("arena", [P, 4096], F32)
        self.stage = arena
        self.v = arena[:, 0:2048].rearrange("p (s b f) -> p s b f", s=2, b=G)
        self.p = arena[:, 2048:3072].rearrange("p (s b k) -> p s b k", s=2, b=G)
        self.z = arena[:, 3072:4096].rearrange("p (b f) -> p b f", b=G)
        self.q = sb("q", [P, 2, TOK], F32)
        self.k = sb("k", [P, 2, TOK], F32)
        self.p_turned = sb("p_turned", [P, 2, G, SEQ], F32)
        self.neg_max = sb("neg_max", [P, 2, G], F32)
        self.sums = sb("sums", [P, 2, G], F32)
        self.inverse = sb("inverse", [P, 2, G], F32)
        self.attended = Split(kit, "attended", [P, 2, TOK])
        self.residual = sb("residual", [P, G, DM], F32)
        self.stats = sb("stats", [P, G, 6], F32)
        self.moments = sb("moments", [P, G, 2], F32)
        self.variance = sb("variance", [P, G], F32)
        self.rstd = sb("rstd", [P, G], F32)
        self.minus_half = sb("minus_half", [P, 4], F32)
        self.y = sb("y", [P, 2, C, 2 * SEQ], F32)
        self.eye = sb("eye", [P, P], F32)
        self.masked_eye = sb("masked_eye", [P, P], BF16)
        self.flags = sb("flags", [P, G, SEQ], BF16)
        self.yt = Split(kit, "yt", [P, C, TOK])
        if feed_forward:
            self.relu = self.p_turned[:].rearrange("p s b q -> p s (b q)")
            self.hidden = Split(kit, "hidden", [P, HIDDEN_SLOTS, TOK])


COLS8 = dict(q_inner=0, k_inner=2, v_inner=4, q=6, k=14, g1=22, s1=24, ff=26)
ROWS8_SELF, ROWS8_CROSS = ["o1"], ["o1", "g1", "s1", "ff"]


def phase8(nc, tag, cross, x, ctx_t, pad, packed, cols, v_row_dram, rows, out, ctx_out):
    with ExitStack() as ctx:
        kit = Kit(nc, ctx, tag)
        sh = Shared8(kit, cross)
        psum = ctx.enter_context(nc.psum_tensor(f"{tag}_psum", [P, 8, 512], F32))
        col = kit.sb("cols", list(cols.shape), F32)
        names = ROWS8_CROSS if cross else ROWS8_SELF
        row = kit.sb("rows", [P, len(names), DM], F32)
        v_row = kit.sb("v_row", [P, H8 * DK8], F32)
        n_big = (packed.shape[1] - 3 * 512) // STAGE_COLS
        weights = Split(kit, "w", [P, n_big * STAGE_COLS])
        inner = sh.p_turned[:].rearrange("p s b q -> p s (b q)")
        stage = sh.stage
        xt = Split(kit, "xt", [P, C, TOK])
        ct = Split(kit, "ct", [P, C, TOK])
        x_rows = kit.sb("x_rows", [P, G, DM], F32)
        pad_ints = kit.sb("pad_ints", [P, G, SEQ], I32)
        fold = ["q", "k", "v"]

        def take(i, inner_width):
            return View(weights, lambda t: t[:, i * STAGE_COLS:(i + 1) * STAGE_COLS].rearrange(
                "p (c n) -> p c n", n=inner_width))

        def rowv(name):
            return row[:, names.index(name), :]

        def colv(name, n):
            return col[:, COLS8[name]:COLS8[name] + n]

        w = {"q": take(0, H8 * DK8), "k": take(1, H8 * DK8), "v": take(2, H8 * DK8), "o": take(3, DM),
             "q_bias": colv("q", H8), "k_bias": colv("k", H8), "v_row": v_row}

        small_loaded = kit.counter("small_loaded", 0)
        stage_loaded = [kit.counter(f"stage_loaded{i}", 0) for i in range(n_big)]
        fold_in_psum = kit.counter("fold_in_psum", 0)
        folded = kit.counter("folded", 0)
        hi_made = kit.counter("w_hi_made", 0)
        lo_made = kit.counter("w_lo_made", 0)
        biases = kit.counter("biases", 0)
        consts = kit.counter("consts", 0)
        consts_pool = kit.counter("consts_pool", 0)

        x_loaded = kit.counter("x_loaded", 32)
        ct_loaded = kit.counter("ct_loaded", 32)
        rows_loaded = kit.counter("rows_loaded", 16)
        pad_loaded = kit.counter("pad_loaded", 16)
        pad_flags = kit.counter("pad_flags", 1)
        flags_ready = kit.counter("flags_ready", 1)
        all_masked = kit.counter("all_masked", 1)
        poison_made = kit.counter("poison_made", 3)
        residual_sum = kit.counter("residual_sum", 1)
        residual_ready = kit.counter("residual_ready", 1)
        stored = kit.counter("stored", 48 if cross else 32)
        masked = kit.sb("masked", [P, G], F32)
        poison = kit.sb("poison", [P, 3, G], F32)
        if not cross:
            x_raw = kit.sb("x_raw", [P, C, TOK], F32)
            ct_raw = kit.sb("ct_raw", [P, C, TOK], F32)
            causal = kit.sb("causal", [P, SEQ], BF16)
            x_raw_loaded = kit.counter("x_raw_loaded", 16)
            ct_raw_loaded = kit.counter("ct_raw_loaded", 16)
            x_hi = kit.counter("x_hi", 1)
            x_lo = kit.counter("x_lo", 1)
            ct_hi = kit.counter("ct_hi", 1)
            ct_lo = kit.counter("ct_lo", 1)
            ct_stored = kit.counter("ct_stored", 32)

        att = Attend8(kit, "a", w, sh)
        norm = [Norm(kit, "n1", att.out_ready, OUT8_BANKS, colv("g1", 2), colv("s1", 2),
                     rowv("g1") if cross else None, rowv("s1") if cross else None, sh)]
        if cross:
            s1_final = kit.sb("s1_final", [P, DM], F32)
            ff = FeedForward(kit, "ff", take(4, DFF), take(5, DM), colv("ff", M), sh)
            norm.append(Norm(kit, "n2", ff.out_ready, FF_OUT_BANKS, colv("g1", 2), colv("s1", 2),
                             rowv("g1"), s1_final[:], sh))
        final = norm[-1]
        block = ctx.enter_context(nc.Block())

        @block.sync
        def _(sp):
            sp.dma_start(col[:], cols).then_inc(small_loaded.sem, 16)
            sp.dma_start(v_row[:], v_row_dram.broadcast_to([P, H8 * DK8])).then_inc(small_loaded.sem, 16)
            for i in range(len(names)):
                sp.dma_start(row[:, i, :], rows[i:i + 1, :].broadcast_to([P, DM])) \
                  .then_inc(small_loaded.sem, 16)
            for i in range(n_big):
                if 2 <= i < 5:
                    sp.wait_ge(folded.sem, i - 1)
                elif i >= 5:
                    sp.wait_ge(lo_made.sem, 4 * 3 + i - 4)
                at = 3 * 512 + i * STAGE_COLS
                half = slice((i % 2) * STAGE_COLS, (i % 2 + 1) * STAGE_COLS)
                sp.dma_start(stage[:, half], packed[:, at:at + STAGE_COLS]) \
                  .then_inc(stage_loaded[i].sem, 16)
                if i < 3:
                    sp.dma_start(inner[:, i % 2, :], packed[:, i * 512:(i + 1) * 512]) \
                      .then_inc(stage_loaded[i].sem, 16)

            def load_round(r):
                tok = bass.ds(r * TOK, TOK)
                if cross:
                    sp.wait_ge(att.k_in_psum.sem, att.k_in_psum.at(r, 0))
                    kit.gated(sp)
                    for tile, src, signal in ((xt.hi, x[0], x_loaded), (xt.lo, x[1], x_loaded),
                                              (ct.hi, ctx_t[0], ct_loaded), (ct.lo, ctx_t[1], ct_loaded)):
                        sp.dma_start(f32(tile[:]), src[:, tok].rearrange("(c p) t -> p c t", p=P)) \
                          .then_inc(signal.sem, 16)
                else:
                    sp.wait_ge(x_lo.sem, x_lo.at(r, 0))
                    kit.gated(sp)
                    sp.dma_start(x_raw[:], x[0][:, tok].rearrange("(c p) t -> p c t", p=P)) \
                      .then_inc(x_raw_loaded.sem, 16)
                    sp.wait_ge(ct_lo.sem, ct_lo.at(r, 0))
                    kit.gated(sp)
                    sp.dma_start(ct_raw[:], ctx_t[:, tok].rearrange("(c p) t -> p c t", p=P)) \
                      .then_inc(ct_raw_loaded.sem, 16)
                sp.wait_ge(pad_flags.sem, pad_flags.at(r, 0))
                kit.gated(sp)
                sp.dma_start(pad_ints[:], pad[bass.ds(r * G, G)].rearrange("b o k -> o b k")
                             .broadcast_to([P, G, SEQ])).then_inc(pad_loaded.sem, 16)
                sp.wait_ge(residual_sum.sem, residual_sum.at(r, 0))
                kit.gated(sp)
                sp.dma_start(x_rows[:], x[-1][tok, :].rearrange("(b t) f -> t b f", b=G)) \
                  .then_inc(rows_loaded.sem, 16)

            def store_round(r):
                tok = bass.ds(r * TOK, TOK)
                if not cross:
                    sp.wait_ge(ct_lo.sem, ct_lo.at(r, 1))
                    kit.gated(sp)
                    for part, dst in ((ct.hi, ctx_out[0]), (ct.lo, ctx_out[1])):
                        sp.dma_start(dst[:, tok].rearrange("(c p) t -> p c t", p=P), f32(part[:])) \
                          .then_inc(ct_stored.sem, 16)
                else:
                    sp.wait_ge(final.rows_ready.sem, final.rows_ready.at(r, 2))
                    kit.gated(sp)
                    sp.dma_start(out[2][tok, :].rearrange("(b t) f -> t b f", b=G), sh.residual[:]) \
                      .then_inc(stored.sem, 16)
                sp.wait_ge(final.lo_ready.sem, final.lo_ready.at(r, 2))
                kit.gated(sp)
                for part, dst in ((sh.yt.hi, out[0]), (sh.yt.lo, out[1])):
                    sp.dma_start(dst[:, tok].rearrange("(c p) t -> p c t", p=P), f32(part[:])) \
                      .then_inc(stored.sem, 16)

            load_round(0)
            with sp.Fori(0, ROUNDS - 1) as r:
                load_round(r + 1)
                store_round(r)
            store_round(ROUNDS - 1)
            sp.wait_ge(stored.sem, stored.at(ROUNDS, 0))
            if not cross:
                sp.wait_ge(ct_stored.sem, ct_stored.at(ROUNDS, 0))

        @block.scalar
        def _(act):
            for i in range(n_big):
                at = i * STAGE_COLS
                if i < 3:
                    for o in range(4):
                        act.wait_ge(fold_in_psum.sem, 4 * i + o + 1)
                        act.copy(weights.hi[:, at + o * 512:at + (o + 1) * 512], psum[:, o, :]) \
                           .then_inc(hi_made.sem, 1)
                else:
                    act.wait_ge(stage_loaded[i].sem, 16)
                    half = slice((i % 2) * STAGE_COLS, (i % 2 + 1) * STAGE_COLS)
                    act.copy(weights.hi[:, at:at + STAGE_COLS], stage[:, half]).then_inc(hi_made.sem, 1)
            act.wait_ge(biases.sem, 1)
            with act.Fori(0, ROUNDS) as r:
                if not cross:
                    act.wait_ge(x_raw_loaded.sem, x_raw_loaded.at(r, 16))
                    act.wait_ge(att.k_in_psum.sem, att.k_in_psum.at(r, 0))
                    act.copy(xt.hi[:], x_raw[:]).then_inc(x_hi.sem, 1)
                    act.wait_ge(ct_raw_loaded.sem, ct_raw_loaded.at(r, 16))
                    act.wait_ge(ct_stored.sem, ct_stored.at(r, 0))
                    act.copy(ct.hi[:], ct_raw[:]).then_inc(ct_hi.sem, 1)
                att.act(act, r, psum)
                norm[0].act(act, r, psum, (final.lo_ready, 0))
                if cross:
                    ff.act(act, r, psum)
                    norm[1].act(act, r, psum, (norm[0].lo_ready, 2))

        @block.vector
        def _(dve):
            dve.memset(sh.minus_half[:], -0.5)
            for i in range(n_big):
                at = i * STAGE_COLS
                if i < 3:
                    for o in range(4):
                        q = slice(at + o * 512, at + (o + 1) * 512)
                        dve.wait_ge(hi_made.sem, 4 * i + o + 1)
                        dve.tensor_tensor(weights.lo[:, q], psum[:, o, :], f32(weights.hi[:, q]),
                                          ALU.subtract).then_inc(lo_made.sem, 1)
                else:
                    half = slice((i % 2) * STAGE_COLS, (i % 2 + 1) * STAGE_COLS)
                    q = slice(at, at + STAGE_COLS)
                    dve.wait_ge(hi_made.sem, 12 + i - 2)
                    dve.tensor_tensor(weights.lo[:, q], stage[:, half], f32(weights.hi[:, q]),
                                      ALU.subtract).then_inc(lo_made.sem, 1)
            dve.wait_ge(folded.sem, 3)
            dve.wait_ge(small_loaded.sem, 16 * (2 + len(names)))
            dve.tensor_tensor(colv("q", H8), colv("q", H8), psum[:, 4, 0:H8], ALU.add) \
               .then_inc(consts.sem, 1)
            dve.tensor_tensor(colv("k", H8), colv("k", H8), psum[:, 5, 0:H8], ALU.add)
            dve.tensor_tensor(v_row[:], v_row[:], psum[:, 6:8, :].rearrange("p a n -> p (a n)"), ALU.add)
            if cross:
                dve.tensor_copy(s1_final[:], rowv("s1")).then_inc(consts.sem, 1)
            dve.wait_ge(consts.sem, 2 if cross else 1)
            dve.tensor_scalar(colv("q", H8), colv("q", H8), DK8 ** -0.5, None, ALU.mult)
            if cross:
                dve.tensor_tensor(rowv("s1"), rowv("s1"), rowv("ff"), ALU.add)
            dve.memset(sh.stats[:], 0.0).then_inc(biases.sem, 1)
            with dve.Fori(0, ROUNDS) as r:
                dve.wait_ge(flags_ready.sem, flags_ready.at(r, 1))
                dve.wait_ge(poison_made.sem, poison_made.at(r, 0))
                dve.tensor_reduce(masked[:], sh.flags[:], AX_X, ALU.min).then_inc(all_masked.sem, 1)
                att.dve(dve, r, psum)
                norm[0].dve_sum(dve, r, psum, (residual_ready, 1),
                                (final.scaled, 0) if cross else (final.hat_turned, 0))
                norm[0].dve_split(dve, r, (stored, 0))
                if cross:
                    ff.dve(dve, r)
                    norm[1].dve_sum(dve, r, psum, (norm[0].rows_ready, 2), None)
                    norm[1].dve_split(dve, r)

        @block.gpsimd
        def _(pool):
            pool.memset(sh.eye[:], 1.0).then_inc(consts_pool.sem, 1)
            pool.wait_ge(consts_pool.sem, 1)
            pool.affine_select(out=sh.eye[:], in_=sh.eye[:], compare_op=ALU.is_equal, fill=0.0,
                               base=0, pattern=[[1, P]], channel_multiplier=-1).then_inc(consts_pool.sem, 1)
            pool.wait_ge(consts_pool.sem, 2)
            pool.tensor_scalar(sh.masked_eye[:], sh.eye[:], MASKED, None, ALU.mult) \
                .then_inc(consts_pool.sem, 1)
            made = 3
            if not cross:
                pool.memset(causal[:], 1.0).then_inc(consts_pool.sem, 1)
                pool.wait_ge(consts_pool.sem, 4)
                pool.affine_select(out=causal[:], in_=causal[:], compare_op=ALU.is_gt, fill=0.0,
                                   base=0, pattern=[[1, SEQ]], channel_multiplier=-1) \
                    .then_inc(consts_pool.sem, 1)
                made = 5
            pool.wait_ge(consts_pool.sem, made)
            pool.wait_ge(biases.sem, 1)
            with pool.Fori(0, ROUNDS) as r:
                tok = bass.ds(r * TOK, TOK)
                if not cross:
                    pool.wait_ge(x_hi.sem, x_hi.at(r, 1))
                    pool.tensor_tensor(xt.lo[:], x_raw[:], f32(xt.hi[:]), ALU.subtract) \
                        .then_inc(x_lo.sem, 1)
                pool.wait_ge(pad_loaded.sem, pad_loaded.at(r, 16))
                pool.wait_ge(att.scores_ready.sem, att.scores_ready.at(r, 0))
                pool.wait_ge(all_masked.sem, all_masked.at(r, 0))
                pool.sem_inc(kit.gate.sem, 1)
                pool.tensor_scalar(sh.flags[:], pad_ints[:], 0.0, None, ALU.is_equal) \
                    .then_inc(pad_flags.sem, 1)
                pool.wait_ge(pad_flags.sem, pad_flags.at(r, 1))
                if not cross:
                    pool.tensor_tensor(sh.flags[:], sh.flags[:],
                                       causal[:].unsqueeze(1).broadcast_to([P, G, SEQ]), ALU.add) \
                        .then_inc(flags_ready.sem, 1)
                else:
                    pool.sem_inc(kit.gate.sem, 1)
                    pool.tensor_scalar(sh.flags[:], sh.flags[:], 1.0, None, ALU.mult) \
                        .then_inc(flags_ready.sem, 1)
                pool.wait_ge(all_masked.sem, all_masked.at(r, 1))
                pool.sem_inc(kit.gate.sem, 1)
                pool.tensor_scalar(poison[:, 0, :], masked[:], 3e38, None, ALU.mult) \
                    .then_inc(poison_made.sem, 1)
                pool.wait_ge(poison_made.sem, poison_made.at(r, 1))
                pool.sem_inc(kit.gate.sem, 1)
                pool.tensor_scalar(poison[:, 1, :], poison[:, 0, :], 10.0, None, ALU.mult) \
                    .then_inc(poison_made.sem, 1)
                pool.wait_ge(poison_made.sem, poison_made.at(r, 2))
                pool.sem_inc(kit.gate.sem, 1)
                pool.tensor_scalar(poison[:, 2, :], poison[:, 1, :], 0.0, None, ALU.mult) \
                    .then_inc(poison_made.sem, 1)
                pool.wait_ge(rows_loaded.sem, rows_loaded.at(r, 16))
                pool.wait_ge(stored.sem, stored.at(r, 0))
                if not cross:
                    pool.wait_ge(final.sum_ready.sem, final.sum_ready.at(r, 0))
                pool.tensor_tensor(sh.residual[:], x_rows[:],
                                   rowv("o1").unsqueeze(1).broadcast_to([P, G, DM]), ALU.add) \
                    .then_inc(residual_sum.sem, 1)
                pool.wait_ge(residual_sum.sem, residual_sum.at(r, 1))
                pool.wait_ge(poison_made.sem, poison_made.at(r, 3))
                pool.tensor_tensor(sh.residual[:], sh.residual[:],
                                   poison[:, 2, :].unsqueeze(2).broadcast_to([P, G, DM]), ALU.add) \
                    .then_inc(residual_ready.sem, 1)
                if not cross:
                    pool.wait_ge(ct_hi.sem, ct_hi.at(r, 1))
                    pool.tensor_tensor(ct.lo[:], ct_raw[:], f32(ct.hi[:]), ALU.subtract) \
                        .then_inc(ct_lo.sem, 1)
                norm[0].pool(pool, r)
                if cross:
                    ff.pool(pool, r)
                    norm[1].pool(pool, r)

        @block.tensor
        def _(pe):
            kit.start(pe)
            pe.wait_ge(small_loaded.sem, 16 * (2 + len(names)))
            for i, name in enumerate(fold):
                pe.wait_ge(stage_loaded[i].sem, 32)
                outer = stage[:, (i % 2) * STAGE_COLS:(i % 2 + 1) * STAGE_COLS].rearrange(
                    "p (c n) -> p c n", c=C)
                small = inner[:, i % 2, :].rearrange("p (c n) -> p c n", c=C)
                for o in range(4):
                    if i > 0:
                        pe.wait_ge(lo_made.sem, 4 * (i - 1) + o + 1)
                    chunk, half = o // 2, o % 2
                    for k in range(C):
                        ins = pe.matmul(psum[:, o, :], small[:, k, chunk * P:(chunk + 1) * P],
                                        outer[:, k, half * 512:(half + 1) * 512],
                                        start=k == 0, stop=k == C - 1)
                    ins.then_inc(fold_in_psum.sem, 1)
                bias = colv(name + "_inner", C)
                if name == "v":
                    for half in range(2):
                        for k in range(C):
                            ins = pe.matmul(psum[:, 6 + half, :], bias[:, k:k + 1].broadcast_to([P, P]),
                                            outer[:, k, half * 512:(half + 1) * 512],
                                            start=k == 0, stop=k == C - 1)
                else:
                    for h in range(H8):
                        for k in range(C):
                            ins = pe.matmul(psum[:, 4 + i, h:h + 1], outer[:, k, h * P:(h + 1) * P],
                                            bias[:, k:k + 1], start=k == 0, stop=k == C - 1)
                ins.then_inc(folded.sem, 1)
            pe.wait_ge(lo_made.sem, 12 + n_big - 3)
            pe.wait_ge(biases.sem, 1)
            pe.wait_ge(consts_pool.sem, 3)
            with pe.Fori(0, ROUNDS) as r:
                banks = Banks(psum)
                for bank in OUT8_BANKS:
                    banks.read(bank, norm[0].sum_ready, 0)
                for bank in NORM_BANKS:
                    banks.read(bank, final.turned_ready, 0)
                if cross:
                    for bank in HIDDEN_BANKS[0:2]:
                        banks.read(bank, ff.hidden_ready, 0)
                    for bank in FF_OUT_BANKS:
                        banks.read(bank, final.sum_ready, 0)
                    pe.wait_ge(x_loaded.sem, x_loaded.at(r, 32))
                    pe.wait_ge(ct_loaded.sem, ct_loaded.at(r, 32))
                    q_src, kv_src = xt, ct
                else:
                    banks.read(V8_BANK, att.v_ready, 0)
                    banks.read(S8_BANK, att.exp_done, 0)
                    banks.read(TURN8_BANK, att.turned_ready, 0)
                    banks.read(MIX8_BANK, att.lo_ready, 0)
                    pe.wait_ge(x_lo.sem, x_lo.at(r, 1))
                    q_src, kv_src = xt, xt
                pe.wait_ge(flags_ready.sem, flags_ready.at(r, 1))
                att.pe(pe, r, banks, q_src, kv_src, norm[0].sum_ready)
                norm[0].pe(pe, r, banks)
                if cross:
                    ff.pe(pe, r, banks, norm[0].lo_ready, norm[1].sum_ready)
                    norm[1].pe(pe, r, banks)


def four_layers(nc, t, out):
    def scratch(name, shape):
        return nc.dram_tensor(name, shape, F32, kind="Internal").ap()

    tokens = BATCH * SEQ
    ctx_split = (scratch("context_hi", (DM, tokens)), scratch("context_lo", (DM, tokens)))
    between = [(scratch(f"x{i}_hi", (DM, tokens)), scratch(f"x{i}_lo", (DM, tokens)),
                scratch(f"x{i}_rows", (tokens, DM))) for i in range(4)]
    phase8(nc, "self8", False, (t["x_t"], t["x_rows"]), t["ctx_t"], t["pad"], t["l0a_packed"],
           t["l0a_cols"], t["l0a_v_row"], t["l0a_rows"], between[0], ctx_split)
    phase8(nc, "cross8", True, (between[0][0], between[0][1], t["x_rows"]), ctx_split, t["pad"],
           t["l0b_packed"], t["l0b_cols"], t["l0b_v_row"], t["l0b_rows"], between[1], None)
    phase16(nc, "second", True, between[1], ctx_split,
            [(t["mask_self"], False, -1e20, True), (t["mask_cross"], False, -1e20, True)],
            t["l1_packed"], t["l1_cols"], t["l1_rows"], between[2])
    phase16(nc, "third", True, between[2], ctx_split,
            [(t["mask_all"].unsqueeze(1), True, -3.3895e38, False), None],
            t["l2_packed"], t["l2_cols"], t["l2_rows"], between[3])
    phase16(nc, "fourth", False, between[3], ctx_split, [None],
            t["l3_packed"], t["l3_cols"], t["l3_rows"], (None, None, out))




def kernel(**inputs):
    import concourse.bacc as _bacc
    from concourse.bass_utils import run_bass_kernel_spmd as _run

    a = {k: np.asarray(v) for k, v in inputs.items()}

    def chunked(w):
        return w.reshape(-1, P, w.shape[1]).transpose(1, 0, 2).reshape(P, -1)

    def column(v):
        return v.reshape(-1, P).T

    def layer0(self_half):
        s, n = ("sa", "1") if self_half else ("ed", "2")
        L = "L0_xattn_"
        packed = [chunked(a[f"{L}{x}{n}_w"]) for x in "qkv"]
        packed += [chunked(a[f"{L}{s}_{x}w"].reshape(-1, DM).T) for x in "qkv"]
        packed += [chunked(a[f"{L}{s}_ow"].T)]
        cols = [column(a[f"{L}{x}{n}_b"]) for x in "qkv"]
        cols += [column(a[f"{L}{s}_qb"].reshape(-1)), column(a[f"{L}{s}_kb"].reshape(-1)),
                 column(a[f"{L}ln{n}_g"]), column(a[f"{L}ln{n}_b"])]
        rows = [a[f"{L}{s}_ob"]]
        if not self_half:
            packed += [chunked(a[L + "ff_w1"].T), chunked(a[L + "ff_w2"].T)]
            cols += [column(a[L + "ff_b1"])]
            rows += [a[L + "ln2_g"], a[L + "ln2_b"], a[L + "ff_b2"]]
        return (np.concatenate(packed, 1), np.concatenate(cols, 1),
                a[f"{L}{s}_vb"].reshape(1, -1), np.stack(rows))

    def full16(L, self_names, cross_names, biases, ff):
        g = lambda n: a[L + n]
        packed = [chunked(g(n)) for n in self_names + cross_names] + [chunked(g(ff[0])), chunked(g(ff[2]))]
        sb, cb = biases
        cols = [sb[0], sb[1], cb[0], cb[1], "ln1_g", "ln1_b", "ln2_g", "ln2_b", "ln3_g", "ln3_b", ff[1]]
        rows = [sb[2], cb[2], sb[3], "ln1_g", "ln1_b", "ln2_g", "ln2_b", "ln3_g", "ln3_b", cb[3], ff[3]]
        return (np.concatenate(packed, 1), np.concatenate([column(g(n)) for n in cols], 1),
                np.stack([g(n) for n in rows]))

    d = {}
    d["x_t"] = a["x"].reshape(-1, DM).T
    d["x_rows"] = a["x"].reshape(-1, DM)
    d["ctx_t"] = a["ctx_1024"].reshape(-1, DM).T
    d["pad"] = a["mask_Bx1xS2_if1"]
    d["mask_self"], d["mask_cross"] = a["mask_BxSxS2_ik0"], a["mask_BxSxS2_if1"]
    d["mask_all"] = a["mask_SxS_ik1"]
    d["l0a_packed"], d["l0a_cols"], d["l0a_v_row"], d["l0a_rows"] = layer0(True)
    d["l0b_packed"], d["l0b_cols"], d["l0b_v_row"], d["l0b_rows"] = layer0(False)
    d["l1_packed"], d["l1_cols"], d["l1_rows"] = full16(
        "L1_xattn_", ["sa_wq", "sa_wk", "sa_wv", "sa_wo"], ["ca_wq", "ca_wk", "ca_wv", "ca_wo"],
        (["sa_bq", "sa_bk", "sa_bv", "sa_bo"], ["ca_bq", "ca_bk", "ca_bv", "ca_bo"]),
        ["ff_w1", "ff_b1", "ff_w2", "ff_b2"])
    d["l2_packed"], d["l2_cols"], d["l2_rows"] = full16(
        "L2_xattn_", ["q_w", "k_w", "v_w", "o_w"], ["cq_w", "ck_w", "cv_w", "co_w"],
        (["q_b", "k_b", "v_b", "o_b"], ["cq_b", "ck_b", "cv_b", "co_b"]),
        ["lin1_w", "lin1_b", "lin2_w", "lin2_b"])
    L = "L3_xattn_"
    d["l3_packed"] = np.concatenate([chunked(a[L + n].T) for n in ("Wq", "Wk", "Wv", "Wo")], 1)
    d["l3_cols"] = np.concatenate([column(a[L + n]) for n in ("bq", "bk")], 1)
    d["l3_rows"] = np.stack([a[L + n] for n in ("bv", "bo", "gamma", "beta")])

    nc = _bacc.Bacc("TRN2", target_bir_lowering=False, num_devices=1)
    arrays, t = {}, {}
    for name, array in d.items():
        arrays[f"in_{name}"] = np.ascontiguousarray(array)
        t[name] = nc.dram_tensor(f"in_{name}", arrays[f"in_{name}"].shape,
                                 mybir.dt.from_np(array.dtype), kind="ExternalInput").ap()
    out = nc.dram_tensor("out_0", (BATCH * SEQ, DM), F32, kind="ExternalOutput").ap()
    four_layers(nc, t, out)
    r = _run(nc, [arrays], core_ids=[0])
    return r.results[0]["out_0"].reshape(BATCH, SEQ, DM)
```

```python
from contextlib import ExitStack

import numpy as np
import concourse.bass as bass
from concourse import mybir

F32 = mybir.dt.float32
F32R = mybir.dt.float32r
BF16 = mybir.dt.bfloat16
I32 = mybir.dt.int32
ALU = mybir.AluOpType
ACT = mybir.ActivationFunctionType
AX_X = mybir.AxisListType.X

P = 128
BATCH, SEQ, DM, DFF = 32, 128, 256, 1024
G = 4
ROUNDS = BATCH // G
TOK = G * SEQ
C = DM // P
M = DFF // P
EPS = 1e-5


class Signal:

    def __init__(self, nc, name, per_round):
        self.sem = nc.alloc_semaphore(name)
        self.per_round = per_round

    def at(self, r, n, ahead=0):
        return r * self.per_round + (n + 1 + ahead * self.per_round) if self.per_round else n


class Kit:

    def __init__(self, nc, ctx, tag):
        self.nc, self.ctx, self.tag = nc, ctx, tag
        self.round_signals = []
        ctx.callback(nc.all_engine_barrier)
        self.gate = Signal(nc, f"{tag}_gate", 0)
        self.all_sems = [self.gate.sem]
        ctx.callback(nc.clear_and_free_semaphores, self.all_sems)

    def sb(self, name, shape, dt):
        return self.ctx.enter_context(self.nc.sbuf_tensor(f"{self.tag}_{name}", shape, dt))

    def counter(self, name, per_round):
        signal = Signal(self.nc, f"{self.tag}_{name}", per_round)
        self.all_sems.append(signal.sem)
        if per_round:
            self.round_signals.append(signal)
        return signal

    def gated(self, engine):
        engine.sem_inc(self.gate.sem, 1)

    def start(self, pe):
        for signal in self.round_signals:
            pe.sem_inc(signal.sem, 1)


class Split:

    def __init__(self, kit, name, shape):
        self.hi = kit.sb(name + "_hi", shape, F32R)
        self.lo = kit.sb(name + "_lo", shape, F32R)


def f32(ap):
    return ap.bitcast(F32)


def product(pe, out, stationary, moving, first, last, skip=False):
    n = 0
    total = 3 * len(stationary)
    for (w_hi, w_lo), (x_hi, x_lo) in zip(stationary, moving):
        for w, x in ((w_lo, x_hi), (w_hi, x_lo), (w_hi, x_hi)):
            ins = pe.matmul(out, w, x, start=first and n == 0, stop=last and n == total - 1,
                            skip_group_check=skip)
            n += 1
    return ins


class Banks:

    def __init__(self, psum):
        self.psum = psum
        self.read_by = {}

    def claim(self, pe, r, *banks):
        need = {}
        for b in banks:
            for reader, n in self.read_by.get(b, []):
                need[reader] = max(n, need.get(reader, 0))
        for reader, n in need.items():
            pe.wait_ge(reader.sem, reader.at(r, n))

    def read(self, bank, reader, n, ahead=0):
        self.read_by[bank] = [(reader, n + ahead * reader.per_round)]

    def read_too(self, bank, reader, n):
        self.read_by[bank].append((reader, n))


PAIRS = G // 2
HALF = 2 * SEQ

SCORE_BANKS = (0, 1, 2)
OUT_BANK = 3
TURN_BANKS = (4, 5)
MIX_BANKS = (6, 7)
K_BANKS = (4, 5)
Q_PAIR_BANKS = (0, 3)
NORM_BANKS = (1, 2)
HIDDEN_BANKS = (4, 5, 0)
FF_OUT_BANKS = (6, 7)
HIDDEN_SLOTS, RELU_SLOTS = 3, 4

HEADS = 16
DK = DM // HEADS
HALVES = G * C * 2


class Project16:

    def __init__(self, kit, name, w, sh, q_banks, v_banks):
        self.w, self.sh, self.q_banks, self.v_banks = w, sh, q_banks, v_banks
        self.q_in_psum = kit.counter(name + "_q_in_psum", 2)
        self.q_ready = kit.counter(name + "_q_ready", 2)
        self.k_in_psum = kit.counter(name + "_k_in_psum", C)
        self.k_ready = kit.counter(name + "_k_ready", C)
        self.k_blocked = [kit.counter(f"{name}_k_blocked{c}", 16 * 8) for c in range(C)]
        self.v_in_psum = kit.counter(name + "_v_in_psum", 2)
        self.v_ready = kit.counter(name + "_v_ready", 2)

    def weight(self, which, c):
        w = self.w[which]
        return [(w.hi[:, k, c * P:(c + 1) * P], w.lo[:, k, c * P:(c + 1) * P]) for k in range(C)]

    def pe_q_chunk(self, pe, r, banks, src, c, ahead=0):
        banks.claim(pe, r, self.q_banks[c])
        product(pe, banks.psum[:, self.q_banks[c], :], self.weight("q", c),
                [(src.hi[:, k, :], src.lo[:, k, :]) for k in range(C)],
                True, True).then_inc(self.q_in_psum.sem, 1)
        banks.read(self.q_banks[c], self.q_ready, c + 1, ahead)

    def pe_q_pair(self, pe, r, banks, src, pair):
        bank = self.q_banks[pair]
        banks.claim(pe, r, bank)
        cols = slice(pair * HALF, (pair + 1) * HALF)
        for c in range(C):
            ins = product(pe, banks.psum[:, bank, c * HALF:(c + 1) * HALF], self.weight("q", c),
                          [(src.hi[:, k, cols], src.lo[:, k, cols]) for k in range(C)], True, True)
        ins.then_inc(self.q_in_psum.sem, 1)
        banks.read(bank, self.q_ready, pair + 1)

    def pe_k(self, pe, r, banks, src, c, ahead=0):
        banks.claim(pe, r, K_BANKS[c])
        product(pe, banks.psum[:, K_BANKS[c], :], self.weight("k", c),
                [(src.hi[:, k, :], src.lo[:, k, :]) for k in range(C)],
                True, True).then_inc(self.k_in_psum.sem, 1)
        banks.read(K_BANKS[c], self.k_ready, c + 1, ahead)

    def pe_v(self, pe, r, banks, src, ahead=0):
        for pair in range(PAIRS):
            bank = self.v_banks[pair]
            banks.claim(pe, r, bank)
            for b in (2 * pair, 2 * pair + 1):
                last = product(pe, banks.psum[:, bank, (b % 2) * DM:(b % 2 + 1) * DM],
                               [(src.hi[:, k, b * SEQ:(b + 1) * SEQ], src.lo[:, k, b * SEQ:(b + 1) * SEQ])
                                for k in range(C)],
                               [(self.w["v"].hi[:, k, :], self.w["v"].lo[:, k, :]) for k in range(C)],
                               True, True)
            last.then_inc(self.v_in_psum.sem, 1)
            banks.read(bank, self.v_ready, pair + 1, ahead)

    def act_q_chunk(self, act, r, psum, c, ahead=0):
        act.wait_ge(self.q_in_psum.sem, self.q_in_psum.at(r, c + 1, ahead))
        act.activation(self.sh.q[:, c, :], psum[:, self.q_banks[c], :], ACT.Identity,
                       bias=self.w["q_bias"][:, c:c + 1], scale=DK ** -0.5) \
           .then_inc(self.q_ready.sem, 1)

    def act_q_pair(self, act, r, psum, pair):
        act.wait_ge(self.q_in_psum.sem, self.q_in_psum.at(r, pair + 1))
        for c in range(C):
            ins = act.activation(self.sh.q[:, c, pair * HALF:(pair + 1) * HALF],
                                 psum[:, self.q_banks[pair], c * HALF:(c + 1) * HALF], ACT.Identity,
                                 bias=self.w["q_bias"][:, c:c + 1], scale=DK ** -0.5)
        ins.then_inc(self.q_ready.sem, 1)

    def dve_k(self, dve, r, psum, c, scattered_before, ahead=0):
        project, n = scattered_before
        dve.wait_ge(project.k_blocked[c].sem, project.k_blocked[c].at(r, n))
        dve.wait_ge(self.k_in_psum.sem, self.k_in_psum.at(r, c + 1, ahead))
        dve.tensor_scalar(self.sh.k[:, c, :], psum[:, K_BANKS[c], :],
                          self.w["k_bias"][:, c:c + 1], None, ALU.add) \
           .then_inc(self.k_ready.sem, 1)

    def sp_k(self, sp, r, ahead=0):
        for c in range(C):
            sp.wait_ge(self.k_ready.sem, self.k_ready.at(r, c + 1, ahead))
            for e in range(2):
                for j in range(4):
                    rows = slice(32 * j + DK * e, 32 * j + DK * (e + 1))
                    sp.dma_start(self.sh.k_block[rows, c, e, j, :], self.sh.k[rows, c, :]) \
                      .then_inc(self.k_blocked[c].sem, 16)

    def dve_v(self, dve, r, psum, ahead=0):
        for b in range(G):
            dve.wait_ge(self.v_in_psum.sem, self.v_in_psum.at(r, b // 2 + 1, ahead))
            ins = dve.tensor_tensor(
                self.sh.v_slots[b],
                psum[:, self.v_banks[b // 2], (b % 2) * DM:(b % 2 + 1) * DM].rearrange(
                    "p (g e d) -> p g e d", e=2, d=DK),
                self.w["v_row"].rearrange("p (g e d) -> p g e d", e=2, d=DK), ALU.add)
            if b % 2:
                ins.then_inc(self.v_ready.sem, 1)


class Attend16:

    def __init__(self, kit, name, proj, mask, w_out, sh, q_by_pair):
        self.proj, self.mask, self.w_out, self.sh, self.q_by_pair = proj, mask, w_out, sh, q_by_pair
        self.gate = kit.gate
        self.scores_ready = kit.counter(name + "_scores_ready", HALVES)
        self.max_ready = kit.counter(name + "_max_ready", HALVES)
        self.exp_done = kit.counter(name + "_exp_done", HALVES)
        self.inverse_made = kit.counter(name + "_inverse_made", G)
        self.inverse_ready = kit.counter(name + "_inverse_ready", G)
        self.turned = kit.counter(name + "_turned", HALVES)
        self.turned_ready = kit.counter(name + "_turned_ready", HALVES)
        self.mixed = kit.counter(name + "_mixed", G)
        self.spread_ready = kit.counter(name + "_spread_ready", G)
        self.normed = kit.counter(name + "_normed", G)
        self.hi_ready = kit.counter(name + "_hi_ready", G)
        self.lo_ready = kit.counter(name + "_lo_ready", G)
        self.out_ready = kit.counter(name + "_out_ready", PAIRS)

    def pe_scores(self, pe, r, banks, h):
        b, c, e = h // 4, (h // 2) % 2, h % 2
        if h == 0:
            pe.wait_ge(self.proj.q_ready.sem, self.proj.q_ready.at(r, 1 if self.q_by_pair else 2))
            if self.mask is not None:
                pe.wait_ge(self.mask.ready.sem, self.mask.ready.at(r, 1))
        if h == 8 and self.q_by_pair:
            pe.wait_ge(self.proj.q_ready.sem, self.proj.q_ready.at(r, 2))
        if h in (0, 2):
            pe.wait_ge(self.proj.k_blocked[c].sem, self.proj.k_blocked[c].at(r, 16 * 8))
        bank = SCORE_BANKS[h % 3]
        banks.claim(pe, r, bank)
        out = banks.psum[:, bank, :].rearrange("p (j k) -> p j k", j=4)
        if self.mask is not None:
            flags = self.mask.flags[:, b if self.mask.per_batch else 0, :]
            pe.matmul(out, self.mask.value_eye[:], flags.unsqueeze(1).broadcast_to([P, 4, SEQ]),
                      start=True, stop=False)
        pe.matmul(out, self.sh.q[:, c, b * SEQ:(b + 1) * SEQ],
                  self.sh.k_block[:, c, e, :, b * SEQ:(b + 1) * SEQ],
                  start=self.mask is None, stop=True).then_inc(self.scores_ready.sem, 1)
        banks.read(bank, self.exp_done, h + 1)

    def pe_turn(self, pe, r, banks, h):
        pe.wait_ge(self.exp_done.sem, self.exp_done.at(r, h + 1))
        banks.claim(pe, r, TURN_BANKS[h % 2])
        for j in range(4):
            ins = pe.transpose(banks.psum[:, TURN_BANKS[h % 2], j * SEQ:(j + 1) * SEQ],
                               self.sh.p[:, h % 4, j, :], self.sh.eye[:])
        ins.then_inc(self.turned.sem, 1)
        banks.read(TURN_BANKS[h % 2], self.turned_ready, h + 1)

    def pe_mix(self, pe, r, banks, h):
        b, c, e = h // 4, (h // 2) % 2, h % 2
        bank = MIX_BANKS[b % 2]
        if h == 0:
            pe.wait_ge(self.proj.v_ready.sem, self.proj.v_ready.at(r, 2))
        if h % 4 == 0:
            banks.claim(pe, r, bank)
        pe.wait_ge(self.turned_ready.sem, self.turned_ready.at(r, h + 1))
        for j in range(4):
            pe.matmul(banks.psum[32 * j:32 * j + 32, bank, c * SEQ:(c + 1) * SEQ],
                      self.sh.v[:, b, c, j, e, :], self.sh.p_turned[:, h % 4, j, :],
                      start=e == 0, stop=e == 1)
        if h % 4 == 3:
            pe.wait_ge(self.inverse_ready.sem, self.inverse_ready.at(r, b + 1))
            for k in range(C):
                ins = pe.transpose(banks.psum[:, bank, DM + k * SEQ:DM + (k + 1) * SEQ],
                                   self.sh.inverse_row[:, b % 2, k * P:(k + 1) * P], self.sh.eye[:])
            ins.then_inc(self.mixed.sem, 1)
            banks.read(bank, self.normed, b + 1)

    def pe_first(self, pe, r, banks):
        self.pe_scores(pe, r, banks, 0)
        self.pe_scores(pe, r, banks, 1)

    def pe_step(self, pe, r, banks, h, reader):
        if h + 2 < HALVES:
            self.pe_scores(pe, r, banks, h + 2)
        self.pe_turn(pe, r, banks, h)
        if h >= 1:
            self.pe_mix(pe, r, banks, h - 1)
        if h in (8, 12):
            self.pe_out(pe, r, banks, h // 4 - 2, reader)

    def pe_out(self, pe, r, banks, b, reader):
        if b % 2 == 0:
            banks.claim(pe, r, OUT_BANK)
        pe.wait_ge(self.lo_ready.sem, self.lo_ready.at(r, b + 1))
        at = self.sh.attended
        ins = product(pe, banks.psum[:, OUT_BANK, (b % 2) * DM:(b % 2 + 1) * DM],
                      [(at.hi[:, k, b * SEQ:(b + 1) * SEQ], at.lo[:, k, b * SEQ:(b + 1) * SEQ])
                       for k in range(C)],
                      [(self.w_out.hi[:, k, :], self.w_out.lo[:, k, :]) for k in range(C)], True, True)
        if b % 2:
            ins.then_inc(self.out_ready.sem, 1)
            banks.read(OUT_BANK, reader, b // 2 + 1)

    def dve_max(self, dve, r, psum, h):
        dve.wait_ge(self.scores_ready.sem, self.scores_ready.at(r, h + 1))
        dve.tensor_reduce(self.sh.neg_max[:, h % 4, :],
                          psum[:, SCORE_BANKS[h % 3], :].rearrange("p (j k) -> p j k", j=4),
                          AX_X, ALU.max, negate=True).then_inc(self.max_ready.sem, 1)

    def dve_step(self, dve, r, psum, h):
        if h + 2 < HALVES:
            self.dve_max(dve, r, psum, h + 2)
        if h % 4 == 3:
            b = h // 4
            dve.wait_ge(self.exp_done.sem, self.exp_done.at(r, h + 1))
            dve.reciprocal(self.sh.inverse[:, b % 2, :], self.sh.sums[:, b % 2, :]) \
               .then_inc(self.inverse_made.sem, 1)
        dve.wait_ge(self.turned.sem, self.turned.at(r, h + 1))
        dve.tensor_copy(self.sh.p_turned[:, h % 4, :, :],
                        psum[:, TURN_BANKS[h % 2], :].rearrange("p (j k) -> p j k", j=4)) \
           .then_inc(self.turned_ready.sem, 1)
        if h >= 5 and h % 4 == 1:
            self.dve_norm(dve, r, psum, h // 4 - 1)

    def dve_norm(self, dve, r, psum, b):
        dve.wait_ge(self.spread_ready.sem, self.spread_ready.at(r, b + 1))
        if b >= 2:
            dve.wait_ge(self.lo_ready.sem, self.lo_ready.at(r, b - 1))
            dve.wait_ge(self.hi_ready.sem, self.hi_ready.at(r, b - 1))
        dve.tensor_tensor(self.sh.mix[:, b % 2, :], psum[:, MIX_BANKS[b % 2], 0:DM],
                          self.sh.spread[:, b % 2, :], ALU.mult).then_inc(self.normed.sem, 1)

    def act_exp(self, act, r, psum, h):
        b, first = h // 4, (h % 4) * 4
        act.wait_ge(self.max_ready.sem, self.max_ready.at(r, h + 1))
        for j in range(4):
            ins = act.activation(self.sh.p[:, h % 4, j, :],
                                 psum[:, SCORE_BANKS[h % 3], j * SEQ:(j + 1) * SEQ],
                                 ACT.Exp, bias=self.sh.neg_max[:, h % 4, j:j + 1],
                                 accum_out=self.sh.sums[:, b % 2, first + j:first + j + 1])
        ins.then_inc(self.exp_done.sem, 1)

    def act_spread(self, act, r, psum, b):
        act.wait_ge(self.mixed.sem, self.mixed.at(r, b + 1))
        act.copy(self.sh.spread[:, b % 2, :], psum[:, MIX_BANKS[b % 2], DM:2 * DM]) \
           .then_inc(self.spread_ready.sem, 1)

    def act_hi(self, act, r, b):
        act.wait_ge(self.normed.sem, self.normed.at(r, b + 1))
        act.copy(self.sh.attended.hi[:, :, b * SEQ:(b + 1) * SEQ],
                 self.sh.mix[:, b % 2, :].rearrange("p (c q) -> p c q", c=C)) \
           .then_inc(self.hi_ready.sem, 1)

    def act_step(self, act, r, psum, h):
        self.act_exp(act, r, psum, h)
        if h >= 5 and h % 4 == 1:
            self.act_spread(act, r, psum, h // 4 - 1)
        if h >= 6 and h % 4 == 2:
            self.act_hi(act, r, h // 4 - 1)

    def pool_inverse(self, pool, r, b):
        pool.wait_ge(self.inverse_made.sem, self.inverse_made.at(r, b + 1))
        pool.sem_inc(self.gate.sem, 1)
        for k in range(C):
            ins = pool.tensor_copy(
                self.sh.inverse_row[:, b % 2, k * P:(k + 1) * P].rearrange(
                    "p (j e d) -> p j e d", j=4, e=2),
                self.sh.inverse[:, b % 2, k * 8:(k + 1) * 8].rearrange(
                    "p (e j) -> p j e", e=2).unsqueeze(3).broadcast_to([P, 4, 2, DK]))
        ins.then_inc(self.inverse_ready.sem, 1)

    def pool_lo(self, pool, r, b):
        pool.wait_ge(self.hi_ready.sem, self.hi_ready.at(r, b + 1))
        pool.tensor_tensor(self.sh.attended.lo[:, :, b * SEQ:(b + 1) * SEQ],
                           self.sh.mix[:, b % 2, :].rearrange("p (c q) -> p c q", c=C),
                           f32(self.sh.attended.hi[:, :, b * SEQ:(b + 1) * SEQ]),
                           ALU.subtract).then_inc(self.lo_ready.sem, 1)

    def pool(self, pool, r, norm):
        for b in range(G):
            self.pool_inverse(pool, r, b)
            if b == G - 1:
                norm.pool_hat(pool, r, 0)
            self.pool_lo(pool, r, b)


class Norm:

    def __init__(self, kit, name, source, source_banks, gain, shift, gain_row, shift_row, sh,
                 norm_banks=NORM_BANKS):
        self.source, self.source_banks, self.norm_banks = source, source_banks, norm_banks
        self.gain, self.shift, self.gain_row, self.shift_row = gain, shift, gain_row, shift_row
        self.sh, self.gate = sh, kit.gate
        self.sum_ready = kit.counter(name + "_sum_ready", 2)
        self.stats_made = kit.counter(name + "_stats_made", G)
        self.moments_ready = kit.counter(name + "_moments_ready", G)
        self.var_made = kit.counter(name + "_var_made", 2)
        self.rstd_made = kit.counter(name + "_rstd_made", 2)
        self.hat_ready = kit.counter(name + "_hat_ready", G)
        self.hat_turned = kit.counter(name + "_hat_turned", 2)
        self.turned_ready = kit.counter(name + "_turned_ready", 2)
        self.hi_ready = kit.counter(name + "_hi_ready", 2)
        self.lo_ready = kit.counter(name + "_lo_ready", 2)
        self.scaled = [kit.counter(f"{name}_scaled{pair}", 1) for pair in range(PAIRS)]
        self.rows_ready = [kit.counter(f"{name}_rows_ready{pair}", 1) for pair in range(PAIRS)]

    def dve_sum(self, dve, r, psum, pair, residual, z_read=None):
        sh = self.sh
        dve.wait_ge(residual[0].sem, residual[0].at(r, residual[1]))
        if z_read is not None:
            dve.wait_ge(z_read[0].sem, z_read[0].at(r, z_read[1]))
        dve.wait_ge(self.source.sem, self.source.at(r, pair + 1))
        dve.tensor_tensor(sh.z[:, 2 * pair:2 * pair + 2, :],
                          psum[:, self.source_banks[pair], :].rearrange("p (b f) -> p b f", b=2),
                          sh.residual[:, 2 * pair:2 * pair + 2, :], ALU.add) \
           .then_inc(self.sum_ready.sem, 1)

    def dve_stats(self, dve, r, pair):
        dve.wait_ge(self.sum_ready.sem, self.sum_ready.at(r, pair + 1))
        for b in (2 * pair, 2 * pair + 1):
            dve.bn_stats(self.sh.stats[:, b, :], self.sh.z[:, b, :]).then_inc(self.stats_made.sem, 1)

    def dve_moments(self, dve, r, pair):
        for b in (2 * pair, 2 * pair + 1):
            dve.wait_ge(self.stats_made.sem, self.stats_made.at(r, b + 1))
            dve.sem_inc(self.gate.sem, 1)
            dve.bn_aggr(self.sh.moments[:, b, :], self.sh.stats[:, b, :]) \
               .then_inc(self.moments_ready.sem, 1)

    def pool_hat(self, pool, r, pair):
        sh = self.sh
        two = slice(2 * pair, 2 * pair + 2)
        pool.wait_ge(self.moments_ready.sem, self.moments_ready.at(r, 2 * pair + 2))
        pool.sem_inc(self.gate.sem, 1)
        pool.tensor_scalar(sh.variance[:, two], sh.moments[:, two, 1], EPS, None, ALU.add) \
            .then_inc(self.var_made.sem, 1)
        pool.wait_ge(self.var_made.sem, self.var_made.at(r, pair + 1))
        pool.tensor_tensor(sh.rstd[:, two], sh.variance[:, two], sh.minus_half[:, 0:2], ALU.pow) \
            .then_inc(self.rstd_made.sem, 1)
        pool.wait_ge(self.rstd_made.sem, self.rstd_made.at(r, pair + 1))
        pool.sem_inc(self.gate.sem, 1)
        for b in (2 * pair, 2 * pair + 1):
            pool.tensor_scalar(sh.z[:, b, :], sh.z[:, b, :], sh.moments[:, b, 0:1],
                               sh.rstd[:, b:b + 1], ALU.subtract, ALU.mult) \
                .then_inc(self.hat_ready.sem, 1)

    def scale_rows(self, engine, r, pair):
        sh = self.sh
        two = slice(2 * pair, 2 * pair + 2)
        engine.wait_ge(self.hat_ready.sem, self.hat_ready.at(r, 2 * pair + 2))
        engine.tensor_tensor(sh.residual[:, two, :], sh.z[:, two, :],
                             self.gain_row.unsqueeze(1).broadcast_to([P, 2, DM]), ALU.mult) \
            .then_inc(self.scaled[pair].sem, 1)

    def shift_rows(self, engine, r, pair):
        sh = self.sh
        two = slice(2 * pair, 2 * pair + 2)
        engine.wait_ge(self.scaled[pair].sem, self.scaled[pair].at(r, 1))
        engine.tensor_tensor(sh.residual[:, two, :], sh.residual[:, two, :],
                             self.shift_row.unsqueeze(1).broadcast_to([P, 2, DM]), ALU.add) \
            .then_inc(self.rows_ready[pair].sem, 1)

    def rows(self, engine, r, pair):
        self.scale_rows(engine, r, pair)
        self.shift_rows(engine, r, pair)

    def pe(self, pe, r, banks, pair):
        bank = self.norm_banks[pair]
        banks.claim(pe, r, bank)
        pe.wait_ge(self.hat_ready.sem, self.hat_ready.at(r, 2 * pair + 2))
        for k in range(C):
            for b in range(2):
                at = (2 * k + b) * SEQ
                ins = pe.transpose(banks.psum[:, bank, at:at + SEQ],
                                   self.sh.z[:, 2 * pair + b, k * P:(k + 1) * P], self.sh.eye[:])
        ins.then_inc(self.hat_turned.sem, 1)
        banks.read(bank, self.turned_ready, pair + 1)

    def act(self, act, r, psum, pair, y_read=None):
        act.wait_ge(self.hat_turned.sem, self.hat_turned.at(r, pair + 1))
        if y_read is not None:
            act.wait_ge(y_read[0].sem, y_read[0].at(r, y_read[1]))
        for k in range(C):
            ins = act.activation(self.sh.y[:, pair, k, :],
                                 psum[:, self.norm_banks[pair], 2 * k * SEQ:(2 * k + 2) * SEQ],
                                 ACT.Identity, bias=self.shift[:, k:k + 1],
                                 scale=self.gain[:, k:k + 1])
        ins.then_inc(self.turned_ready.sem, 1)

    def dve_split(self, dve, r, pair, stored=None):
        sh = self.sh
        if stored is not None:
            dve.wait_ge(stored[0].sem, stored[0].at(r, stored[1]))
        cols = slice(pair * HALF, (pair + 1) * HALF)
        dve.wait_ge(self.turned_ready.sem, self.turned_ready.at(r, pair + 1))
        dve.tensor_copy(sh.yt.hi[:, :, cols], sh.y[:, pair, :, :]).then_inc(self.hi_ready.sem, 1)
        dve.wait_ge(self.hi_ready.sem, self.hi_ready.at(r, pair + 1))
        dve.tensor_tensor(sh.yt.lo[:, :, cols], sh.y[:, pair, :, :], f32(sh.yt.hi[:, :, cols]),
                          ALU.subtract).then_inc(self.lo_ready.sem, 1)


PIECES = PAIRS * M


class FeedForward:

    def __init__(self, kit, name, w1, w2, b1, y_ready, sh):
        self.w1, self.w2, self.b1, self.y_ready, self.sh = w1, w2, b1, y_ready, sh
        self.hidden_in_psum = kit.counter(name + "_hidden_in_psum", PIECES)
        self.hidden_ready = kit.counter(name + "_hidden_ready", PIECES)
        self.hi_ready = kit.counter(name + "_hidden_hi", PIECES)
        self.lo_ready = kit.counter(name + "_hidden_lo", PIECES)
        self.out_ready = kit.counter(name + "_ff_out", PAIRS)

    def pe_hidden(self, pe, r, banks, t):
        pair, m = t // M, t % M
        yt, cols = self.sh.yt, slice(pair * HALF, (pair + 1) * HALF)
        if m == 0:
            pe.wait_ge(self.y_ready.sem, self.y_ready.at(r, pair + 1))
        bank = HIDDEN_BANKS[t % 3]
        banks.claim(pe, r, bank)
        product(pe, banks.psum[:, bank, 0:HALF],
                [(self.w1.hi[:, k, m * P:(m + 1) * P], self.w1.lo[:, k, m * P:(m + 1) * P])
                 for k in range(C)],
                [(yt.hi[:, k, cols], yt.lo[:, k, cols]) for k in range(C)],
                True, True).then_inc(self.hidden_in_psum.sem, 1)
        banks.read(bank, self.hidden_ready, t + 1)

    def pe_out(self, pe, r, banks, t, reader):
        pair, m = t // M, t % M
        h, bank = self.sh.hidden, FF_OUT_BANKS[pair]
        if m == 0:
            banks.claim(pe, r, bank)
        pe.wait_ge(self.lo_ready.sem, self.lo_ready.at(r, t + 1))
        for b in range(2):
            cols = slice(b * SEQ, (b + 1) * SEQ)
            ins = product(pe, banks.psum[:, bank, b * DM:(b + 1) * DM],
                          [(h.hi[:, t % HIDDEN_SLOTS, cols], h.lo[:, t % HIDDEN_SLOTS, cols])],
                          [(self.w2.hi[:, m, :], self.w2.lo[:, m, :])],
                          m == 0 and b == 0, m == M - 1 and b == 1, skip=True)
        if m == M - 1:
            ins.then_inc(self.out_ready.sem, 1)
            banks.read(bank, reader, pair + 1)

    def act_relu(self, act, r, psum, t):
        act.wait_ge(self.hidden_in_psum.sem, self.hidden_in_psum.at(r, t + 1))
        if t >= RELU_SLOTS:
            act.wait_ge(self.lo_ready.sem, self.lo_ready.at(r, t - RELU_SLOTS + 1))
        act.activation(self.sh.relu[:, t % RELU_SLOTS, :], psum[:, HIDDEN_BANKS[t % 3], 0:HALF], ACT.Relu,
                       bias=self.b1[:, t % M:t % M + 1]).then_inc(self.hidden_ready.sem, 1)

    def dve_hi(self, dve, r, t):
        dve.wait_ge(self.hidden_ready.sem, self.hidden_ready.at(r, t + 1))
        dve.tensor_copy(self.sh.hidden.hi[:, t % HIDDEN_SLOTS, :], self.sh.relu[:, t % RELU_SLOTS, :]) \
           .then_inc(self.hi_ready.sem, 1)

    def pool_lo(self, pool, r, t):
        pool.wait_ge(self.hi_ready.sem, self.hi_ready.at(r, t + 1))
        pool.tensor_tensor(self.sh.hidden.lo[:, t % HIDDEN_SLOTS, :], self.sh.relu[:, t % RELU_SLOTS, :],
                           f32(self.sh.hidden.hi[:, t % HIDDEN_SLOTS, :]), ALU.subtract) \
            .then_inc(self.lo_ready.sem, 1)


NORM_BEFORE_STEP = 5
SUM_AFTER_STEP, TURN_AFTER_STEP = 10, 15


class FeedForwardNorms:

    def __init__(self, ff, before, after):
        self.ff, self.before, self.after = ff, before, after

    def pe(self, pe, r, banks):
        for t in range(PIECES + 2):
            if t == NORM_BEFORE_STEP:
                self.before.pe(pe, r, banks, 1)
            if t < PIECES:
                self.ff.pe_hidden(pe, r, banks, t)
            if t == TURN_AFTER_STEP:
                self.after.pe(pe, r, banks, 0)
            if t >= 2:
                self.ff.pe_out(pe, r, banks, t - 2, self.after.sum_ready)

    def act(self, act, r, psum):
        for t in range(PIECES):
            if t == NORM_BEFORE_STEP:
                self.before.act(act, r, psum, 1)
            self.ff.act_relu(act, r, psum, t)
            if t == TURN_AFTER_STEP:
                self.after.act(act, r, psum, 0)

    def dve(self, dve, r, psum):
        for t in range(PIECES):
            if t == NORM_BEFORE_STEP:
                self.before.dve_split(dve, r, 1)
            self.ff.dve_hi(dve, r, t)
            if t == 1:
                self.before.scale_rows(dve, r, 0)
            elif t == 3:
                self.before.shift_rows(dve, r, 0)
            elif t == 6:
                self.before.scale_rows(dve, r, 1)
            elif t == 8:
                self.before.shift_rows(dve, r, 1)
            elif t == SUM_AFTER_STEP:
                self.after.dve_sum(dve, r, psum, 0, (self.before.rows_ready[0], 1))
            elif t == SUM_AFTER_STEP + 1:
                self.after.dve_stats(dve, r, 0)
            elif t == SUM_AFTER_STEP + 2:
                self.after.dve_moments(dve, r, 0)
        self.after.dve_split(dve, r, 0)
        self.after.dve_sum(dve, r, psum, 1, (self.before.rows_ready[1], 1))
        self.after.dve_stats(dve, r, 1)
        self.after.dve_moments(dve, r, 1)
        self.after.rows(dve, r, 0)

    def pool(self, pool, r):
        for t in range(PIECES):
            self.ff.pool_lo(pool, r, t)
            if t == SUM_AFTER_STEP + 2:
                self.after.pool_hat(pool, r, 0)
        self.after.pool_hat(pool, r, 1)
        self.after.rows(pool, r, 1)


class Mask:

    def __init__(self, kit, name, nonzero_masked, value_eye, per_batch):
        self.nonzero_masked, self.value_eye, self.per_batch = nonzero_masked, value_eye, per_batch
        self.gate = kit.gate
        width = G if per_batch else 1
        self.ints = kit.sb(name + "_ints", [P, width, SEQ], I32)
        self.flags = kit.sb(name + "_flags", [P, width, SEQ], BF16)
        self.loaded = kit.counter(name + "_loaded", 16 if per_batch else 0)
        self.ready = kit.counter(name + "_flags_ready", 1 if per_batch else 0)

    def sp(self, sp, r, src):
        if self.per_batch:
            sp.wait_ge(self.ready.sem, self.ready.at(r, 0))
            sp.sem_inc(self.gate.sem, 1)
        sp.dma_start(self.ints[:], src).then_inc(self.loaded.sem, 16)

    def pool(self, pool, r, scores_read=None, ahead=0):
        if scores_read is not None:
            pool.wait_ge(scores_read.sem, scores_read.at(r, 0, ahead))
        pool.wait_ge(self.loaded.sem, self.loaded.at(r, 16, ahead))
        pool.sem_inc(self.gate.sem, 1)
        if self.nonzero_masked:
            pool.tensor_scalar(self.flags[:], self.ints[:], 0.0, 0.0, ALU.is_equal, ALU.is_equal) \
                .then_inc(self.ready.sem, 1)
        else:
            pool.tensor_scalar(self.flags[:], self.ints[:], 0.0, None, ALU.is_equal) \
                .then_inc(self.ready.sem, 1)


class Shared16:

    def __init__(self, kit, feed_forward):
        sb = kit.sb
        self.k_block = sb("k_block", [P, C, 2, 4, TOK], F32)
        self.q = sb("q", [P, C, TOK], F32)
        self.k = sb("k", [P, C, TOK], F32)
        self.v = sb("v", [P, G, C, 4, 2, 32], F32)
        self.p = sb("p", [P, 4, 4, SEQ], F32)
        self.p_turned = sb("p_turned", [P, 4, 4, SEQ], F32)
        self.neg_max = sb("neg_max", [P, 4, 4], F32)
        self.sums = sb("sums", [P, 2, HEADS], F32)
        self.inverse = sb("inverse", [P, 2, HEADS], F32)
        self.inverse_row = sb("inverse_row", [P, 2, DM], F32)
        self.spread = sb("spread", [P, 2, DM], F32)
        self.mix = sb("mix", [P, 2, DM], F32)
        self.attended = Split(kit, "attended", [P, C, TOK])
        self.z = sb("z", [P, G, DM], F32)
        self.residual = sb("residual", [P, G, DM], F32)
        self.stats = sb("stats", [P, G, 6], F32)
        self.moments = sb("moments", [P, G, 2], F32)
        self.variance = sb("variance", [P, G], F32)
        self.rstd = sb("rstd", [P, G], F32)
        self.minus_half = sb("minus_half", [P, 4], F32)
        self.eye = sb("eye", [P, P], F32)
        self.v_slots = [self.v[:, b].rearrange("p c j e f -> p (c j) (e f)").rearrange(
            "p g (x d) -> p g x d", d=DK)[:, :, 0:4:3, :] for b in range(G)]
        if feed_forward:
            self.y = sb("y", [P, PAIRS, C, HALF], F32)
            self.yt = Split(kit, "yt", [P, C, TOK])
            self.relu = self.p_turned[:].rearrange("p u j q -> p (u j q)").rearrange(
                "p (s t) -> p s t", t=HALF)
            self.hidden = Split(kit, "hidden", [P, HIDDEN_SLOTS, HALF])


class View:

    def __init__(self, split, cut):
        self.hi, self.lo = cut(split.hi), cut(split.lo)


STAGE_COLS = 2048


FULL_COLS = dict(q1=0, k1=2, q2=4, k2=6, g1=8, s1=10, g2=12, s2=14, g3=16, s3=18, ff=20)
FULL_ROWS = ["v1", "v2", "o1", "g1", "s1", "g2", "s2", "g3", "s3", "o2", "ff"]
LAST_COLS = dict(q1=0, k1=2)
LAST_ROWS = ["v1", "o1", "g1", "s1"]


def phase16(nc, tag, full, x, ctx_t, masks, packed, cols, rows, out):
    with ExitStack() as ctx:
        kit = Kit(nc, ctx, tag)
        sh = Shared16(kit, full)
        psum = ctx.enter_context(nc.psum_tensor(f"{tag}_psum", [P, 8, 512], F32))
        col = kit.sb("cols", list(cols.shape), F32)
        names = FULL_ROWS if full else LAST_ROWS
        at_col = FULL_COLS if full else LAST_COLS
        extra = 2 if full else 0
        row = kit.sb("rows", [P, len(names) - extra, DM], F32)
        n_cols = packed.shape[1]
        weights = Split(kit, "w", [P, n_cols])
        xt = Split(kit, "xt", [P, C, TOK])
        ct = Split(kit, "ct", [P, C, TOK])
        x_rows = kit.sb("x_rows", [P, G, DM], F32)
        stage = sh.k_block[:].rearrange("p c e j t -> p (c e j t)")

        def take(at, width, inner):
            return View(weights, lambda t: t[:, at:at + width].rearrange("p (c n) -> p c n", n=inner))

        def rowv(name):
            i = names.index(name)
            return row[:, i, :] if i < len(names) - extra else sh.z[:, i - len(names) + extra, :]

        def colv(name, n=2):
            return col[:, at_col[name]:at_col[name] + n]

        W1, W2 = 4 * 512 * (2 if full else 1), 4 * 512 * (2 if full else 1) + 2048
        wq = [take(i * 2048, 512, DM) for i in range(2 if full else 1)]
        wk = [take(i * 2048 + 512, 512, DM) for i in range(2 if full else 1)]
        wv = [take(i * 2048 + 1024, 512, DM) for i in range(2 if full else 1)]
        wo = [take(i * 2048 + 1536, 512, DM) for i in range(2 if full else 1)]

        def weights_of(i):
            n = str(i + 1)
            return {"q": wq[i], "k": wk[i], "v": wv[i], "q_bias": colv("q" + n), "k_bias": colv("k" + n),
                    "v_row": rowv("v" + n)}

        small_loaded = kit.counter("small_loaded", 0)
        hi_made = kit.counter("w_hi_made", 0)
        lo_made = kit.counter("w_lo_made", 0)
        consts = kit.counter("consts", 0)
        biases = kit.counter("biases", 0)
        zeroed = kit.counter("zeroed", 0)
        block_zeroed = kit.counter("block_zeroed", 0)
        slots = n_cols // STAGE_COLS
        stage_loaded = [kit.counter(f"stage_loaded{s}", 0) for s in range(slots)]

        x_loaded = kit.counter("x_loaded", 32)
        ct_loaded = kit.counter("ct_loaded", 32)
        rows_loaded = kit.counter("rows_loaded", 16)
        residual_ready = kit.counter("residual_ready", 1)
        stored = kit.counter("stored", 48 if full else 16)

        def mask_of(name, spec):
            if spec is None:
                return None
            src, nonzero_masked, value, per_batch = spec
            eye = kit.sb(name + "_eye", [P, P], BF16)
            m = Mask(kit, name, nonzero_masked, eye, per_batch)
            m.src, m.value = src, value
            return m

        mask = [mask_of(f"mask{i + 1}", spec) for i, spec in enumerate(masks)]
        if full:
            proj = [Project16(kit, "a1", weights_of(0), sh, (0, 3), (4, 5)),
                    Project16(kit, "a2", weights_of(1), sh, (0, 3), (6, 7))]
        else:
            proj = [Project16(kit, "a1", weights_of(0), sh, (0, 1), (6, 7))]
        att = [Attend16(kit, f"a{i + 1}", proj[i], mask[i], wo[i], sh, q_by_pair=i == 1)
               for i in range(len(proj))]
        norm = [Norm(kit, f"n{i + 1}", att[i].out_ready, (OUT_BANK, OUT_BANK),
                     colv(f"g{i + 1}") if full else None, colv(f"s{i + 1}") if full else None,
                     rowv(f"g{i + 1}"), rowv(f"s{i + 1}"), sh) for i in range(len(proj))]
        if full:
            w1 = take(W1, 2048, DFF)
            w2 = take(W2, 2048, DM)
            ff = FeedForward(kit, "ff", w1, w2, colv("ff", M), norm[1].lo_ready, sh)
            norm.append(Norm(kit, "n3", ff.out_ready, FF_OUT_BANKS, colv("g3"), colv("s3"),
                             rowv("g3"), rowv("s3"), sh))
            ff_norms = FeedForwardNorms(ff, norm[1], norm[2])
        final = norm[-1]

        block = ctx.enter_context(nc.Block())

        @block.sync
        def _(sp):
            def load_stage(s):
                sp.dma_start(stage[:, s * STAGE_COLS:(s + 1) * STAGE_COLS],
                             packed[:, s * STAGE_COLS:(s + 1) * STAGE_COLS]) \
                  .then_inc(stage_loaded[s].sem, 16)

            load_stage(0)
            sp.dma_start(col[:], cols).then_inc(small_loaded.sem, 16)
            kept = len(names) - extra
            for first, end, dst in ((0, kept, row), (kept, len(names), sh.z)):
                if end > first:
                    sp.dma_start(dst[:, 0:end - first, :].rearrange("p n f -> p (n f)"),
                                 rows[first:end, :].rearrange("(o n) f -> o (n f)", o=1)
                                 .broadcast_to([P, (end - first) * DM])).then_inc(small_loaded.sem, 16)
            for m in mask:
                if m is not None and not m.per_batch:
                    m.sp(sp, 0, m.src)

            def load_x(r):
                tok = bass.ds(r * TOK, TOK)
                sp.wait_ge(proj[0].v_in_psum.sem, proj[0].v_in_psum.at(r, 0))
                sp.wait_ge(proj[0].q_in_psum.sem, proj[0].q_in_psum.at(r, 0))
                kit.gated(sp)
                for part, src in ((xt.hi, x[0]), (xt.lo, x[1])):
                    sp.dma_start(f32(part[:]), src[:, tok].rearrange("(c p) t -> p c t", p=P)) \
                      .then_inc(x_loaded.sem, 16)

            def load_context(r):
                tok = bass.ds(r * TOK, TOK)
                sp.wait_ge(proj[-1].v_in_psum.sem, proj[-1].v_in_psum.at(r, 0))
                kit.gated(sp)
                for part, src in ((ct.hi, ctx_t[0]), (ct.lo, ctx_t[1])):
                    sp.dma_start(f32(part[:]), src[:, tok].rearrange("(c p) t -> p c t", p=P)) \
                      .then_inc(ct_loaded.sem, 16)

            def load_beside(r):
                tok = bass.ds(r * TOK, TOK)
                sp.wait_ge(residual_ready.sem, residual_ready.at(r, 0))
                kit.gated(sp)
                sp.dma_start(x_rows[:], x[2][tok, :].rearrange("(b t) f -> t b f", b=G)) \
                  .then_inc(rows_loaded.sem, 16)
                for m in mask:
                    if m is not None and m.per_batch:
                        m.sp(sp, r, m.src[bass.ds(r * G, G)].rearrange("b q k -> q b k"))

            def one_round(r, more):
                tok = bass.ds(r * TOK, TOK)
                if more:
                    load_x(r + 1)
                    load_beside(r + 1)
                    if not full:
                        load_context(r + 1)
                if full:
                    proj[1].sp_k(sp, r)
                    if more:
                        load_context(r + 1)
                if more:
                    proj[0].sp_k(sp, r, 1)
                for rows_ready in final.rows_ready:
                    sp.wait_ge(rows_ready.sem, rows_ready.at(r, 1))
                kit.gated(sp)
                sp.dma_start(out[2][tok, :].rearrange("(b t) f -> t b f", b=G), sh.residual[:]) \
                  .then_inc(stored.sem, 16)
                if full:
                    sp.wait_ge(final.lo_ready.sem, final.lo_ready.at(r, 2))
                    kit.gated(sp)
                    for part, dst in ((sh.yt.hi, out[0]), (sh.yt.lo, out[1])):
                        sp.dma_start(dst[:, tok].rearrange("(c p) t -> p c t", p=P), f32(part[:])) \
                          .then_inc(stored.sem, 16)

            load_x(0)
            if not full:
                load_context(0)
            for s in range(1, slots):
                load_stage(s)
            if full:
                load_context(0)
            load_beside(0)
            if slots > 1:
                sp.wait_ge(block_zeroed.sem, slots - 1)
            proj[0].sp_k(sp, 0)
            with sp.Fori(0, ROUNDS - 1) as r:
                one_round(r, True)
            one_round(ROUNDS - 1, False)
            sp.wait_ge(stored.sem, stored.at(ROUNDS, 0))

        @block.scalar
        def _(act):
            for s in range(slots):
                act.wait_ge(stage_loaded[s].sem, 16)
                at = slice(s * STAGE_COLS, (s + 1) * STAGE_COLS)
                act.copy(weights.hi[:, at], stage[:, at]).then_inc(hi_made.sem, 1)
            act.wait_ge(biases.sem, 1)

            def one_round(r, more):
                for h in range(HALVES):
                    att[0].act_step(act, r, psum, h)
                att[0].act_spread(act, r, psum, G - 1)
                att[0].act_hi(act, r, G - 1)
                if not full:
                    if more:
                        proj[0].act_q_chunk(act, r, psum, 0, 1)
                        proj[0].act_q_chunk(act, r, psum, 1, 1)
                    return
                norm[0].act(act, r, psum, 0, (norm[2].lo_ready, 0))
                proj[1].act_q_pair(act, r, psum, 0)
                norm[0].act(act, r, psum, 1)
                for h in range(HALVES):
                    att[1].act_step(act, r, psum, h)
                    if h == 4:
                        proj[1].act_q_pair(act, r, psum, 1)
                att[1].act_spread(act, r, psum, G - 1)
                att[1].act_hi(act, r, G - 1)
                norm[1].act(act, r, psum, 0)
                if more:
                    proj[0].act_q_chunk(act, r, psum, 0, 1)
                ff_norms.act(act, r, psum)
                if more:
                    proj[0].act_q_chunk(act, r, psum, 1, 1)
                norm[2].act(act, r, psum, 1)

            for c in range(C):
                proj[0].act_q_chunk(act, 0, psum, c)
            with act.Fori(0, ROUNDS - 1) as r:
                one_round(r, True)
            one_round(ROUNDS - 1, False)

        @block.vector
        def _(dve):
            dve.memset(sh.minus_half[:], -0.5)
            dve.memset(sh.v[:], 0.0).then_inc(zeroed.sem, 1)

            def split_lo(s):
                dve.wait_ge(hi_made.sem, s + 1)
                at = slice(s * STAGE_COLS, (s + 1) * STAGE_COLS)
                dve.tensor_tensor(weights.lo[:, at], stage[:, at], f32(weights.hi[:, at]),
                                  ALU.subtract).then_inc(lo_made.sem, 1)

            split_lo(0)
            dve.wait_ge(small_loaded.sem, 16 * (3 if full else 2))
            for i in range(len(proj)):
                dve.tensor_scalar(colv(f"q{i + 1}"), colv(f"q{i + 1}"), DK ** -0.5, None, ALU.mult)
            if full:
                dve.tensor_tensor(rowv("s1"), rowv("s1"), rowv("o2"), ALU.add)
                dve.tensor_tensor(rowv("s2"), rowv("s2"), rowv("ff"), ALU.add)
            dve.memset(sh.stats[:], 0.0).then_inc(biases.sem, 1)
            dve.wait_ge(biases.sem, 1)
            for s in range(1, slots):
                split_lo(s)
            dve.wait_ge(lo_made.sem, slots)
            dve.memset(stage[:, (slots - 1) * STAGE_COLS:], 0.0).then_inc(zeroed.sem, 1)
            dve.wait_ge(zeroed.sem, 2)

            def attend(r, att, norm, residual, z_read, k_next, steps):
                att.dve_max(dve, r, psum, 0)
                att.dve_max(dve, r, psum, 1)
                for h in range(HALVES):
                    att.dve_step(dve, r, psum, h)
                    if h == 0 and steps is not None:
                        steps.dve_split(dve, r, 1)
                    if h == 13:
                        norm.dve_sum(dve, r, psum, 0, residual[0], z_read and z_read[0])
                    elif h == 14:
                        norm.dve_stats(dve, r, 0)
                    elif h == 15:
                        norm.dve_moments(dve, r, 0)
                if k_next is not None:
                    k_next[0].dve_k(dve, r, psum, 0, *k_next[1:])
                att.dve_norm(dve, r, psum, G - 1)
                if k_next is not None:
                    k_next[0].dve_k(dve, r, psum, 1, *k_next[1:])
                norm.dve_sum(dve, r, psum, 1, residual[1], z_read and z_read[1])
                norm.dve_stats(dve, r, 1)
                norm.dve_moments(dve, r, 1)

            def one_round(r, more):
                first = ((residual_ready, 1), (residual_ready, 1))
                scaled = ((final.scaled[0], 0), (final.scaled[1], 0))
                if not full:
                    attend(r, att[0], norm[0], first, scaled,
                           (proj[0], (proj[0], 16 * 8), 1) if more else None, None)
                    if more:
                        proj[0].dve_v(dve, r, psum, 1)
                    return
                attend(r, att[0], norm[0], first, scaled, (proj[1], (proj[0], 16 * 8)), None)
                norm[0].dve_split(dve, r, 0, (stored, 0))
                proj[1].dve_v(dve, r, psum)
                attend(r, att[1], norm[1], ((norm[0].rows_ready[0], 1), (norm[0].rows_ready[1], 1)), None,
                       (proj[0], (proj[1], 16 * 8), 1) if more else None, norm[0])
                norm[1].dve_split(dve, r, 0)
                ff_norms.dve(dve, r, psum)
                if more:
                    proj[0].dve_v(dve, r, psum, 1)
                norm[2].dve_split(dve, r, 1)

            for c in range(C):
                proj[0].dve_k(dve, 0, psum, c, (proj[0], 0))
            proj[0].dve_v(dve, 0, psum)
            with dve.Fori(0, ROUNDS - 1) as r:
                one_round(r, True)
            one_round(ROUNDS - 1, False)

        @block.gpsimd
        def _(pool):
            pool.memset(sh.eye[:], 1.0).then_inc(consts.sem, 1)
            pool.wait_ge(consts.sem, 1)
            pool.affine_select(out=sh.eye[:], in_=sh.eye[:], compare_op=ALU.is_equal, fill=0.0,
                               base=0, pattern=[[1, P]], channel_multiplier=-1).then_inc(consts.sem, 1)
            pool.wait_ge(consts.sem, 2)
            made = 2
            for m in mask:
                if m is not None:
                    pool.tensor_scalar(m.value_eye[:], sh.eye[:], m.value, None, ALU.mult) \
                        .then_inc(consts.sem, 1)
                    made += 1
                    if not m.per_batch:
                        m.pool(pool, 0)
            pool.wait_ge(consts.sem, made)
            for s in range(slots - 1):
                pool.wait_ge(lo_made.sem, s + 1)
                pool.memset(stage[:, s * STAGE_COLS:(s + 1) * STAGE_COLS], 0.0) \
                    .then_inc(block_zeroed.sem, 1)
            pool.wait_ge(biases.sem, 1)

            def one_round(r, more):
                pool.wait_ge(stored.sem, stored.at(r, 0))
                pool.wait_ge(rows_loaded.sem, rows_loaded.at(r, 16))
                pool.tensor_tensor(sh.residual[:], x_rows[:],
                                   rowv("o1").unsqueeze(1).broadcast_to([P, G, DM]), ALU.add) \
                    .then_inc(residual_ready.sem, 1)
                for i in range(len(att)):
                    att[i].pool(pool, r, norm[i])
                    norm[i].pool_hat(pool, r, 1)
                    if i == 0:
                        for pair in range(PAIRS):
                            norm[0].rows(pool, r, pair)
                    else:
                        ff_norms.pool(pool, r)
                    if more and mask[i] is not None and mask[i].per_batch:
                        mask[i].pool(pool, r, att[i].scores_ready, 1)

            for m in mask:
                if m is not None and m.per_batch:
                    m.pool(pool, 0)
            with pool.Fori(0, ROUNDS - 1) as r:
                one_round(r, True)
            one_round(ROUNDS - 1, False)

        @block.tensor
        def _(pe):
            kit.start(pe)

            def one_round(r, more):
                banks = Banks(psum)
                if full:
                    for bank, reader, n in ((0, ff.hidden_ready, 0), (1, final.turned_ready, 0),
                                            (2, final.turned_ready, 0), (3, proj[0].q_ready, 2),
                                            (4, proj[0].v_ready, 1), (5, proj[0].v_ready, 2),
                                            (6, final.sum_ready, 0), (7, final.sum_ready, 0)):
                        banks.read(bank, reader, n)
                else:
                    for bank, reader, n in ((0, proj[0].q_ready, 1), (1, proj[0].q_ready, 2),
                                            (2, att[0].exp_done, 0), (3, final.sum_ready, 0),
                                            (4, proj[0].k_ready, 1), (5, proj[0].k_ready, 2),
                                            (6, proj[0].v_ready, 1), (7, proj[0].v_ready, 2)):
                        banks.read(bank, reader, n)
                att[0].pe_first(pe, r, banks)
                for h in range(HALVES):
                    att[0].pe_step(pe, r, banks, h, norm[0].sum_ready)
                if not full:
                    if more:
                        pe.wait_ge(ct_loaded.sem, ct_loaded.at(r, 32, 1))
                        proj[0].pe_k(pe, r, banks, ct, 0, 1)
                    att[0].pe_mix(pe, r, banks, HALVES - 1)
                    if more:
                        proj[0].pe_k(pe, r, banks, ct, 1, 1)
                        pe.wait_ge(x_loaded.sem, x_loaded.at(r, 32, 1))
                        proj[0].pe_q_chunk(pe, r, banks, xt, 0, 1)
                    att[0].pe_out(pe, r, banks, 2, norm[0].sum_ready)
                    att[0].pe_out(pe, r, banks, 3, norm[0].sum_ready)
                    if more:
                        proj[0].pe_q_chunk(pe, r, banks, xt, 1, 1)
                        proj[0].pe_v(pe, r, banks, ct, 1)
                    return
                pe.wait_ge(ct_loaded.sem, ct_loaded.at(r, 32))
                proj[1].pe_k(pe, r, banks, ct, 0)
                att[0].pe_mix(pe, r, banks, HALVES - 1)
                proj[1].pe_k(pe, r, banks, ct, 1)
                att[0].pe_out(pe, r, banks, 2, norm[0].sum_ready)
                norm[0].pe(pe, r, banks, 0)
                att[0].pe_out(pe, r, banks, 3, norm[0].sum_ready)
                proj[1].pe_v(pe, r, banks, ct)
                pe.wait_ge(norm[0].lo_ready.sem, norm[0].lo_ready.at(r, 1))
                proj[1].pe_q_pair(pe, r, banks, sh.yt, 0)
                norm[0].pe(pe, r, banks, 1)
                att[1].pe_first(pe, r, banks)
                for h in range(HALVES):
                    att[1].pe_step(pe, r, banks, h, norm[1].sum_ready)
                    if h == 3:
                        pe.wait_ge(norm[0].lo_ready.sem, norm[0].lo_ready.at(r, 2))
                        proj[1].pe_q_pair(pe, r, banks, sh.yt, 1)
                if more:
                    pe.wait_ge(x_loaded.sem, x_loaded.at(r, 32, 1))
                    proj[0].pe_k(pe, r, banks, xt, 0, 1)
                att[1].pe_mix(pe, r, banks, HALVES - 1)
                if more:
                    proj[0].pe_k(pe, r, banks, xt, 1, 1)
                att[1].pe_out(pe, r, banks, 2, norm[1].sum_ready)
                norm[1].pe(pe, r, banks, 0)
                att[1].pe_out(pe, r, banks, 3, norm[1].sum_ready)
                if more:
                    proj[0].pe_q_chunk(pe, r, banks, xt, 0, 1)
                ff_norms.pe(pe, r, banks)
                if more:
                    proj[0].pe_v(pe, r, banks, xt, 1)
                    proj[0].pe_q_chunk(pe, r, banks, xt, 1, 1)
                norm[2].pe(pe, r, banks, 1)

            banks = Banks(psum)
            pe.wait_ge(lo_made.sem, 1)
            pe.wait_ge(x_loaded.sem, x_loaded.at(0, 32))
            if not full:
                pe.wait_ge(ct_loaded.sem, ct_loaded.at(0, 32))
            kv = xt if full else ct
            for c in range(C):
                proj[0].pe_k(pe, 0, banks, kv, c)
            for c in range(C):
                proj[0].pe_q_chunk(pe, 0, banks, xt, c)
            proj[0].pe_v(pe, 0, banks, kv)
            pe.wait_ge(lo_made.sem, slots)
            pe.wait_ge(zeroed.sem, 2)
            pe.wait_ge(consts.sem, 2 + sum(m is not None for m in mask))
            with pe.Fori(0, ROUNDS - 1) as r:
                one_round(r, True)
            one_round(ROUNDS - 1, False)



H8 = 8
OUT8_BANKS = (0, 1)
Q8_BANK, K8_BANK, V8_BANK, S8_BANK, TURN8_BANK, MIX8_BANK = 2, 3, 4, 5, 6, 7
DK8 = 128
MASKED = -1.5e38


class Attend8:

    def __init__(self, kit, name, w, sh):
        self.w, self.sh = w, sh
        self.q_in_psum = kit.counter(name + "_q_in_psum", H8)
        self.q_ready = kit.counter(name + "_q_ready", H8)
        self.k_in_psum = kit.counter(name + "_k_in_psum", H8)
        self.k_ready = kit.counter(name + "_k_ready", H8)
        self.v_in_psum = kit.counter(name + "_v_in_psum", H8)
        self.v_ready = kit.counter(name + "_v_ready", H8)
        self.scores_ready = kit.counter(name + "_scores_ready", H8)
        self.max_ready = kit.counter(name + "_max_ready", H8)
        self.exp_done = kit.counter(name + "_exp_done", H8)
        self.inverse_ready = kit.counter(name + "_inverse_ready", H8)
        self.p_ready = kit.counter(name + "_p_ready", H8)
        self.turned = kit.counter(name + "_turned", H8)
        self.turned_ready = kit.counter(name + "_turned_ready", H8)
        self.mixed = kit.counter(name + "_mixed", H8)
        self.hi_ready = kit.counter(name + "_hi_ready", H8)
        self.lo_ready = kit.counter(name + "_lo_ready", H8)
        self.out_ready = kit.counter(name + "_out_ready", 2)

    def pe_head(self, pe, r, banks, which, src, h, ahead=0):
        bank, done, reader = ((Q8_BANK, self.q_in_psum, self.q_ready) if which == "q" else
                              (K8_BANK, self.k_in_psum, self.k_ready))
        banks.claim(pe, r, bank)
        w = self.w[which]
        product(pe, banks.psum[:, bank, :],
                [(w.hi[:, k, h * P:(h + 1) * P], w.lo[:, k, h * P:(h + 1) * P]) for k in range(C)],
                [(src.hi[:, k, :], src.lo[:, k, :]) for k in range(C)],
                True, True).then_inc(done.sem, 1)
        banks.read(bank, reader, h + 1, ahead)

    def pe_v(self, pe, r, banks, src, i, ahead=0):
        banks.claim(pe, r, V8_BANK)
        w = self.w["v"]
        heads = slice((i // 2) * 2 * DK8, (i // 2 + 1) * 2 * DK8)
        for k in range(2):
            b = 2 * (i % 2) + k
            ins = product(pe, banks.psum[:, V8_BANK, k * DM:(k + 1) * DM],
                          [(src.hi[:, c, b * SEQ:(b + 1) * SEQ], src.lo[:, c, b * SEQ:(b + 1) * SEQ])
                           for c in range(C)],
                          [(w.hi[:, c, heads], w.lo[:, c, heads]) for c in range(C)], True, True)
        ins.then_inc(self.v_in_psum.sem, 1)
        banks.read(V8_BANK, self.v_ready, i + 1, ahead)

    def pe_scores(self, pe, r, banks, h):
        sh = self.sh
        banks.claim(pe, r, S8_BANK)
        out = banks.psum[:, S8_BANK, :]
        pe.matmul(out, sh.masked_eye[:], sh.flags[:].rearrange("p b k -> p (b k)"),
                  start=True, stop=False, skip_group_check=True)
        pe.wait_ge(self.q_ready.sem, self.q_ready.at(r, h + 1))
        pe.wait_ge(self.k_ready.sem, self.k_ready.at(r, h + 1))
        for b in range(G):
            at = slice(b * SEQ, (b + 1) * SEQ)
            ins = pe.matmul(out[:, at], sh.q[:, h % 2, at], sh.k[:, h % 2, at],
                            start=False, stop=b == G - 1, skip_group_check=True)
        ins.then_inc(self.scores_ready.sem, 1)
        banks.read(S8_BANK, self.exp_done, h + 1)

    def pe_turn(self, pe, r, banks, h):
        banks.claim(pe, r, TURN8_BANK)
        pe.wait_ge(self.p_ready.sem, self.p_ready.at(r, h + 1))
        for b in range(G):
            ins = pe.transpose(banks.psum[:, TURN8_BANK, b * SEQ:(b + 1) * SEQ],
                               self.sh.p[:, h % 2, b, :], self.sh.eye[:])
        ins.then_inc(self.turned.sem, 1)
        banks.read(TURN8_BANK, self.turned_ready, h + 1)

    def pe_mix(self, pe, r, banks, h):
        banks.claim(pe, r, MIX8_BANK)
        if h % 2 == 0:
            pe.wait_ge(self.v_ready.sem, self.v_ready.at(r, h + 2))
        pe.wait_ge(self.turned_ready.sem, self.turned_ready.at(r, h + 1))
        for b in range(G):
            ins = pe.matmul(banks.psum[:, MIX8_BANK, b * SEQ:(b + 1) * SEQ],
                            self.sh.v[:, (h // 2) % 2, b, (h % 2) * DK8:(h % 2 + 1) * DK8],
                            self.sh.p_turned[:, h % 2, b, :], start=True, stop=True)
        ins.then_inc(self.mixed.sem, 1)
        banks.read(MIX8_BANK, self.lo_ready, h + 1)

    def pe_out(self, pe, r, banks, h, reader):
        at, w = self.sh.attended, self.w["o"]
        if h == 0:
            banks.claim(pe, r, *OUT8_BANKS)
        pe.wait_ge(self.lo_ready.sem, self.lo_ready.at(r, h + 1))
        for b in range(G):
            cols = slice(b * SEQ, (b + 1) * SEQ)
            ins = product(pe, banks.psum[:, OUT8_BANKS[b // 2], (b % 2) * DM:(b % 2 + 1) * DM],
                          [(at.hi[:, h % 2, cols], at.lo[:, h % 2, cols])],
                          [(w.hi[:, h, :], w.lo[:, h, :])],
                          h == 0 and b % 2 == 0, h == H8 - 1 and b % 2 == 1, skip=True)
            if h == H8 - 1 and b % 2:
                ins.then_inc(self.out_ready.sem, 1)
                banks.read(OUT8_BANKS[b // 2], reader, b // 2 + 1)

    def pe_first(self, pe, banks, q_src, kv_src):
        for h in range(2):
            self.pe_v(pe, 0, banks, kv_src, h)
            self.pe_head(pe, 0, banks, "q", q_src, h)
            self.pe_head(pe, 0, banks, "k", kv_src, h)

    def pe(self, pe, r, banks, q_src, kv_src, reader, more, next_q, next_kv):
        for h in range(H8):
            self.pe_scores(pe, r, banks, h)
            i, ahead = (h + 2) % H8, (h + 2) // H8
            if not ahead or more:
                if h == H8 - 2:
                    pe.wait_ge(next_kv.sem, next_kv.at(r, next_kv.per_round, 1))
                self.pe_v(pe, r, banks, kv_src, i, ahead)
                if h == H8 - 2:
                    pe.wait_ge(next_q.sem, next_q.at(r, next_q.per_round, 1))
                self.pe_head(pe, r, banks, "q", q_src, i, ahead)
                if h < H8 - 1:
                    self.pe_head(pe, r, banks, "k", kv_src, i, ahead)
            self.pe_turn(pe, r, banks, h)
            if h >= 1:
                self.pe_out(pe, r, banks, h - 1, reader)
            self.pe_mix(pe, r, banks, h)
        if more:
            self.pe_head(pe, r, banks, "k", kv_src, 1, 1)
        self.pe_out(pe, r, banks, H8 - 1, reader)

    def act_q(self, act, r, psum, h, ahead=0):
        act.wait_ge(self.q_in_psum.sem, self.q_in_psum.at(r, h + 1, ahead))
        act.activation(self.sh.q[:, h % 2, :], psum[:, Q8_BANK, :], ACT.Identity,
                       bias=self.w["q_bias"][:, h:h + 1], scale=DK8 ** -0.5) \
           .then_inc(self.q_ready.sem, 1)

    def act_exp(self, act, r, psum, h):
        sh = self.sh
        act.wait_ge(self.max_ready.sem, self.max_ready.at(r, h + 1))
        for b in range(G):
            ins = act.activation(sh.p[:, h % 2, b, :], psum[:, S8_BANK, b * SEQ:(b + 1) * SEQ],
                                 ACT.Exp, bias=sh.neg_max[:, h % 2, b:b + 1],
                                 accum_out=sh.sums[:, h % 2, b:b + 1])
        ins.then_inc(self.exp_done.sem, 1)

    def act_step(self, act, r, psum, h, more, split_x):
        self.act_exp(act, r, psum, h)
        if h + 2 < H8 or more:
            self.act_q(act, r, psum, (h + 2) % H8, (h + 2) // H8)
        if h == H8 - 3 and split_x is not None:
            split_x(r + 1)
        act.wait_ge(self.turned.sem, self.turned.at(r, h + 1))
        act.copy(self.sh.p_turned[:, h % 2, :, :],
                 psum[:, TURN8_BANK, :].rearrange("p (b q) -> p b q", b=G)) \
           .then_inc(self.turned_ready.sem, 1)
        act.wait_ge(self.mixed.sem, self.mixed.at(r, h + 1))
        act.copy(self.sh.attended.hi[:, h % 2, :], psum[:, MIX8_BANK, :]) \
           .then_inc(self.hi_ready.sem, 1)

    def dve_v(self, dve, r, psum, i, ahead=0):
        dve.wait_ge(self.v_in_psum.sem, self.v_in_psum.at(r, i + 1, ahead))
        heads = slice((i // 2) * 2 * DK8, (i // 2 + 1) * 2 * DK8)
        two = 2 * (i % 2)
        dve.tensor_tensor(self.sh.v[:, (i // 2) % 2, two:two + 2, :],
                          psum[:, V8_BANK, :].rearrange("p (b f) -> p b f", b=2),
                          self.w["v_row"][:, heads].unsqueeze(1).broadcast_to([P, 2, DM]),
                          ALU.add).then_inc(self.v_ready.sem, 1)

    def dve_k(self, dve, r, psum, h, ahead=0):
        dve.wait_ge(self.k_in_psum.sem, self.k_in_psum.at(r, h + 1, ahead))
        dve.tensor_scalar(self.sh.k[:, h % 2, :], psum[:, K8_BANK, :],
                          self.w["k_bias"][:, h:h + 1], None, ALU.add) \
           .then_inc(self.k_ready.sem, 1)

    def dve(self, dve, r, psum, more):
        sh = self.sh
        for h in range(H8):
            dve.wait_ge(self.scores_ready.sem, self.scores_ready.at(r, h + 1))
            dve.tensor_reduce(sh.neg_max[:, h % 2, :],
                              psum[:, S8_BANK, :].rearrange("p (b k) -> p b k", b=G),
                              AX_X, ALU.max, negate=True).then_inc(self.max_ready.sem, 1)
            project = h + 2 < H8 or more
            i, ahead = (h + 2) % H8, (h + 2) // H8
            if project and h != H8 - 2:
                self.dve_v(dve, r, psum, i, ahead)
            dve.wait_ge(self.exp_done.sem, self.exp_done.at(r, h + 1))
            dve.reciprocal(sh.inverse[:, h % 2, :], sh.sums[:, h % 2, :]) \
               .then_inc(self.inverse_ready.sem, 1)
            dve.wait_ge(self.inverse_ready.sem, self.inverse_ready.at(r, h + 1))
            dve.tensor_tensor(sh.p[:, h % 2, :, :], sh.p[:, h % 2, :, :],
                              sh.inverse[:, h % 2, :].unsqueeze(2).broadcast_to([P, G, SEQ]),
                              ALU.mult).then_inc(self.p_ready.sem, 1)
            if project and h == H8 - 2:
                self.dve_v(dve, r, psum, i, ahead)
            if project and h < H8 - 1:
                self.dve_k(dve, r, psum, i, ahead)
            dve.wait_ge(self.hi_ready.sem, self.hi_ready.at(r, h + 1))
            dve.tensor_tensor(sh.attended.lo[:, h % 2, :], psum[:, MIX8_BANK, :],
                              f32(sh.attended.hi[:, h % 2, :]), ALU.subtract) \
               .then_inc(self.lo_ready.sem, 1)
        if more:
            self.dve_k(dve, r, psum, 1, 1)


class Shared8:

    def __init__(self, kit, feed_forward):
        sb = kit.sb
        arena = sb("arena", [P, 4096], F32)
        self.stage = arena
        self.v = arena[:, 0:2048].rearrange("p (s b f) -> p s b f", s=2, b=G)
        self.p = arena[:, 2048:3072].rearrange("p (s b k) -> p s b k", s=2, b=G)
        self.z = arena[:, 3072:4096].rearrange("p (b f) -> p b f", b=G)
        self.q = sb("q", [P, 2, TOK], F32)
        self.k = sb("k", [P, 2, TOK], F32)
        self.p_turned = sb("p_turned", [P, 2, G, SEQ], F32)
        self.neg_max = sb("neg_max", [P, 2, G], F32)
        self.sums = sb("sums", [P, 2, G], F32)
        self.inverse = sb("inverse", [P, 2, G], F32)
        self.attended = Split(kit, "attended", [P, 2, TOK])
        self.residual = sb("residual", [P, G, DM], F32)
        self.stats = sb("stats", [P, G, 6], F32)
        self.moments = sb("moments", [P, G, 2], F32)
        self.variance = sb("variance", [P, G], F32)
        self.rstd = sb("rstd", [P, G], F32)
        self.minus_half = sb("minus_half", [P, 4], F32)
        self.y = sb("y", [P, 2, C, 2 * SEQ], F32)
        self.eye = sb("eye", [P, P], F32)
        self.masked_eye = sb("masked_eye", [P, P], BF16)
        self.flags = sb("flags", [P, G, SEQ], BF16)
        self.yt = Split(kit, "yt", [P, C, TOK])
        if feed_forward:
            self.relu = self.p_turned[:].rearrange("p s b q -> p (s b q)").rearrange(
                "p (s t) -> p s t", t=HALF)
            self.hidden = Split(kit, "hidden", [P, HIDDEN_SLOTS, HALF])


COLS8 = dict(q_inner=0, k_inner=2, v_inner=4, q=6, k=14, g1=22, s1=24, ff=26)
ROWS8_SELF, ROWS8_CROSS = ["o1"], ["o1", "g1", "s1", "ff"]


def phase8(nc, tag, cross, x, ctx_t, pad, packed, cols, v_row_dram, rows, out, ctx_out):
    with ExitStack() as ctx:
        kit = Kit(nc, ctx, tag)
        sh = Shared8(kit, cross)
        psum = ctx.enter_context(nc.psum_tensor(f"{tag}_psum", [P, 8, 512], F32))
        col = kit.sb("cols", list(cols.shape), F32)
        names = ROWS8_CROSS if cross else ROWS8_SELF
        row = kit.sb("rows", [P, len(names), DM], F32)
        v_row = kit.sb("v_row", [P, H8 * DK8], F32)
        n_big = (packed.shape[1] - 3 * 512) // STAGE_COLS
        weights = Split(kit, "w", [P, n_big * STAGE_COLS])
        inner = sh.p_turned[:].rearrange("p s b q -> p s (b q)")
        stage = sh.stage
        xt = Split(kit, "xt", [P, C, TOK])
        ct = Split(kit, "ct", [P, C, TOK])
        x_rows = kit.sb("x_rows", [P, G, DM], F32)
        pad_ints = kit.sb("pad_ints", [P, G, SEQ], I32)
        fold = ["q", "k", "v"]

        def take(i, inner_width):
            return View(weights, lambda t: t[:, i * STAGE_COLS:(i + 1) * STAGE_COLS].rearrange(
                "p (c n) -> p c n", n=inner_width))

        def rowv(name):
            return row[:, names.index(name), :]

        def colv(name, n):
            return col[:, COLS8[name]:COLS8[name] + n]

        w = {"q": take(0, H8 * DK8), "k": take(1, H8 * DK8), "v": take(2, H8 * DK8), "o": take(3, DM),
             "q_bias": colv("q", H8), "k_bias": colv("k", H8), "v_row": v_row}

        small_loaded = kit.counter("small_loaded", 0)
        stage_loaded = [kit.counter(f"stage_loaded{i}", 0) for i in range(n_big)]
        fold_in_psum = kit.counter("fold_in_psum", 0)
        folded = kit.counter("folded", 0)
        hi_made = kit.counter("w_hi_made", 0)
        lo_made = kit.counter("w_lo_made", 0)
        biases = kit.counter("biases", 0)
        consts = kit.counter("consts", 0)
        consts_pool = kit.counter("consts_pool", 0)

        x_loaded = kit.counter("x_loaded", 32)
        ct_loaded = kit.counter("ct_loaded", 32)
        rows_loaded = kit.counter("rows_loaded", 16)
        pad_loaded = kit.counter("pad_loaded", 16)
        pad_flags = kit.counter("pad_flags", 1)
        flags_ready = kit.counter("flags_ready", 1)
        all_masked = kit.counter("all_masked", 1)
        poison_made = kit.counter("poison_made", 3)
        residual_sum = kit.counter("residual_sum", 1)
        residual_ready = kit.counter("residual_ready", 1)
        stored = kit.counter("stored", 48 if cross else 32)
        masked = kit.sb("masked", [P, G], F32)
        poison = kit.sb("poison", [P, 3, G], F32)
        if not cross:
            x_raw = kit.sb("x_raw", [P, C, TOK], F32)
            ct_raw = kit.sb("ct_raw", [P, C, TOK], F32)
            causal = kit.sb("causal", [P, SEQ], BF16)
            x_raw_loaded = kit.counter("x_raw_loaded", 16)
            ct_raw_loaded = kit.counter("ct_raw_loaded", 16)
            x_hi = kit.counter("x_hi", 1)
            x_lo = kit.counter("x_lo", 1)
            ct_hi = kit.counter("ct_hi", 1)
            ct_lo = kit.counter("ct_lo", 1)
            ct_stored = kit.counter("ct_stored", 32)

        att = Attend8(kit, "a", w, sh)
        norm = [Norm(kit, "n1", att.out_ready, OUT8_BANKS, colv("g1", 2), colv("s1", 2),
                     rowv("g1") if cross else None, rowv("s1") if cross else None, sh, (2, 3))]
        if cross:
            s1_final = kit.sb("s1_final", [P, DM], F32)
            ff = FeedForward(kit, "ff", take(4, DFF), take(5, DM), colv("ff", M), norm[0].lo_ready, sh)
            norm.append(Norm(kit, "n2", ff.out_ready, FF_OUT_BANKS, colv("g1", 2), colv("s1", 2),
                             rowv("g1"), s1_final[:], sh))
            ff_norms = FeedForwardNorms(ff, norm[0], norm[1])
        final = norm[-1]
        block = ctx.enter_context(nc.Block())

        @block.sync
        def _(sp):
            def load_round(r):
                tok = bass.ds(r * TOK, TOK)
                if not cross:
                    sp.wait_ge(x_lo.sem, x_lo.at(r, 0))
                    kit.gated(sp)
                    sp.dma_start(x_raw[:], x[0][:, tok].rearrange("(c p) t -> p c t", p=P)) \
                      .then_inc(x_raw_loaded.sem, 16)
                sp.wait_ge(pad_flags.sem, pad_flags.at(r, 0))
                kit.gated(sp)
                sp.dma_start(pad_ints[:], pad[bass.ds(r * G, G)].rearrange("b o k -> o b k")
                             .broadcast_to([P, G, SEQ])).then_inc(pad_loaded.sem, 16)
                sp.wait_ge(residual_sum.sem, residual_sum.at(r, 0))
                kit.gated(sp)
                sp.dma_start(x_rows[:], x[-1][tok, :].rearrange("(b t) f -> t b f", b=G)) \
                  .then_inc(rows_loaded.sem, 16)
                if cross:
                    sp.wait_ge(att.k_in_psum.sem, att.k_in_psum.at(r, 0))
                    kit.gated(sp)
                    for tile, src, loaded in ((ct.hi, ctx_t[0], ct_loaded), (ct.lo, ctx_t[1], ct_loaded),
                                              (xt.hi, x[0], x_loaded), (xt.lo, x[1], x_loaded)):
                        sp.dma_start(f32(tile[:]), src[:, tok].rearrange("(c p) t -> p c t", p=P)) \
                          .then_inc(loaded.sem, 16)
                else:
                    sp.wait_ge(ct_lo.sem, ct_lo.at(r, 0))
                    kit.gated(sp)
                    sp.dma_start(ct_raw[:], ctx_t[:, tok].rearrange("(c p) t -> p c t", p=P)) \
                      .then_inc(ct_raw_loaded.sem, 16)

            sp.dma_start(col[:], cols).then_inc(small_loaded.sem, 16)
            sp.dma_start(v_row[:], v_row_dram.broadcast_to([P, H8 * DK8])).then_inc(small_loaded.sem, 16)
            sp.dma_start(row[:].rearrange("p n f -> p (n f)"),
                         rows.rearrange("(o n) f -> o (n f)", o=1).broadcast_to([P, len(names) * DM])) \
              .then_inc(small_loaded.sem, 16)
            for i in range(n_big):
                if i == 2:
                    load_round(0)
                if 2 <= i < 5:
                    sp.wait_ge(folded.sem, i - 1)
                elif i >= 5:
                    sp.wait_ge(lo_made.sem, 4 * 3 + i - 4)
                at = 3 * 512 + i * STAGE_COLS
                half = slice((i % 2) * STAGE_COLS, (i % 2 + 1) * STAGE_COLS)
                sp.dma_start(stage[:, half], packed[:, at:at + STAGE_COLS]) \
                  .then_inc(stage_loaded[i].sem, 16)
                if i < 3:
                    sp.dma_start(inner[:, i % 2, :], packed[:, i * 512:(i + 1) * 512]) \
                      .then_inc(stage_loaded[i].sem, 16)

            def store_round(r):
                tok = bass.ds(r * TOK, TOK)
                if not cross:
                    sp.wait_ge(ct_lo.sem, ct_lo.at(r, 1))
                    kit.gated(sp)
                    for part, dst in ((ct.hi, ctx_out[0]), (ct.lo, ctx_out[1])):
                        sp.dma_start(dst[:, tok].rearrange("(c p) t -> p c t", p=P), f32(part[:])) \
                          .then_inc(ct_stored.sem, 16)
                else:
                    for rows_ready in final.rows_ready:
                        sp.wait_ge(rows_ready.sem, rows_ready.at(r, 1))
                    kit.gated(sp)
                    sp.dma_start(out[2][tok, :].rearrange("(b t) f -> t b f", b=G), sh.residual[:]) \
                      .then_inc(stored.sem, 16)
                sp.wait_ge(final.lo_ready.sem, final.lo_ready.at(r, 2))
                kit.gated(sp)
                for part, dst in ((sh.yt.hi, out[0]), (sh.yt.lo, out[1])):
                    sp.dma_start(dst[:, tok].rearrange("(c p) t -> p c t", p=P), f32(part[:])) \
                      .then_inc(stored.sem, 16)

            with sp.Fori(0, ROUNDS - 1) as r:
                load_round(r + 1)
                store_round(r)
            store_round(ROUNDS - 1)
            sp.wait_ge(stored.sem, stored.at(ROUNDS, 0))
            if not cross:
                sp.wait_ge(ct_stored.sem, ct_stored.at(ROUNDS, 0))

        @block.scalar
        def _(act):
            def split_x(r):
                act.wait_ge(x_raw_loaded.sem, x_raw_loaded.at(r, 16))
                act.wait_ge(att.k_in_psum.sem, att.k_in_psum.at(r, 0))
                act.copy(xt.hi[:], x_raw[:]).then_inc(x_hi.sem, 1)

            def split_context(r):
                act.wait_ge(ct_raw_loaded.sem, ct_raw_loaded.at(r, 16))
                act.wait_ge(ct_stored.sem, ct_stored.at(r, 0))
                act.copy(ct.hi[:], ct_raw[:]).then_inc(ct_hi.sem, 1)

            for i in range(3):
                for o in range(4):
                    at = i * STAGE_COLS + o * 512
                    act.wait_ge(fold_in_psum.sem, 4 * i + o + 1)
                    act.copy(weights.hi[:, at:at + 512], psum[:, o, :]).then_inc(hi_made.sem, 1)
            if not cross:
                split_x(0)
            for i in range(3, n_big):
                act.wait_ge(stage_loaded[i].sem, 16)
                half = slice((i % 2) * STAGE_COLS, (i % 2 + 1) * STAGE_COLS)
                act.copy(weights.hi[:, i * STAGE_COLS:(i + 1) * STAGE_COLS], stage[:, half]) \
                   .then_inc(hi_made.sem, 1)
            act.wait_ge(biases.sem, 1)

            def one_round(r, more):
                for h in range(H8):
                    att.act_step(act, r, psum, h, more, split_x if more and not cross else None)
                    if not cross and h == 1:
                        split_context(r)
                norm[0].act(act, r, psum, 0, (final.lo_ready, 0))
                if cross:
                    ff_norms.act(act, r, psum)
                final.act(act, r, psum, 1)

            for h in range(2):
                att.act_q(act, 0, psum, h)
            with act.Fori(0, ROUNDS - 1) as r:
                one_round(r, True)
            one_round(ROUNDS - 1, False)

        @block.vector
        def _(dve):
            dve.memset(sh.minus_half[:], -0.5)
            for i in range(3):
                for o in range(4):
                    q = slice(i * STAGE_COLS + o * 512, i * STAGE_COLS + (o + 1) * 512)
                    dve.wait_ge(hi_made.sem, 4 * i + o + 1)
                    dve.tensor_tensor(weights.lo[:, q], psum[:, o, :], f32(weights.hi[:, q]),
                                      ALU.subtract).then_inc(lo_made.sem, 1)
            dve.wait_ge(folded.sem, 3)
            dve.wait_ge(small_loaded.sem, 16 * 3)
            dve.tensor_tensor(colv("q", H8), colv("q", H8), psum[:, 4, 0:H8], ALU.add) \
               .then_inc(consts.sem, 1)
            dve.tensor_tensor(colv("k", H8), colv("k", H8), psum[:, 5, 0:H8], ALU.add)
            dve.tensor_tensor(v_row[:], v_row[:], psum[:, 6:8, :].rearrange("p a n -> p (a n)"), ALU.add)
            if cross:
                dve.tensor_copy(s1_final[:], rowv("s1")).then_inc(consts.sem, 1)
            dve.wait_ge(consts.sem, 2 if cross else 1)
            dve.tensor_scalar(colv("q", H8), colv("q", H8), DK8 ** -0.5, None, ALU.mult)
            if cross:
                dve.tensor_tensor(rowv("s1"), rowv("s1"), rowv("ff"), ALU.add)
            dve.memset(sh.stats[:], 0.0).then_inc(biases.sem, 1)
            for i in range(3, n_big):
                half = slice((i % 2) * STAGE_COLS, (i % 2 + 1) * STAGE_COLS)
                q = slice(i * STAGE_COLS, (i + 1) * STAGE_COLS)
                dve.wait_ge(hi_made.sem, 12 + i - 2)
                dve.tensor_tensor(weights.lo[:, q], stage[:, half], f32(weights.hi[:, q]),
                                  ALU.subtract).then_inc(lo_made.sem, 1)
            dve.wait_ge(lo_made.sem, 12 + n_big - 3)

            def one_round(r, more):
                dve.wait_ge(flags_ready.sem, flags_ready.at(r, 1))
                dve.wait_ge(poison_made.sem, poison_made.at(r, 0))
                dve.tensor_reduce(masked[:], sh.flags[:], AX_X, ALU.min).then_inc(all_masked.sem, 1)
                att.dve(dve, r, psum, more)
                for pair in range(PAIRS):
                    norm[0].dve_sum(dve, r, psum, pair, (residual_ready, 1),
                                    (final.scaled[pair], 0) if cross else (final.hat_turned, 0))
                    norm[0].dve_stats(dve, r, pair)
                    norm[0].dve_moments(dve, r, pair)
                norm[0].dve_split(dve, r, 0, (stored, 0))
                if cross:
                    ff_norms.dve(dve, r, psum)
                final.dve_split(dve, r, 1)

            for h in range(2):
                att.dve_v(dve, 0, psum, h)
                att.dve_k(dve, 0, psum, h)
            with dve.Fori(0, ROUNDS - 1) as r:
                one_round(r, True)
            one_round(ROUNDS - 1, False)

        @block.gpsimd
        def _(pool):
            pool.memset(sh.eye[:], 1.0).then_inc(consts_pool.sem, 1)
            pool.wait_ge(consts_pool.sem, 1)
            pool.affine_select(out=sh.eye[:], in_=sh.eye[:], compare_op=ALU.is_equal, fill=0.0,
                               base=0, pattern=[[1, P]], channel_multiplier=-1).then_inc(consts_pool.sem, 1)
            pool.wait_ge(consts_pool.sem, 2)
            pool.tensor_scalar(sh.masked_eye[:], sh.eye[:], MASKED, None, ALU.mult) \
                .then_inc(consts_pool.sem, 1)
            made = 3
            if not cross:
                pool.memset(causal[:], 1.0).then_inc(consts_pool.sem, 1)
                pool.wait_ge(consts_pool.sem, 4)
                pool.affine_select(out=causal[:], in_=causal[:], compare_op=ALU.is_gt, fill=0.0,
                                   base=0, pattern=[[1, SEQ]], channel_multiplier=-1) \
                    .then_inc(consts_pool.sem, 1)
                made = 5
            pool.wait_ge(consts_pool.sem, made)
            pool.wait_ge(biases.sem, 1)

            def split_x(r):
                pool.wait_ge(x_hi.sem, x_hi.at(r, 1))
                pool.tensor_tensor(xt.lo[:], x_raw[:], f32(xt.hi[:]), ALU.subtract) \
                    .then_inc(x_lo.sem, 1)

            def make_flags(r):
                pool.wait_ge(pad_loaded.sem, pad_loaded.at(r, 16))
                pool.wait_ge(att.scores_ready.sem, att.scores_ready.at(r, 0))
                pool.wait_ge(all_masked.sem, all_masked.at(r, 0))
                pool.sem_inc(kit.gate.sem, 1)
                pool.tensor_scalar(sh.flags[:], pad_ints[:], 0.0, None, ALU.is_equal) \
                    .then_inc(pad_flags.sem, 1)
                pool.wait_ge(pad_flags.sem, pad_flags.at(r, 1))
                if not cross:
                    pool.tensor_tensor(sh.flags[:], sh.flags[:],
                                       causal[:].unsqueeze(1).broadcast_to([P, G, SEQ]), ALU.add) \
                        .then_inc(flags_ready.sem, 1)
                else:
                    pool.sem_inc(flags_ready.sem, 1)

            def one_round(r, more):
                pool.wait_ge(all_masked.sem, all_masked.at(r, 1))
                pool.sem_inc(kit.gate.sem, 1)
                pool.tensor_scalar(poison[:, 0, :], masked[:], 3e38, None, ALU.mult) \
                    .then_inc(poison_made.sem, 1)
                pool.wait_ge(poison_made.sem, poison_made.at(r, 1))
                pool.sem_inc(kit.gate.sem, 1)
                pool.tensor_scalar(poison[:, 1, :], poison[:, 0, :], 10.0, None, ALU.mult) \
                    .then_inc(poison_made.sem, 1)
                pool.wait_ge(poison_made.sem, poison_made.at(r, 2))
                pool.sem_inc(kit.gate.sem, 1)
                pool.tensor_scalar(poison[:, 2, :], poison[:, 1, :], 0.0, None, ALU.mult) \
                    .then_inc(poison_made.sem, 1)
                pool.wait_ge(rows_loaded.sem, rows_loaded.at(r, 16))
                pool.wait_ge(stored.sem, stored.at(r, 0))
                if not cross:
                    pool.wait_ge(final.sum_ready.sem, final.sum_ready.at(r, 0))
                pool.tensor_tensor(sh.residual[:], x_rows[:],
                                   rowv("o1").unsqueeze(1).broadcast_to([P, G, DM]), ALU.add) \
                    .then_inc(residual_sum.sem, 1)
                pool.wait_ge(residual_sum.sem, residual_sum.at(r, 1))
                pool.wait_ge(poison_made.sem, poison_made.at(r, 3))
                pool.tensor_tensor(sh.residual[:], sh.residual[:],
                                   poison[:, 2, :].unsqueeze(2).broadcast_to([P, G, DM]), ALU.add) \
                    .then_inc(residual_ready.sem, 1)
                if not cross:
                    pool.wait_ge(ct_hi.sem, ct_hi.at(r, 1))
                    pool.tensor_tensor(ct.lo[:], ct_raw[:], f32(ct.hi[:]), ALU.subtract) \
                        .then_inc(ct_lo.sem, 1)
                    if more:
                        split_x(r + 1)
                if more:
                    make_flags(r + 1)
                for pair in range(PAIRS):
                    norm[0].pool_hat(pool, r, pair)
                if cross:
                    ff_norms.pool(pool, r)

            if not cross:
                split_x(0)
            make_flags(0)
            with pool.Fori(0, ROUNDS - 1) as r:
                one_round(r, True)
            one_round(ROUNDS - 1, False)

        @block.tensor
        def _(pe):
            kit.start(pe)
            pe.wait_ge(small_loaded.sem, 16 * 3)
            for i, name in enumerate(fold):
                pe.wait_ge(stage_loaded[i].sem, 32)
                outer = stage[:, (i % 2) * STAGE_COLS:(i % 2 + 1) * STAGE_COLS].rearrange(
                    "p (c n) -> p c n", c=C)
                small = inner[:, i % 2, :].rearrange("p (c n) -> p c n", c=C)
                for o in range(4):
                    if i > 0:
                        pe.wait_ge(lo_made.sem, 4 * (i - 1) + o + 1)
                    chunk, half = o // 2, o % 2
                    for k in range(C):
                        ins = pe.matmul(psum[:, o, :], small[:, k, chunk * P:(chunk + 1) * P],
                                        outer[:, k, half * 512:(half + 1) * 512],
                                        start=k == 0, stop=k == C - 1)
                    ins.then_inc(fold_in_psum.sem, 1)
                bias = colv(name + "_inner", C)
                if name == "v":
                    for half in range(2):
                        for k in range(C):
                            ins = pe.matmul(psum[:, 6 + half, :], bias[:, k:k + 1].broadcast_to([P, P]),
                                            outer[:, k, half * 512:(half + 1) * 512],
                                            start=k == 0, stop=k == C - 1)
                else:
                    for h in range(H8):
                        for k in range(C):
                            ins = pe.matmul(psum[:, 4 + i, h:h + 1], outer[:, k, h * P:(h + 1) * P],
                                            bias[:, k:k + 1], start=k == 0, stop=k == C - 1)
                ins.then_inc(folded.sem, 1)
            pe.wait_ge(lo_made.sem, 12)
            pe.wait_ge(biases.sem, 1)

            if cross:
                q_src, kv_src, q_there, kv_there = xt, ct, x_loaded, ct_loaded
            else:
                q_src, kv_src, q_there, kv_there = xt, xt, x_lo, x_lo

            def one_round(r, more):
                banks = Banks(psum)
                if cross:
                    for bank, reader in ((0, ff.hidden_ready), (1, final.turned_ready),
                                         (2, final.turned_ready), (3, norm[0].turned_ready),
                                         (4, ff.hidden_ready), (5, ff.hidden_ready),
                                         (6, final.sum_ready), (7, final.sum_ready)):
                        banks.read(bank, reader, 0)
                else:
                    for bank, reader in ((0, final.sum_ready), (1, final.sum_ready),
                                         (2, final.turned_ready), (3, final.turned_ready),
                                         (V8_BANK, att.v_ready), (S8_BANK, att.exp_done),
                                         (TURN8_BANK, att.turned_ready), (MIX8_BANK, att.lo_ready)):
                        banks.read(bank, reader, 0)
                for bank, reader in ((Q8_BANK, att.q_ready), (K8_BANK, att.k_ready), (V8_BANK, att.v_ready)):
                    banks.read_too(bank, reader, 2)
                pe.wait_ge(flags_ready.sem, flags_ready.at(r, 1))
                att.pe(pe, r, banks, q_src, kv_src, norm[0].sum_ready, more,
                       q_there, kv_there)
                norm[0].pe(pe, r, banks, 0)
                if cross:
                    ff_norms.pe(pe, r, banks)
                final.pe(pe, r, banks, 1)

            for there in (q_there, kv_there):
                pe.wait_ge(there.sem, there.at(0, there.per_round))
            att.pe_first(pe, Banks(psum), q_src, kv_src)
            pe.wait_ge(lo_made.sem, 12 + n_big - 3)
            pe.wait_ge(consts_pool.sem, 3)
            with pe.Fori(0, ROUNDS - 1) as r:
                one_round(r, True)
            one_round(ROUNDS - 1, False)


def four_layers(nc, t, out):
    def scratch(name, shape):
        return nc.dram_tensor(name, shape, F32, kind="Internal").ap()

    tokens = BATCH * SEQ
    ctx_split = (scratch("context_hi", (DM, tokens)), scratch("context_lo", (DM, tokens)))
    between = [(scratch(f"x{i}_hi", (DM, tokens)), scratch(f"x{i}_lo", (DM, tokens)),
                scratch(f"x{i}_rows", (tokens, DM))) for i in range(4)]
    phase8(nc, "self8", False, (t["x_t"], t["x_rows"]), t["ctx_t"], t["pad"], t["l0a_packed"],
           t["l0a_cols"], t["l0a_v_row"], t["l0a_rows"], between[0], ctx_split)
    phase8(nc, "cross8", True, (between[0][0], between[0][1], t["x_rows"]), ctx_split, t["pad"],
           t["l0b_packed"], t["l0b_cols"], t["l0b_v_row"], t["l0b_rows"], between[1], None)
    phase16(nc, "second", True, between[1], ctx_split,
            [(t["mask_self"], False, -1e20, True), (t["mask_cross"], False, -1e20, True)],
            t["l1_packed"], t["l1_cols"], t["l1_rows"], between[2])
    phase16(nc, "third", True, between[2], ctx_split,
            [(t["mask_all"].unsqueeze(1), True, -3.3895e38, False), None],
            t["l2_packed"], t["l2_cols"], t["l2_rows"], between[3])
    phase16(nc, "fourth", False, between[3], ctx_split, [None],
            t["l3_packed"], t["l3_cols"], t["l3_rows"], (None, None, out))




def kernel(**inputs):
    import concourse.bacc as _bacc
    from concourse.bass_utils import run_bass_kernel_spmd as _run

    a = {k: np.asarray(v) for k, v in inputs.items()}

    def chunked(w):
        return w.reshape(-1, P, w.shape[1]).transpose(1, 0, 2).reshape(P, -1)

    def column(v):
        return v.reshape(-1, P).T

    def layer0(self_half):
        s, n = ("sa", "1") if self_half else ("ed", "2")
        L = "L0_xattn_"
        packed = [chunked(a[f"{L}{x}{n}_w"]) for x in "qkv"]
        packed += [chunked(a[f"{L}{s}_{x}w"].reshape(-1, DM).T) for x in "qkv"]
        packed += [chunked(a[f"{L}{s}_ow"].T)]
        cols = [column(a[f"{L}{x}{n}_b"]) for x in "qkv"]
        cols += [column(a[f"{L}{s}_qb"].reshape(-1)), column(a[f"{L}{s}_kb"].reshape(-1)),
                 column(a[f"{L}ln{n}_g"]), column(a[f"{L}ln{n}_b"])]
        rows = [a[f"{L}{s}_ob"]]
        if not self_half:
            packed += [chunked(a[L + "ff_w1"].T), chunked(a[L + "ff_w2"].T)]
            cols += [column(a[L + "ff_b1"])]
            rows += [a[L + "ln2_g"], a[L + "ln2_b"], a[L + "ff_b2"]]
        return (np.concatenate(packed, 1), np.concatenate(cols, 1),
                a[f"{L}{s}_vb"].reshape(1, -1), np.stack(rows))

    def full16(L, self_names, cross_names, biases, ff):
        g = lambda n: a[L + n]
        packed = [chunked(g(n)) for n in self_names + cross_names] + [chunked(g(ff[0])), chunked(g(ff[2]))]
        sb, cb = biases
        cols = [sb[0], sb[1], cb[0], cb[1], "ln1_g", "ln1_b", "ln2_g", "ln2_b", "ln3_g", "ln3_b", ff[1]]
        rows = [sb[2], cb[2], sb[3], "ln1_g", "ln1_b", "ln2_g", "ln2_b", "ln3_g", "ln3_b", cb[3], ff[3]]
        return (np.concatenate(packed, 1), np.concatenate([column(g(n)) for n in cols], 1),
                np.stack([g(n) for n in rows]))

    d = {}
    d["x_t"] = a["x"].reshape(-1, DM).T
    d["x_rows"] = a["x"].reshape(-1, DM)
    d["ctx_t"] = a["ctx_1024"].reshape(-1, DM).T
    d["pad"] = a["mask_Bx1xS2_if1"]
    d["mask_self"], d["mask_cross"] = a["mask_BxSxS2_ik0"], a["mask_BxSxS2_if1"]
    d["mask_all"] = a["mask_SxS_ik1"]
    d["l0a_packed"], d["l0a_cols"], d["l0a_v_row"], d["l0a_rows"] = layer0(True)
    d["l0b_packed"], d["l0b_cols"], d["l0b_v_row"], d["l0b_rows"] = layer0(False)
    d["l1_packed"], d["l1_cols"], d["l1_rows"] = full16(
        "L1_xattn_", ["sa_wq", "sa_wk", "sa_wv", "sa_wo"], ["ca_wq", "ca_wk", "ca_wv", "ca_wo"],
        (["sa_bq", "sa_bk", "sa_bv", "sa_bo"], ["ca_bq", "ca_bk", "ca_bv", "ca_bo"]),
        ["ff_w1", "ff_b1", "ff_w2", "ff_b2"])
    d["l2_packed"], d["l2_cols"], d["l2_rows"] = full16(
        "L2_xattn_", ["q_w", "k_w", "v_w", "o_w"], ["cq_w", "ck_w", "cv_w", "co_w"],
        (["q_b", "k_b", "v_b", "o_b"], ["cq_b", "ck_b", "cv_b", "co_b"]),
        ["lin1_w", "lin1_b", "lin2_w", "lin2_b"])
    L = "L3_xattn_"
    d["l3_packed"] = np.concatenate([chunked(a[L + n].T) for n in ("Wq", "Wk", "Wv", "Wo")], 1)
    d["l3_cols"] = np.concatenate([column(a[L + n]) for n in ("bq", "bk")], 1)
    d["l3_rows"] = np.stack([a[L + n] for n in ("bv", "bo", "gamma", "beta")])

    nc = _bacc.Bacc("TRN2", target_bir_lowering=False, num_devices=1)
    arrays, t = {}, {}
    for name, array in d.items():
        arrays[f"in_{name}"] = np.ascontiguousarray(array)
        t[name] = nc.dram_tensor(f"in_{name}", arrays[f"in_{name}"].shape,
                                 mybir.dt.from_np(array.dtype), kind="ExternalInput").ap()
    out = nc.dram_tensor("out_0", (BATCH * SEQ, DM), F32, kind="ExternalOutput").ap()
    four_layers(nc, t, out)
    r = _run(nc, [arrays], core_ids=[0])
    return r.results[0]["out_0"].reshape(BATCH, SEQ, DM)
```
